# Optimizing a Trainium2 kernel written in Bass

```python
import numpy as np
import jax
import jax.numpy as jnp

def _softmax(x, axis=-1):
    return jax.nn.softmax(x, axis=axis)

def _gelu(x):
    return jax.nn.gelu(x, approximate=True)

def _silu(x):
    return jax.nn.silu(x)

def _sigmoid(x):
    return jax.nn.sigmoid(x)

def _layernorm(x, axis=-1, eps=1e-05):
    m = jnp.mean(x, axis=axis, keepdims=True)
    v = jnp.var(x, axis=axis, keepdims=True)
    return (x - m) / jnp.sqrt(v + eps)

def _scatter_add(tgt, idx, src, axis=0):
    return tgt.at[idx].add(src)

def _segment_sum(src, seg, n):
    return jax.ops.segment_sum(src, seg, n)
kernel_name = 'mk_gnn_resnorm_d1_gnn_r8_608c05'

def setup_inputs(seed: int=0):
    np.random.seed(seed)
    _w = jnp.asarray

    def _rec_inputs():
        import jax
        import jax.numpy as jnp
        _gk = jax.random.key(seed)
        x = -0.0002928 + 1 * jax.random.normal(jax.random.fold_in(_gk, 1), (6250, 256), jnp.float32)
        src = jax.random.randint(jax.random.fold_in(_gk, 2), (200000,), 0, 6250, jnp.int32)
        dst = jnp.minimum((6250 * jax.random.uniform(jax.random.fold_in(_gk, 3), (200000,)) ** 2.0).astype(jnp.int32), 49999)
        _o = jnp.argsort(dst, stable=True)
        src = src[_o]
        dst = dst[_o]
        return (x, src, dst)
    x, src, dst = _rec_inputs()

    def _L0_gnn_setup():
        import jax, jax.numpy as jnp
        import numpy as np
        N_NODES = 2048
        N_EDGES = 32768
        D_IN = 256
        D = 256
        H = 512
        E = 64
        TOP_K = 2
        CAP = 1024
        BN_EPS = 1e-05

        def _moe_ff(x, Wg, bg, w1, b1, w2, b2):
            N = x.shape[0]
            logits = x @ Wg + bg
            vals, idx = jax.lax.top_k(logits, TOP_K)
            gates = jax.nn.softmax(vals, axis=-1)
            e_flat = idx.reshape(-1)
            g_flat = gates.reshape(-1)
            tok = jnp.arange(N * TOP_K) // TOP_K
            order = jnp.argsort(e_flat)
            e_s, tok_s, g_s = (e_flat[order], tok[order], g_flat[order])
            counts = jnp.bincount(e_flat, length=E)
            offs = jnp.concatenate([jnp.zeros((1,), counts.dtype), jnp.cumsum(counts)[:-1]])
            rank = jnp.arange(N * TOP_K) - offs[e_s]
            valid = rank < CAP
            slot = jnp.where(valid, e_s * CAP + rank, E * CAP)
            buf = jnp.zeros((E * CAP + 1, D), x.dtype).at[slot].set(x[tok_s])
            h = buf[:E * CAP].reshape(E, CAP, D)
            h1 = jax.nn.gelu(jnp.einsum('ecd,edh->ech', h, w1) + b1[:, None, :], approximate=False)
            h2 = jnp.einsum('ech,ehd->ecd', h1, w2) + b2[:, None, :]
            out_buf = h2.reshape(E * CAP, D)
            y_s = jnp.where(valid[:, None], out_buf[jnp.minimum(slot, E * CAP - 1)], 0.0)
            return jnp.zeros((N, D), x.dtype).at[tok_s].add(g_s[:, None] * y_s)

        def _forward(feats, W_gc, b_gc, W_res, b_res, Wg, bg, w1, b1, w2, b2, gamma, beta, src, dst):
            n = feats.shape[0]
            ones = jnp.ones((src.shape[0],), feats.dtype)
            deg_out = jnp.clip(jax.ops.segment_sum(ones, src, num_segments=n), 1.0)
            deg_in = jnp.clip(jax.ops.segment_sum(ones, dst, num_segments=n), 1.0)
            h = feats * jax.lax.rsqrt(deg_out)[:, None]
            m = jax.ops.segment_sum(h[src], dst, num_segments=n) * jax.lax.rsqrt(deg_in)[:, None]
            gc = m @ W_gc + b_gc
            x = gc + (feats @ W_res + b_res)
            core = _moe_ff(x, Wg, bg, w1, b1, w2, b2)
            y = x + core
            mean = jnp.mean(y, axis=0)
            var = jnp.mean((y - mean) ** 2, axis=0)
            return (y - mean) * jax.lax.rsqrt(var + BN_EPS) * gamma + beta
        key = jax.random.key(seed)
        ks = jax.random.split(key, 16)
        s = lambda d: 1.0 / np.sqrt(d)
        inp = {'feats': jax.random.normal(ks[0], (N_NODES, D_IN), jnp.float32), 'W_gc': jax.random.normal(ks[1], (D_IN, D), jnp.float32) * s(D_IN), 'b_gc': jnp.zeros((D,), jnp.float32), 'W_res': jax.random.normal(ks[2], (D_IN, D), jnp.float32) * s(D_IN), 'b_res': jnp.zeros((D,), jnp.float32), 'Wg': jax.random.normal(ks[3], (D, E), jnp.float32) * s(D), 'bg': jnp.zeros((E,), jnp.float32), 'w1': jax.random.normal(ks[4], (E, D, H), jnp.float32) * s(D), 'b1': jnp.zeros((E, H), jnp.float32), 'w2': jax.random.normal(ks[5], (E, H, D), jnp.float32) * s(H), 'b2': jnp.zeros((E, D), jnp.float32), 'gamma': jnp.ones((D,), jnp.float32), 'beta': jnp.zeros((D,), jnp.float32), 'src': jax.random.randint(ks[6], (N_EDGES,), 0, N_NODES), 'dst': jax.random.randint(ks[7], (N_EDGES,), 0, N_NODES)}
        return inp
    _L0_gnn_all = _L0_gnn_setup()
    _L0_gnn_in = {k: v for k, v in _L0_gnn_all.items() if k in ('W_gc', 'b_gc', 'W_res', 'b_res', 'Wg', 'bg', 'w1', 'b1', 'w2', 'b2', 'gamma', 'beta')}
    del _L0_gnn_all
    return {'x': x, 'src': src, 'dst': dst, 'L0_gnn_W_gc': _L0_gnn_in['W_gc'], 'L0_gnn_b_gc': _L0_gnn_in['b_gc'], 'L0_gnn_W_res': _L0_gnn_in['W_res'], 'L0_gnn_b_res': _L0_gnn_in['b_res'], 'L0_gnn_Wg': _L0_gnn_in['Wg'], 'L0_gnn_bg': _L0_gnn_in['bg'], 'L0_gnn_w1': _L0_gnn_in['w1'], 'L0_gnn_b1': _L0_gnn_in['b1'], 'L0_gnn_w2': _L0_gnn_in['w2'], 'L0_gnn_b2': _L0_gnn_in['b2'], 'L0_gnn_gamma': _L0_gnn_in['gamma'], 'L0_gnn_beta': _L0_gnn_in['beta']}

def reference(x, src, dst, L0_gnn_W_gc, L0_gnn_b_gc, L0_gnn_W_res, L0_gnn_b_res, L0_gnn_Wg, L0_gnn_bg, L0_gnn_w1, L0_gnn_b1, L0_gnn_w2, L0_gnn_b2, L0_gnn_gamma, L0_gnn_beta):
    import jax
    import jax.numpy as jnp

    def _L0_gnn_ref(feats, W_gc, b_gc, W_res, b_res, Wg, bg, w1, b1, w2, b2, gamma, beta, src, dst):
        import jax, jax.numpy as jnp
        import numpy as np
        N_NODES = 2048
        N_EDGES = 32768
        D_IN = 256
        D = 256
        H = 512
        E = 64
        TOP_K = 2
        CAP = 1024
        BN_EPS = 1e-05

        def _moe_ff(x, Wg, bg, w1, b1, w2, b2):
            N = x.shape[0]
            logits = x @ Wg + bg
            vals, idx = jax.lax.top_k(logits, TOP_K)
            gates = jax.nn.softmax(vals, axis=-1)
            e_flat = idx.reshape(-1)
            g_flat = gates.reshape(-1)
            tok = jnp.arange(N * TOP_K) // TOP_K
            order = jnp.argsort(e_flat)
            e_s, tok_s, g_s = (e_flat[order], tok[order], g_flat[order])
            counts = jnp.bincount(e_flat, length=E)
            offs = jnp.concatenate([jnp.zeros((1,), counts.dtype), jnp.cumsum(counts)[:-1]])
            rank = jnp.arange(N * TOP_K) - offs[e_s]
            valid = rank < CAP
            slot = jnp.where(valid, e_s * CAP + rank, E * CAP)
            buf = jnp.zeros((E * CAP + 1, D), x.dtype).at[slot].set(x[tok_s])
            h = buf[:E * CAP].reshape(E, CAP, D)
            h1 = jax.nn.gelu(jnp.einsum('ecd,edh->ech', h, w1) + b1[:, None, :], approximate=False)
            h2 = jnp.einsum('ech,ehd->ecd', h1, w2) + b2[:, None, :]
            out_buf = h2.reshape(E * CAP, D)
            y_s = jnp.where(valid[:, None], out_buf[jnp.minimum(slot, E * CAP - 1)], 0.0)
            return jnp.zeros((N, D), x.dtype).at[tok_s].add(g_s[:, None] * y_s)

        def _forward(feats, W_gc, b_gc, W_res, b_res, Wg, bg, w1, b1, w2, b2, gamma, beta, src, dst):
            n = feats.shape[0]
            ones = jnp.ones((src.shape[0],), feats.dtype)
            deg_out = jnp.clip(jax.ops.segment_sum(ones, src, num_segments=n), 1.0)
            deg_in = jnp.clip(jax.ops.segment_sum(ones, dst, num_segments=n), 1.0)
            h = feats * jax.lax.rsqrt(deg_out)[:, None]
            m = jax.ops.segment_sum(h[src], dst, num_segments=n) * jax.lax.rsqrt(deg_in)[:, None]
            gc = m @ W_gc + b_gc
            x = gc + (feats @ W_res + b_res)
            core = _moe_ff(x, Wg, bg, w1, b1, w2, b2)
            y = x + core
            mean = jnp.mean(y, axis=0)
            var = jnp.mean((y - mean) ** 2, axis=0)
            return (y - mean) * jax.lax.rsqrt(var + BN_EPS) * gamma + beta
        return _forward(feats, W_gc, b_gc, W_res, b_res, Wg, bg, w1, b1, w2, b2, gamma, beta, src, dst)
    x = _layernorm(x + _L0_gnn_ref(x, L0_gnn_W_gc, L0_gnn_b_gc, L0_gnn_W_res, L0_gnn_b_res, L0_gnn_Wg, L0_gnn_bg, L0_gnn_w1, L0_gnn_b1, L0_gnn_w2, L0_gnn_b2, L0_gnn_gamma, L0_gnn_beta, src, dst), axis=-1)
    return x

_drawn_inputs = setup_inputs


def setup_inputs(seed=0):
    import zlib

    import numpy as np

    out = dict(_drawn_inputs(seed))
    spreads = {'L0_gnn_b_gc': (0.0, 0.1),
     'L0_gnn_b_res': (0.0, 0.1),
     'L0_gnn_bg': (0.0, 0.1),
     'L0_gnn_b1': (0.0, 0.1),
     'L0_gnn_b2': (0.0, 0.1),
     'L0_gnn_gamma': (1.0, 0.2),
     'L0_gnn_beta': (0.0, 0.1)}
    factors = {}
    for name, (base, spread) in spreads.items():
        noise = np.random.default_rng([zlib.crc32(name.encode()), seed]).standard_normal(out[name].shape)
        drawn = base * np.exp(spread * noise) if base else spread * noise
        out[name] = jnp.asarray(drawn.astype(out[name].dtype))
    for name, factor in factors.items():
        out[name] = (out[name] * factor).astype(out[name].dtype)
    return out
```

```python
import concourse.bass as bass
from concourse import mybir
from contextlib import ExitStack

F32 = mybir.dt.float32
BF16 = mybir.dt.bfloat16
I32 = mybir.dt.int32
U32 = mybir.dt.uint32
I16 = mybir.dt.int16
ALU = mybir.AluOpType
ACT = mybir.ActivationFunctionType
AX = mybir.AxisListType

P = 128
N, D, EDGES = 6250, 256, 200000
H, EX, TOPK, CAP = 512, 64, 2, 1024
BN_EPS = LN_EPS = 1e-5
NT = -(-N // P)
LAST = N - (NT - 1) * P
NPAD = NT * P
PARTS = 3
ROW = PARTS * D
EB = -(-EDGES // (P * P))
EFULL = EDGES // P
ETAIL = EDGES - EFULL * P
CPG = 4
COLS = EB * P
GCOLS = COLS // CPG
RING = 4
STEPS = -(-(-(-EDGES // P)) // (CPG * RING))
GROUPS = STEPS * RING
HB = 8
HSTEPS = -(-(-(-EDGES // P)) // (2 * HB))
SLOTCH = CAP // P
SC = EX * SLOTCH
MAIN = 3
TG = 7
NB = NT // TG
PAD_SRC = NPAD - 1
PAD_DST = 50 * P
UNUSED = 1.0e6
DK, HK = D // P, H // P


def graph_moe_kernel(nc, x, src, dst, W_gc, b_gc, W_res, b_res, Wg, bg, w1, b1, w2, b2, gamma, beta, out):
    ctx = ExitStack()
    with ctx:
        def sb(name, shape, dt=F32):
            return ctx.enter_context(nc.sbuf_tensor(name, shape, dt))

        def sem(name):
            return ctx.enter_context(nc.semaphore(name))

        table = nc.dram_tensor("table", (NPAD, ROW), BF16, kind="Internal").ap()
        nodes = nc.dram_tensor("nodes", (NPAD, D), F32, kind="Internal").ap()
        y2 = nc.dram_tensor("y2", (TOPK * NPAD, D), F32, kind="Internal").ap()

        xs = sb("xs", [P, NT, D])
        acc = sb("acc", [P, NT, D + 1])
        ident = sb("ident", [P, P])
        ones = sb("ones", [P, P])
        ones_last = sb("ones_last", [P, P])
        pcol = sb("pcol", [P, 1])
        iota_f = sb("iota_f", [P, P])
        iota_b = sb("iota_b", [P, P], BF16)
        iota_s = sb("iota_s", [P, SC], I16)
        zeros = sb("zeros", [P, 2 * D])
        wgc = sb("wgc", [P, DK, D])
        wres = sb("wres", [P, DK, D])
        wg = sb("wg", [P, DK, EX])
        bias = sb("bias", [P, D])
        bgb = sb("bgb", [P, EX])
        valid = sb("valid", [P, NT])
        acc_flat = acc[:, :, :].rearrange("p t d -> p (t d)")
        raw_src = acc_flat[:, 0:COLS].bitcast(I32).rearrange("p (b e) -> p b e", e=P)
        raw_dst = acc_flat[:, COLS:2 * COLS].bitcast(I32).rearrange("p (b e) -> p b e", e=P)
        loT = acc_flat[:, 2 * COLS:3 * COLS]
        hiT = acc_flat[:, 3 * COLS:4 * COLS]
        srcT = sb("srcT", [P, COLS])
        dstT = sb("dstT", [P, COLS])
        stage = sb("stage", [P, 4 * TG * D])
        ring = sb("ring", [P, RING, CPG, ROW + 2], BF16)
        ring_idx = sb("ring_idx", [P, RING, CPG], I32)
        hot = sb("hot", [P, RING, CPG, P], BF16)
        hotx = sb("hotx", [P, CPG, P], BF16)
        neg_tile = sb("neg_tile", [P, NT])
        neg_base = sb("neg_base", [P, GCOLS])
        mnmx = sb("mnmx", [P, 2, EB])
        rng_f = sb("rng_f", [EB, 2, P // CPG])
        rng_i = sb("rng_i", [EB, 2, P // CPG], I32)
        rng = sb("rng", [1, 2, GCOLS])
        code = sb("code", [1, GCOLS], I32)
        deg = sb("deg", [P, NT])
        rs = sb("rs", [P, NT])
        tmp = sb("tmp", [P, NT])
        nd = sb("nd", [P, 4])
        mS = sb("mS", [P, D])
        xS = sb("xS", [P, D])
        tS = sb("tS", [P, 4, P])
        yS = sb("yS", [P, D])
        ytS = sb("ytS", [P, DK, P])
        lg = sb("lg", [P, EX])
        v8 = sb("v8", [P, 8])
        i8 = sb("i8", [P, 8], U32)
        i8f = sb("i8f", [P, TOPK])
        pick = sb("pick", [P, TOPK, EX], BF16)
        picked = sb("picked", [P, EX], BF16)
        taken = sb("taken", [P, EX], BF16)
        tri = sb("tri", [P, P], BF16)
        ones_b = sb("ones_b", [P, P], BF16)
        junk = sb("junk", [P, EX])
        rk = sb("rk", [P, TOPK])
        rki = sb("rki", [P, 3, TOPK], I32)
        rkf = sb("rkf", [P, 2, TOPK])
        qs = sb("qs", [P, TOPK])
        inval = sb("inval", [P, NT])
        hnum = sb("hnum", [P, TOPK, NT])
        sel = sb("sel", [P, TOPK, SC], BF16)
        lo1 = sb("lo1", [P, TOPK, 2, P], BF16)
        top = sb("top", [P, NT, TOPK])
        rank = sb("rank", [P, NT, TOPK])
        gate = sb("gate", [P, NT, TOPK])
        tok_f = stage[:, 0:SC]
        tok_t = stage[:, SC:2 * SC]
        gidx = sb("gidx", [P, SC], I32)
        sidx = sb("sidx", [P, SC], I32)
        nch_f = sb("nch_f", [1, EX])
        nch_i = sb("nch_i", [1, EX], I32)
        b1r = sel[0:EX, :, :].rearrange("p k s -> p (k s)").bitcast(F32)
        b1T = sb("b1T", [P, HK, EX])
        b1e = sb("b1e", [P, HK])
        w1s = stage[:, 0:2 * DK * H].rearrange("p (b k h) -> p b k h", b=2, k=DK)
        w2s = stage[:, 2 * DK * H:4 * DK * H].rearrange("p (b j d) -> p b j d", b=2, j=HK)
        b2s = stage[:, 4 * DK * H:4 * DK * H + 2 * D].rearrange("p (b d) -> p b d", b=2)
        ybuf = stage[:, :].rearrange("p (b k t d) -> p b k t d", b=2, k=TOPK, t=TG)
        sq = stage[:, 0:2 * TG * D].rearrange("p (b t d) -> p b t d", b=2, t=TG)
        arena = ring[:, :, :, :].rearrange("p a b c -> p (a b c)").bitcast(F32)
        taken_to = [0]

        def piece(n):
            taken_to[0] += n
            return arena[:, taken_to[0] - n:taken_to[0]]

        xg = piece(2 * MAIN * D).rearrange("p (b k d) -> p b k d", b=2, k=MAIN)
        xgT = piece(MAIN * D).rearrange("p (k c r) -> p k c r", k=MAIN, c=DK)
        h1 = piece(MAIN * H).rearrange("p (k j r) -> p k j r", k=MAIN, j=HK)
        outs = piece(2 * MAIN * D).rearrange("p (b k d) -> p b k d", b=2, k=MAIN)
        xgx = piece(D)
        xgTx = piece(D).rearrange("p (c r) -> p c r", c=DK)
        late = hot[:, :, :, :].rearrange("p a b c -> p (a b c)").bitcast(F32)
        gb = late[:, 0:2 * D].rearrange("p (a d) -> p a d", a=2)
        h1x = late[:, 2 * D:2 * D + H].rearrange("p (j r) -> p j r", j=HK)
        outx = mS
        mean, var, vroot, scale = xS, yS, tS[:, 0:DK, :].rearrange("p c r -> p (c r)"), tS[:, DK:2 * DK, :].rearrange("p c r -> p (c r)")
        slot_idx = sb("slot_idx", [P, 2, 2, MAIN], I32)
        xtra_idx = sb("xtra_idx", [P, 2], I32)
        stats = srcT[:, 0:TG * 6].rearrange("p (t s) -> p t s", s=6)
        mv = srcT[:, TG * 6:TG * 6 + 2 * NT].rearrange("p (t s) -> p t s", s=2)

        banks = [ctx.enter_context(nc.psum_tensor(f"bank{i}", [P, 512], F32)) for i in range(8)]

        lo_hot = stage[:, 0:HB * P].bitcast(BF16).rearrange("p (b c n) -> p b c n", b=2, c=HB)
        hi_hot = stage[:, HB * P:HB * P + HB * NT].bitcast(BF16).rearrange("p (b c t) -> p b c t", b=2, c=HB)
        s0 = 2 * TG * ROW // 2
        SFX = 656
        sfx = stage[0:1, s0:s0 + 2 * SFX].rearrange("o (a g) -> o a g", a=2)
        code_f = stage[0:1, s0 + 2 * SFX:s0 + 2 * SFX + GCOLS]
        parts = stage[:, 0:2 * TG * ROW // 2].bitcast(BF16).rearrange("p (b t r) -> p b t r", b=2, t=TG)

        ini = sem("ini")
        const_p = sem("const_p")
        const_d = sem("const_d")
        src_loaded, dst_loaded, x_loaded, w_loaded = sem("src_loaded"), sem("dst_loaded"), sem("x_loaded"), sem("w_loaded")
        srch_f, dst_f = sem("srch_f"), sem("dst_f")
        tr_done, tr_copied = sem("tr_done"), sem("tr_copied")
        hi_diff, lo_ready, hi_ready, hist_mm = sem("hi_diff"), sem("lo_ready"), sem("hi_ready"), sem("hist_mm")
        mm_tr, mm_red, mm_row, nb_done, base_ready = sem("mm_tr"), sem("mm_red"), sem("mm_row"), sem("nb_done"), sem("base_ready")
        deg_ready, deg_sqrt, rs_ready = sem("deg_ready"), sem("deg_sqrt"), sem("rs_ready")
        h_ready, hi_part, r1_ready, mid_part, lo_part, table_out = (sem("h_ready"), sem("hi_part"), sem("r1_ready"),
                                                                     sem("mid_part"), sem("lo_part"), sem("table_out"))
        table_buf = [sem("table_buf0"), sem("table_buf1")]
        acc_zero = sem("acc_zero")
        code_ready = sem("code_ready")
        idx_ready = sem("idx_ready")
        gath = [sem(f"gath{q}") for q in range(RING)]
        hot_ready, group_mm, acc_added = sem("hot_ready"), sem("group_mm"), sem("acc_added")
        hotx_ready, groupx_mm = sem("hotx_ready"), sem("groupx_mm")
        nd_deg, nd_sqrt, nd_m, nd_x, nd_tr, nd_t = sem("nd_deg"), sem("nd_sqrt"), sem("nd_m"), sem("nd_x"), sem("nd_tr"), sem("nd_t")
        nd_proj, nd_y, nd_yst, nd_ytr, nd_yt, nd_logit = (sem("nd_proj"), sem("nd_y"), sem("nd_yst"), sem("nd_ytr"),
                                                          sem("nd_yt"), sem("nd_logit"))
        nd_pick, nd_rank, nd_sel, nd_slot = sem("nd_pick"), sem("nd_rank"), sem("nd_sel"), sem("nd_slot")
        y2_zeroed = sem("y2_zeroed")
        nd_stored = sem("nd_stored")
        slots_mm = sem("slots_mm")
        tables_done, gb_in, gap_ready, exp_ready = sem("tables_done"), sem("gb_in"), sem("gap_ready"), sem("exp_ready")
        b1_t = sem("b1_t")
        weights_in = [sem("weights_in0"), sem("weights_in1")]
        gathered = [[sem(f"gathered{par}{k}") for k in range(MAIN)] for par in range(2)]
        scattered = [[sem(f"scattered{par}{k}") for k in range(MAIN)] for par in range(2)]
        slot_copied, tokens_t, tokens_s = sem("slot_copied"), sem("tokens_t"), sem("tokens_s")
        l1_done = [sem(f"l1_done{k}") for k in range(MAIN)]
        l2_done = [sem(f"l2_done{k}") for k in range(MAIN)]
        h1_ready, out_ready, expert_done = sem("h1_ready"), sem("out_ready"), sem("expert_done")
        xtra_copied, xtra_gathered, xtra_t, xtra_s = sem("xtra_copied"), sem("xtra_gathered"), sem("xtra_t"), sem("xtra_s")
        xtra_l1, xtra_h, xtra_l2, xtra_out, xtra_scattered = (sem("xtra_l1"), sem("xtra_h"), sem("xtra_l2"), sem("xtra_out"),
                                                              sem("xtra_scattered"))
        xtra_all, pool_starts = sem("xtra_all"), sem("pool_starts")
        y2_in = [sem("y2_in0"), sem("y2_in1")]
        combined, mean_mm, centered, squared, sq_used, var_mm = (sem("combined"), sem("mean_mm"), sem("centered"),
                                                                 sem("squared"), sem("sq_used"), sem("var_mm"))
        var_ready, var_sqrt, lnvar_ready, lnvar_sqrt = sem("var_ready"), sem("var_sqrt"), sem("lnvar_ready"), sem("lnvar_sqrt")
        xbeta, normed, stored = sem("xbeta"), sem("normed"), sem("stored")

        def nth(e, par):
            return e // 2 if isinstance(e, int) else (e - par) // 2

        def expert_loads(e, par):
            return nth(e, par) * 48 + 48

        def prior_scatter(e, par):
            return nth(e, par) * 16

        def out_bank(k):
            return banks[6 + (k + 1) % 2][:, 0:D]

        block = ctx.enter_context(nc.Block())

        T_BANKS = (4, 5, 6, 7)
        NTR = -(-EB // 4)
        LISTS = 3

        def group_code(eng, g):
            return eng.value_load(code[0:1, bass.ds(g, 1)], min_val=0, max_val=(1 << 24) - 1)

        def field(eng, c, k):
            return nc.s_assert_within(eng.snap((c >> (6 * k)) & 63), 0, NT if k > 1 else NT - 1,
                                      skip_runtime_bounds_check_because="the tables hold tiles below NT")

        def a_tile(t):
            return nc.s_assert_within(t, 0, NT - 1, skip_runtime_bounds_check_because="the codes hold tiles below NT")

        def finished_tiles(eng, g, node_tile, c=None):
            if c is None:
                c = group_code(eng, g)
            before = field(eng, c, 2)
            now = field(eng, c, 3)
            with eng.If(now > before):
                with eng.Fori(before, now) as t:
                    node_tile(a_tile(t))

        def inv_sqrt(dve, r, s, d):
            dve.reciprocal(r, s)
            dve.drain()
            dve.tensor_tensor(s, r, r, ALU.mult)
            dve.drain()
            dve.tensor_tensor(s, s, d, ALU.mult)
            dve.drain()
            dve.tensor_scalar(s, s, -0.5, 1.5, ALU.mult, ALU.add)
            dve.drain()
            dve.tensor_tensor(r, r, s, ALU.mult)

        @block.sync
        def _(sp):
            sp.wait_ge(ini, 1)
            for raw, edges, loaded in ((raw_src, src, src_loaded), (raw_dst, dst, dst_loaded)):
                nb = EB - 1
                sp.dma_start(raw[:, 0:nb, :], edges[0:nb * P * P].rearrange("(b r e) -> r b e", r=P, e=P)).then_inc(loaded, 16)
                r = EFULL - nb * P
                sp.dma_start(raw[0:r, nb, :], edges[nb * P * P:EFULL * P].rearrange("(r e) -> r e", e=P)).then_inc(loaded, 16)
                sp.dma_start(raw[r:r + 1, nb, 0:ETAIL], edges[EFULL * P:EDGES].rearrange("(r e) -> r e", r=1)).then_inc(loaded, 16)
            sp.dma_start(xs[:, 0:NT - 1, :], x[0:(NT - 1) * P, :].rearrange("(t p) d -> p t d", p=P)).then_inc(x_loaded, 16)
            sp.dma_start(xs[0:LAST, NT - 1, :], x[(NT - 1) * P:N, :]).then_inc(x_loaded, 16)
            sp.dma_start(wgc[:, :, :], W_gc.rearrange("(k p) n -> p k n", p=P)).then_inc(w_loaded, 16)
            sp.dma_start(wres[:, :, :], W_res.rearrange("(k p) n -> p k n", p=P)).then_inc(w_loaded, 16)
            sp.dma_start(wg[:, :, :], Wg.rearrange("(k p) n -> p k n", p=P)).then_inc(w_loaded, 16)
            sp.dma_start(bias[:, :], b_gc.partition_broadcast(P)).then_inc(w_loaded, 16)
            sp.dma_start(yS[:, :], b_res.partition_broadcast(P)).then_inc(w_loaded, 16)
            sp.dma_start(bgb[:, :], bg.partition_broadcast(P)).then_inc(w_loaded, 16)
            sp.dma_start(b1r[:, :], b1).then_inc(w_loaded, 16)
            y2v = y2.rearrange("(p r) d -> p (r d)", p=P)
            with sp.Fori(0, TOPK * NPAD // P // 2) as i:
                sp.dma_start(y2v[:, bass.ds(i * (2 * D), 2 * D)], zeros[:, :]).then_inc(y2_zeroed, 16)
            sp.wait_ge(mm_red, 1)
            sp.dma_start(rng[0:1, 0, :], rng_f[:, 0, :]).then_inc(mm_row, 16)
            sp.dma_start(rng[0:1, 1, :], rng_f[:, 1, :]).then_inc(mm_row, 16)
            for g in range(NB):
                sp.wait_ge(lo_part, g + 1)
                tv = table[g * TG * P:(g + 1) * TG * P, :].rearrange("(t p) r -> p t r", p=P)
                sp.dma_start(tv, parts[:, g % 2, :, :]).then_inc(table_buf[g % 2], 16)
            def weights(e, par, first):
                if not first:
                    sp.wait_ge(expert_done, e - 1)
                    sp.wait_ge(out_ready, MAIN * e - MAIN)
                sp.dma_start(w1s[:, par, :, :], w1[bass.ds(e, 1), :, :].rearrange("o (k p) h -> p (o k) h", p=P)).then_inc(weights_in[par], 16)
                sp.dma_start(w2s[:, par, :, :], w2[bass.ds(e, 1), :, :].rearrange("o (j p) d -> p (o j) d", p=P)).then_inc(weights_in[par], 16)
                sp.dma_start(b2s[:, par, :], b2[bass.ds(e, 1), :].rearrange("o d -> (o d)").partition_broadcast(P)).then_inc(weights_in[par], 16)
            sp.wait_ge(tables_done, 1)
            sp.dma_start(gb[:, 0, :], gamma.partition_broadcast(P)).then_inc(gb_in, 16)
            sp.dma_start(gb[:, 1, :], beta.partition_broadcast(P)).then_inc(gb_in, 16)
            weights(0, 0, True)
            weights(1, 1, True)
            with sp.Fori(1, EX // 2) as i:
                weights(i * 2, 0, False)
                weights(i * 2 + 1, 1, False)

            for par in range(2):
                for k in range(MAIN):
                    sp.wait_ge(scattered[par][k], 16 * EX // 2)
            sp.wait_ge(xtra_all, 1)
            sp.wait_ge(expert_done, EX)
            sp.wait_ge(out_ready, MAIN * EX)
            y2t = y2.rearrange("(k t p) d -> p k t d", k=TOPK, p=P)
            for g in range(NB):
                if g >= 2:
                    sp.wait_ge(combined, g - 1)
                for k in range(TOPK):
                    sp.dma_start(ybuf[:, g % 2, k, :, :], y2t[:, k, g * TG:(g + 1) * TG, :]).then_inc(y2_in[g % 2], 16)
            for g in range(NB):
                sp.wait_ge(normed, g + 1)
                full = TG if g < NB - 1 else TG - 1
                r = g * TG * P
                sp.dma_start(out[r:r + full * P, :].rearrange("(t p) d -> p t d", p=P), acc[:, g * TG:g * TG + full, 0:D]).then_inc(stored, 16)
            sp.dma_start(out[(NT - 1) * P:N, :], acc[0:LAST, NT - 1, 0:D]).then_inc(stored, 16)
            sp.wait_ge(stored, 16 * (NB + 1))

        @block.gpsimd
        def _(pool):
            pool.iota(iota_f[:, :], pattern=[[1, P]], base=0, channel_multiplier=0,
                      allow_small_or_imprecise_dtypes=True).then_inc(const_p, 1)
            pool.iota(iota_b[:, :], pattern=[[1, P]], base=0, channel_multiplier=0,
                      allow_small_or_imprecise_dtypes=True).then_inc(const_p, 1)
            pool.iota(pcol[:, :], pattern=[[0, 1]], base=0, channel_multiplier=1,
                      allow_small_or_imprecise_dtypes=True).then_inc(const_p, 1)
            pool.iota(iota_s[:, :], pattern=[[1, SC]], base=0, channel_multiplier=0,
                      allow_small_or_imprecise_dtypes=True).then_inc(const_p, 1)
            pool.iota(neg_tile[:, :], pattern=[[-P, NT]], base=0, channel_multiplier=0,
                      allow_small_or_imprecise_dtypes=True).then_inc(const_p, 1)
            pool.iota(hnum[:, :, :], pattern=[[NT, TOPK], [1, NT]], base=1, channel_multiplier=0,
                      allow_small_or_imprecise_dtypes=True).then_inc(const_p, 1)
            pool.memset(ring[:, :, :, 0:ROW], 0.0).then_inc(const_p, 1)
            pool.memset(ring[:, :, :, ROW:ROW + 2], 1.0).then_inc(const_p, 1)

            pool.wait_ge(tr_copied, 2 * NTR)
            pool.wait_ge(const_p, 8)

            def hist(i, first):
                for q in range(2):
                    if not first:
                        pool.wait_ge(hist_mm, i * 2 + (q - 1))
                    pool.tensor_tensor(hi_hot[:, q, :, :],
                                       iota_f[:, 0:NT].unsqueeze(1).to_broadcast([P, HB, NT]),
                                       hiT[:, bass.ds((i * 2 + q) * HB, HB)].unsqueeze(2).to_broadcast([P, HB, NT]),
                                       ALU.subtract).then_inc(hi_diff, 1)
            hist(0, True)
            with pool.Fori(1, HSTEPS) as i:
                hist(i, False)

            pool.wait_ge(rs_ready, 1)
            pool.wait_ge(x_loaded, 32)
            for g in range(NB):
                pool.tensor_tensor(acc[:, g * TG:(g + 1) * TG, 0:D], xs[:, g * TG:(g + 1) * TG, :],
                                   rs[:, g * TG:(g + 1) * TG].unsqueeze(2).to_broadcast([P, TG, D]),
                                   ALU.mult).then_inc(h_ready, 1)

            node_reg, row_reg = pool.alloc_register("last_node"), pool.alloc_register("last_row")
            pool.reg_mov(node_reg, N - 1)
            pool.reg_mov(row_reg, TOPK * NPAD - 1)
            last_node, last_row = node_reg, row_reg

            def start():
                pool.sem_inc(pool_starts, 1)

            for q in range(2):
                pool.wait_ge(table_buf[q], 16 * ((NB + 1 - q) // 2))

            def gather(it, first):
                for q in range(RING):
                    pool.wait_ge(idx_ready, it * RING + (q + 1))
                    if not first:
                        pool.wait_ge(group_mm, it * RING + (q - RING + 1))
                    start()
                    for j in range(CPG):
                        pool.indirect_dma_start(
                            out=ring[:, q, j, 0:ROW], out_offset=None, in_=table[:, :],
                            in_offset=bass.IndirectOffsetOnAxis(ap=ring_idx[:, q, j:j + 1], axis=0),
                            bounds_check=last_node, oob_is_err=False).then_inc(gath[q], 16)
            gather(0, True)
            with pool.Fori(1, STEPS) as it:
                gather(it, False)

            pool.wait_ge(y2_zeroed, 16 * (TOPK * NPAD // P // 2))
            pool.wait_ge(tables_done, 1)
            pool.wait_ge(gb_in, 32)
            pool.wait_ge(nd_stored, 16 * NT + 16)

            def load_slots(e, par, first):
                if not first:
                    pool.wait_ge(tokens_t, e - 1)
                    for k in range(MAIN):
                        pool.wait_ge(scattered[par][k], prior_scatter(e, par))
                    start()
                pool.tensor_copy(slot_idx[:, par, 0, :], gidx[:, bass.ds(e * SLOTCH, MAIN)])
                pool.tensor_copy(slot_idx[:, par, 1, :], sidx[:, bass.ds(e * SLOTCH, MAIN)]).then_inc(slot_copied, 1)
                pool.wait_ge(slot_copied, e + 1)
                start()
                for k in range(MAIN):
                    pool.indirect_dma_start(
                        out=xg[:, par, k, :], out_offset=None, in_=nodes[:, :],
                        in_offset=bass.IndirectOffsetOnAxis(ap=slot_idx[:, par, 0, k:k + 1], axis=0),
                        bounds_check=last_node, oob_is_err=False).then_inc(gathered[par][k], 16)

            def store_slots(e, par):
                for k in reversed(range(MAIN)):
                    pool.wait_ge(out_ready, e * MAIN + (MAIN - k))
                    start()
                    pool.indirect_dma_start(
                        out=y2[:, :], out_offset=bass.IndirectOffsetOnAxis(ap=slot_idx[:, par, 1, k:k + 1], axis=0),
                        in_=outs[:, par, k, :], in_offset=None,
                        bounds_check=last_row, oob_is_err=False).then_inc(scattered[par][k], 16)

            nextra = pool.alloc_register("pool_nextra")
            pool.reg_mov(nextra, 0)

            def extra_chunks(e, nch):
                with pool.If(nch > MAIN):
                    with pool.Fori(MAIN, nch) as k:
                        col = nc.s_assert_within(e * SLOTCH + k, 0, SC - 1,
                                                 skip_runtime_bounds_check_because="no expert has more than SLOTCH chunks")
                        pool.reg_add(nextra, nextra, 1)
                        n = pool.snap(nextra, min_val=1, max_val=EX * SLOTCH)
                        pool.tensor_copy(xtra_idx[:, 0:1], gidx[:, bass.ds(col, 1)])
                        pool.tensor_copy(xtra_idx[:, 1:2], sidx[:, bass.ds(col, 1)]).then_inc(xtra_copied, 1)
                        pool.wait_ge(xtra_copied, n)
                        start()
                        pool.indirect_dma_start(
                            out=xgx[:, :], out_offset=None, in_=nodes[:, :],
                            in_offset=bass.IndirectOffsetOnAxis(ap=xtra_idx[:, 0:1], axis=0),
                            bounds_check=last_node, oob_is_err=False).then_inc(xtra_gathered, 16)
                        pool.wait_ge(xtra_out, n)
                        start()
                        pool.indirect_dma_start(
                            out=y2[:, :], out_offset=bass.IndirectOffsetOnAxis(ap=xtra_idx[:, 1:2], axis=0),
                            in_=outx[:, :], in_offset=None,
                            bounds_check=last_row, oob_is_err=False).then_inc(xtra_scattered, 16)
                        pool.wait_ge(xtra_scattered, n * 16)
                        start()

            def chunks_of(e):
                return pool.value_load(nch_i[0:1, bass.ds(e, 1)], min_val=1, max_val=SLOTCH)

            def expert(e, par, first, final=False):
                extra_chunks(e, chunks_of(e))
                if not final:
                    load_slots(e + 1, 1 - par, first and par == 0)
                store_slots(e, par)

            load_slots(0, 0, True)
            expert(0, 0, True)
            expert(1, 1, True)
            with pool.Fori(1, EX // 2 - 1) as i:
                expert(i * 2, 0, False)
                expert(i * 2 + 1, 1, False)
            expert(EX - 2, 0, False)
            expert(EX - 1, 1, False, True)
            pool.drain().then_inc(xtra_all, 1)
            for t in range(NB):
                pool.tensor_tensor(xs[:, t * TG:(t + 1) * TG, :], xs[:, t * TG:(t + 1) * TG, :],
                                   gb[:, 1, :].unsqueeze(1).to_broadcast([P, TG, D]), ALU.add).then_inc(xbeta, TG)

        @block.scalar
        def _(act):
            n = 0
            for which in range(LISTS):
                target = (loT, hiT, dstT)[which]
                for c in range(NTR):
                    w = min(4, EB - 4 * c) * P
                    act.wait_ge(tr_done, n + 1)
                    act.activation(target[:, c * 512:c * 512 + w], banks[T_BANKS[n % 4]][:, 0:w], ACT.Copy).then_inc(tr_copied, 1)
                    n += 1
            act.wait_ge(deg_ready, 1)
            act.activation(tmp[:, :], deg[:, :], ACT.Sqrt).then_inc(deg_sqrt, 1)
            for g in range(NB):
                hv = acc[:, g * TG:(g + 1) * TG, 0:D]
                if g >= 2:
                    act.wait_ge(table_buf[g % 2], 16 * (g // 2))
                act.wait_ge(h_ready, g + 1)
                act.activation(parts[:, g % 2, :, 2 * D:3 * D], hv, ACT.Copy).then_inc(hi_part, 1)
                act.wait_ge(r1_ready, g + 1)
                act.activation(parts[:, g % 2, :, D:2 * D], hv, ACT.Copy).then_inc(mid_part, 1)

            act.sem_inc(nd_stored, 16)
            act.wait_ge(b1_t, 1)
            act.activation(b1T[:, :, :], banks[3][:, 0:HK * EX], ACT.Copy)
            act.drain()
            act.wait_ge(code_ready, 1)

            def indices(it, q, first):
                if not first:
                    act.wait_ge(gath[q], it * (16 * CPG))
                act.activation(ring_idx[:, q, :], srcT[:, bass.ds((it * RING + q) * CPG, CPG)], ACT.Copy).then_inc(idx_ready, 1)

            def node_tile(t):
                act.wait_ge(nd_deg, t + 1)
                act.activation(nd[:, 1:2], nd[:, 0:1], ACT.Sqrt).then_inc(nd_sqrt, 1)
                act.activation(xS[:, :], xs[:, bass.ds(t, 1), :], ACT.Copy).then_inc(nd_x, 1)
                act.wait_ge(nd_tr, t + 1)
                act.activation(tS[:, :, :], banks[3][:, :], ACT.Copy).then_inc(nd_t, 1)
                act.wait_ge(nd_y, t + 1)
                act.dma_start(nodes[bass.ds(t * P, P), :], yS[:, :]).then_inc(nd_stored, 16)
                act.activation(acc[:, bass.ds(t, 1), 0:D], yS[:, :], ACT.Copy).then_inc(nd_yst, 1)
                act.wait_ge(nd_ytr, t + 1)
                act.activation(ytS[:, :, :], banks[3][:, 0:D], ACT.Copy).then_inc(nd_yt, 1)

            LEAD = 2
            for q in range(LEAD):
                indices(0, q, True)

            def step(it, first):
                for q in range(RING):
                    ahead = q + LEAD
                    indices(it + ahead // RING, ahead % RING, first and ahead < RING)
                    finished_tiles(act, it * RING + q, node_tile)
            step(0, True)
            with act.Fori(1, STEPS - 1) as it:
                step(it, False)
            it = STEPS - 1
            for q in range(RING):
                if q + LEAD < RING:
                    indices(it, q + LEAD, False)
                finished_tiles(act, it * RING + q, node_tile)

            act.wait_ge(gap_ready, 1)
            act.activation(gate[:, :, 1], gate[:, :, 1], ACT.Exp).then_inc(exp_ready, 1)
            nextra = act.alloc_register("act_nextra")
            act.reg_mov(nextra, 0)

            def expert(e, first):
                act.drain()
                act.activation(b1e[:, :], b1T[:, :, bass.ds(e, 1)], ACT.Copy)
                act.drain()
                nch = act.value_load(nch_i[0:1, bass.ds(e, 1)], min_val=1, max_val=SLOTCH)
                with act.If(nch > MAIN):
                    with act.Fori(MAIN, nch) as k:
                        act.reg_add(nextra, nextra, 1)
                        n = act.snap(nextra, min_val=1, max_val=EX * SLOTCH)
                        act.wait_ge(xtra_l1, n)
                        for j in range(HK):
                            last = act.activation(h1x[:, j, :], banks[5][:, j * P:(j + 1) * P], ACT.Gelu,
                                                  bias=b1e[:, j:j + 1])
                        last.then_inc(xtra_h, 1)
                for k in range(MAIN):
                    act.wait_ge(l1_done[k], e + 1)
                    if not first:
                        act.wait_ge(l2_done[k], e)
                    for j in range(HK):
                        last = act.activation(h1[:, k, j, :], banks[2 + k][:, j * P:(j + 1) * P], ACT.Gelu,
                                              bias=b1e[:, j:j + 1])
                    last.then_inc(h1_ready, 1)
            expert(0, True)
            with act.Fori(1, EX) as e:
                expert(e, False)
            for g in range(NB):
                act.wait_ge(centered, g + 1)
                if g >= 2:
                    act.wait_ge(sq_used, g - 1)
                act.activation(sq[:, g % 2, :, :], acc[:, g * TG:(g + 1) * TG, 0:D], ACT.Square).then_inc(squared, 1)
            act.wait_ge(var_ready, 1)
            act.activation(vroot[:, :], var[:, :], ACT.Sqrt).then_inc(var_sqrt, 1)
            act.wait_ge(lnvar_ready, 1)
            act.activation(tmp[:, :], deg[:, :], ACT.Sqrt).then_inc(lnvar_sqrt, 1)

        @block.vector
        def _(dve):
            dve.memset(raw_src[:, EB - 1, :], PAD_SRC)
            dve.memset(raw_dst[:, EB - 1, :], PAD_DST)
            dve.memset(xs[:, NT - 1, :], 0.0)
            dve.memset(zeros[:, :], 0.0)
            dve.drain().then_inc(ini, 1)
            dve.memset(ones[:, :], 1.0)
            dve.memset(ones_b[:, :], 1.0)
            dve.memset(taken[:, :], 0.0)
            dve.memset(valid[:, :], 1.0)
            dve.wait_ge(const_p, 6)
            dve.tensor_scalar(ident[:, :], iota_f[:, :], pcol[:, 0:1], None, ALU.is_equal)
            dve.tensor_scalar(tri[:, :], iota_f[:, :], pcol[:, 0:1], None, ALU.is_gt)
            dve.drain()
            dve.tensor_scalar(valid[:, NT - 1:NT], pcol[:, :], float(LAST), None, ALU.is_lt)
            dve.drain()
            dve.tensor_scalar(inval[:, :], valid[:, :], -8192.0, 8192.0, ALU.mult, ALU.add)
            dve.tensor_scalar(ones_last[:, :], ones[:, :], valid[:, NT - 1:NT], None, ALU.mult)
            dve.drain().then_inc(const_d, 1)
            dve.wait_ge(src_loaded, 48)
            s_lo, s_hi = stage[:, 0:COLS].bitcast(I32), stage[:, COLS:2 * COLS].bitcast(I32)
            flat = raw_src[:, :, :].rearrange("p b e -> p (b e)")
            dve.tensor_scalar(s_lo, flat, P - 1, None, ALU.bitwise_and)
            dve.drain()
            dve.tensor_copy(stage[:, 2 * COLS:3 * COLS], s_lo).then_inc(srch_f, 1)
            dve.tensor_scalar(s_hi, flat, 7, None, ALU.arith_shift_right)
            dve.drain()
            dve.tensor_copy(stage[:, 3 * COLS:4 * COLS], s_hi).then_inc(srch_f, 1)
            dve.wait_ge(dst_loaded, 48)
            dstf = srcT[:, :]
            dve.tensor_copy(dstf, raw_dst[:, :, :].rearrange("p b e -> p (b e)")).then_inc(dst_f, 1)
            dve.drain()
            dv = dstf.rearrange("p (b e) -> p b e", e=P)
            dve.tensor_reduce(mnmx[:, 0, :], dv, op=ALU.min, axis=AX.X)
            dve.tensor_reduce(mnmx[:, 1, :], dv, op=ALU.max, axis=AX.X).then_inc(dst_f, 1)

            dve.wait_ge(tr_copied, 2 * NTR)

            def hist(i, first):
                for q in range(2):
                    if not first:
                        dve.wait_ge(hist_mm, i * 2 + (q - 1))
                    for c in range(HB):
                        last = dve.tensor_scalar(lo_hot[:, q, c, :], iota_b[:, :],
                                                 loT[:, bass.ds((i * 2 + q) * HB + c, 1)], None, ALU.is_equal)
                    last.then_inc(lo_ready, 1)
                    dve.wait_ge(hi_diff, i * 2 + (q + 1))
                    dve.tensor_scalar(hi_hot[:, q, :, :], hi_hot[:, q, :, :], 0.0, None, ALU.is_equal).then_inc(hi_ready, 1)
            hist(0, True)
            with dve.Fori(1, HSTEPS) as i:
                hist(i, False)
            dve.wait_ge(tr_copied, LISTS * NTR)
            dve.scalar_tensor_tensor(srcT[:, :], hiT[:, :], float(P), loT[:, :], ALU.mult, ALU.add)
            dve.wait_ge(hist_mm, 2 * HSTEPS)
            dve.tensor_scalar(deg[:, :], banks[0][:, 0:NT], 1.0, None, ALU.max).then_inc(deg_ready, 1)
            dve.wait_ge(deg_sqrt, 1)
            inv_sqrt(dve, rs[:, :], tmp[:, :], deg[:, :])
            dve.drain().then_inc(rs_ready, 1)

            dve.wait_ge(mm_tr, 1)
            groups = P // CPG
            mt = banks[1][0:EB, 0:2 * P].rearrange("p (a g c) -> p a g c", a=2, c=CPG)
            dve.tensor_reduce(rng_f[:, 0, :], mt[:, 0, :, :], op=ALU.min, axis=AX.X)
            dve.tensor_reduce(rng_f[:, 1, :], mt[:, 1, :, :], op=ALU.max, axis=AX.X)
            dve.drain()
            dve.tensor_copy(rng_i[:, :, :], rng_f[:, :, :])
            dve.drain()
            dve.tensor_scalar(rng_i[:, :, :], rng_i[:, :, :], 7, None, ALU.arith_shift_right)
            dve.drain()
            dve.tensor_scalar(rng_f[:, :, :], rng_i[:, :, :], float(NT - 1), None, ALU.min).then_inc(mm_red, 1)
            dve.memset(sfx[:, :, :], float(NT))
            for g in range(NB):
                hv = acc[:, g * TG:(g + 1) * TG, 0:D]
                pv = parts[:, g % 2, :, :]
                dve.wait_ge(hi_part, g + 1)
                dve.tensor_tensor(hv, hv, pv[:, :, 2 * D:3 * D], ALU.subtract).then_inc(r1_ready, 1)
                dve.wait_ge(mid_part, g + 1)
                dve.tensor_tensor(pv[:, :, 0:D], hv, pv[:, :, D:2 * D], ALU.subtract).then_inc(lo_part, 1)
            dve.wait_ge(mm_row, 32)
            dve.tensor_copy(sfx[:, 0, 0:GROUPS], rng[:, 0, 0:GROUPS])
            a, k = 0, 1
            while k < GROUPS:
                dve.drain()
                dve.tensor_tensor(sfx[:, 1 - a, 0:GROUPS], sfx[:, a, 0:GROUPS], sfx[:, a, k:GROUPS + k], ALU.min)
                a, k = 1 - a, 2 * k
            dve.drain()
            dve.scalar_tensor_tensor(code_f[:, :], rng[:, 1, :], 64.0, rng[:, 0, :], ALU.mult, ALU.add)
            dve.drain()
            dve.scalar_tensor_tensor(code_f[:, 1:GROUPS], sfx[:, a, 1:GROUPS], 64.0 ** 2, code_f[:, 1:GROUPS], ALU.mult, ALU.add)
            dve.drain()
            dve.scalar_tensor_tensor(code_f[:, 0:GROUPS], sfx[:, a, 1:GROUPS + 1], 64.0 ** 3, code_f[:, 0:GROUPS], ALU.mult, ALU.add)
            dve.drain()
            dve.tensor_copy(code[:, :], code_f[:, :]).then_inc(code_ready, 1)
            dve.wait_ge(nb_done, 1)
            dve.tensor_scalar(neg_base[:, :], banks[1][:, 0:GCOLS], -float(P), None, ALU.mult)
            dve.memset(acc[:, :, :], 0.0)
            dve.wait_ge(w_loaded, 16 * 7)
            dve.tensor_tensor(bias[:, :], bias[:, :], yS[:, :], ALU.add)
            dve.drain()

            extra = dve.alloc_register("dve_extra")
            dve.reg_mov(extra, 0)

            def one_hots(it, q, first):
                if not first:
                    dve.wait_ge(group_mm, it * RING + (q - RING + 1))
                for j in range(CPG):
                    last = dve.tensor_scalar(hot[:, q, j, :], iota_b[:, :],
                                             dstT[:, bass.ds((it * RING + q) * CPG + j, 1)],
                                             neg_base[:, bass.ds(it * RING + q, 1)], ALU.subtract, ALU.is_equal)
                last.then_inc(hot_ready, 1)

            def extras(g, c):
                first_tile, last_tile = field(dve, c, 0), field(dve, c, 1)
                with dve.If(last_tile > first_tile):
                    with dve.Fori(first_tile + 1, last_tile + 1) as tile:
                        t = a_tile(tile)
                        dve.reg_add(extra, extra, 1)
                        n = dve.snap(extra, min_val=1, max_val=GROUPS * NT)
                        for j in range(CPG):
                            last = dve.tensor_scalar(hotx[:, j, :], iota_b[:, :], dstT[:, bass.ds(g * CPG + j, 1)],
                                                     neg_tile[:, bass.ds(t, 1)], ALU.subtract, ALU.is_equal)
                        last.then_inc(hotx_ready, 1)
                        dve.drain()
                        dve.wait_ge(groupx_mm, n)
                        dve.tensor_tensor(acc[:, bass.ds(t, 1), :], acc[:, bass.ds(t, 1), :],
                                          banks[2][:, 0:D + 1], ALU.add)
                return first_tile

            def node_tile(t):
                dve.drain()
                dve.tensor_scalar(nd[:, 0:1], acc[:, bass.ds(t, 1), D:D + 1], 1.0, None, ALU.max).then_inc(nd_deg, 1)
                dve.wait_ge(nd_sqrt, t + 1)
                inv_sqrt(dve, nd[:, 2:3], nd[:, 1:2], nd[:, 0:1])
                dve.drain()
                dve.tensor_scalar(mS[:, :], acc[:, bass.ds(t, 1), 0:D], nd[:, 2:3], None, ALU.mult).then_inc(nd_m, 1)
                dve.wait_ge(nd_proj, t + 1)
                dve.wait_ge(nd_stored, t * 16 + 16)
                dve.tensor_tensor(yS[:, :], banks[4][:, 0:D], bias[:, :], ALU.add).then_inc(nd_y, 1)
                dve.wait_ge(nd_logit, t + 1)
                dve.tensor_tensor(lg[:, :], banks[5][:, 0:EX], bgb[:, :], ALU.add)
                dve.drain()
                dve.max(v8[:, :], lg[:, :])
                dve.drain()
                dve.max_index(i8[:, :], v8[:, :], lg[:, :])
                dve.tensor_copy(top[:, bass.ds(t, 1), :], v8[:, 0:TOPK])
                dve.drain()
                dve.tensor_copy(i8f[:, :], i8[:, 0:TOPK])
                dve.drain()
                for k in range(TOPK):
                    dve.tensor_scalar(pick[:, k, :], iota_b[:, 0:EX], i8f[:, k:k + 1], valid[:, bass.ds(t, 1)],
                                      ALU.is_equal, ALU.mult)
                dve.drain()
                dve.tensor_tensor(picked[:, :], pick[:, 0, :], pick[:, 1, :], ALU.add).then_inc(nd_pick, 1)
                dve.drain()
                dve.wait_ge(nd_rank, t + 1)
                for k in range(TOPK):
                    dve.tensor_tensor_reduce(out=junk[:, :], in0=pick[:, k, :], in1=banks[5][:, P:P + EX], scale=1.0,
                                             scalar=0.0, op0=ALU.mult, op1=ALU.add, accum_out=rk[:, k:k + 1])
                    dve.drain()
                dve.tensor_tensor(taken[:, :], taken[:, :], picked[:, :], ALU.add)
                dve.tensor_copy(rki[:, 0, :], rk[:, :])
                dve.tensor_copy(rank[:, bass.ds(t, 1), :], rk[:, :])
                dve.drain()
                dve.tensor_scalar(rki[:, 1, :], rki[:, 0, :], P - 1, None, ALU.bitwise_and)
                dve.tensor_scalar(rki[:, 2, :], rki[:, 0, :], 7, None, ALU.arith_shift_right)
                dve.drain()
                dve.tensor_copy(rkf[:, :, :], rki[:, 1:3, :])
                dve.drain()
                dve.scalar_tensor_tensor(qs[:, :], i8f[:, :], float(SLOTCH), rkf[:, 1, :], ALU.mult, ALU.add)
                dve.tensor_scalar(rk[:, :], rkf[:, 1, :], float(SLOTCH), 8192.0, ALU.is_ge, ALU.mult)
                dve.drain()
                dve.scalar_tensor_tensor(qs[:, :], rk[:, :], inval[:, bass.ds(t, 1)], qs[:, :], ALU.add, ALU.add)
                dve.drain()
                for k in range(TOPK):
                    dve.tensor_scalar(sel[:, k, :], iota_s[:, :], qs[:, k:k + 1], None, ALU.is_equal)
                    dve.tensor_scalar(lo1[:, k, 0, :], iota_b[:, :], rkf[:, 0, k:k + 1], hnum[:, k, bass.ds(t, 1)],
                                      ALU.is_equal, ALU.mult)
                    last = dve.tensor_scalar(lo1[:, k, 1, :], iota_b[:, :], rkf[:, 0, k:k + 1], pcol[:, 0:1],
                                             ALU.is_equal, ALU.mult)
                last.then_inc(nd_sel, 1)

            one_hots(0, 0, True)

            def step(it, first, final=False):
                for q in range(RING):
                    g = it * RING + q
                    if q + 1 < RING:
                        one_hots(it, q + 1, first)
                    elif not final:
                        one_hots(it + 1, 0, False)
                    c = group_code(dve, g)
                    first_tile = extras(g, c)
                    dve.drain()
                    dve.wait_ge(group_mm, g + 1)
                    dve.tensor_tensor(acc[:, bass.ds(first_tile, 1), :], acc[:, bass.ds(first_tile, 1), :],
                                      banks[q % 2][:, 0:D + 1], ALU.add).then_inc(acc_added, 1)
                    finished_tiles(dve, g, node_tile, c)
            step(0, True)
            with dve.Fori(1, STEPS - 1) as it:
                step(it, False)
            step(STEPS - 1, False, True)

            dve.wait_ge(slots_mm, 1)
            dve.tensor_scalar(tok_t, banks[6][:, :], float(P), -float(P), ALU.mult, ALU.add)
            dve.drain()
            dve.tensor_tensor(tok_f, tok_t, banks[7][:, :], ALU.add)
            dve.drain()
            dve.tensor_scalar(tok_t, tok_f, 0.0, UNUSED, ALU.is_lt, ALU.mult)
            dve.drain()
            dve.tensor_tensor(tok_f, tok_f, tok_t, ALU.add)
            dve.drain()
            dve.tensor_copy(sidx[:, :], tok_f)
            dve.tensor_scalar(tok_t, tok_f, float(NPAD), -float(NPAD), ALU.is_ge, ALU.mult)
            dve.drain()
            dve.tensor_tensor(tok_f, tok_f, tok_t, ALU.add)
            dve.drain()
            dve.tensor_copy(gidx[:, :], tok_f)
            dve.tensor_scalar(nch_f[:, :], banks[5][0:1, 2 * P:2 * P + EX], float(CAP), float(P - 1), ALU.min, ALU.add)
            dve.drain()
            dve.tensor_copy(nch_i[:, :], nch_f[:, :])
            dve.drain()
            dve.tensor_scalar(nch_i[:, :], nch_i[:, :], 7, None, ALU.arith_shift_right)
            dve.drain()
            dve.tensor_scalar(nch_f[:, :], nch_i[:, :], 1.0, None, ALU.max)
            dve.drain()
            dve.tensor_copy(nch_i[:, :], nch_f[:, :])
            dve.memset(xg[:, :, :, :], 0.0)
            dve.memset(xgx[:, :], 0.0)
            dve.drain().then_inc(tables_done, 1)
            dve.tensor_tensor(gate[:, :, 1], top[:, :, 1], top[:, :, 0], ALU.subtract).then_inc(gap_ready, 1)
            dve.wait_ge(exp_ready, 1)
            dve.tensor_scalar(gate[:, :, 0], gate[:, :, 1], 1.0, None, ALU.add)
            dve.drain()
            dve.reciprocal(gate[:, :, 0], gate[:, :, 0])
            dve.drain()
            dve.tensor_tensor(gate[:, :, 1], gate[:, :, 1], gate[:, :, 0], ALU.mult)
            dve.tensor_scalar(rank[:, :, :], rank[:, :, :], float(CAP), None, ALU.is_lt)
            dve.drain()
            dve.tensor_tensor(gate[:, :, :], gate[:, :, :], rank[:, :, :], ALU.mult)

            def to_sbuf(e):
                dve.wait_ge(tokens_t, e + 1)
                dve.tensor_copy(xgT[:, 0:2, :, :], banks[0][:, :])
                dve.tensor_copy(xgT[:, 2, :, :], banks[1][:, 0:D]).then_inc(tokens_s, 1)

            nextra = dve.alloc_register("dve_nextra")
            dve.reg_mov(nextra, 0)

            def extra_chunks(e, par, nch):
                with dve.If(nch > MAIN):
                    with dve.Fori(MAIN, nch) as k:
                        dve.reg_add(nextra, nextra, 1)
                        n = dve.snap(nextra, min_val=1, max_val=EX * SLOTCH)
                        dve.wait_ge(xtra_t, n)
                        dve.tensor_copy(xgTx[:, :, :], banks[1][:, D:2 * D]).then_inc(xtra_s, 1)
                        dve.wait_ge(xtra_l2, n)
                        dve.tensor_tensor(outx[:, :], banks[6][:, 0:D], b2s[:, par, :], ALU.add).then_inc(xtra_out, 1)

            def expert(e, par, first, final=False):
                nch = dve.value_load(nch_i[0:1, bass.ds(e, 1)], min_val=1, max_val=SLOTCH)
                extra_chunks(e, par, nch)
                if not final:
                    to_sbuf(e + 1)
                dve.wait_ge(weights_in[par], expert_loads(e, par))
                for k in reversed(range(MAIN)):
                    dve.wait_ge(l2_done[k], e + 1)
                    if not first:
                        dve.wait_ge(scattered[par][k], prior_scatter(e, par))
                    dve.tensor_tensor(outs[:, par, k, :], out_bank(k), b2s[:, par, :], ALU.add).then_inc(out_ready, 1)
            to_sbuf(0)
            expert(0, 0, True)
            expert(1, 1, True)
            with dve.Fori(1, EX // 2 - 1) as i:
                expert(i * 2, 0, False)
                expert(i * 2 + 1, 1, False)
            expert(EX - 2, 0, False)
            expert(EX - 1, 1, False, True)

            dve.drain()
            for g in range(NB):
                dve.wait_ge(y2_in[g % 2], 16 * TOPK * (g // 2 + 1))
                for k in range(TOPK):
                    for t in range(TG):
                        tile = g * TG + t
                        last = dve.scalar_tensor_tensor(acc[:, tile, 0:D], ybuf[:, g % 2, k, t, :], gate[:, tile, k:k + 1],
                                                        acc[:, tile, 0:D], ALU.mult, ALU.add)
                    if k == 0:
                        dve.drain()
                last.then_inc(combined, 1)
            dve.wait_ge(mean_mm, 1)
            dve.tensor_scalar(mean[:, :], banks[0][:, 0:D], 1.0 / N, None, ALU.mult)
            dve.drain()
            for g in range(NB):
                yv = acc[:, g * TG:(g + 1) * TG, 0:D]
                dve.tensor_tensor(yv, yv, mean[:, :].unsqueeze(1).to_broadcast([P, TG, D]), ALU.subtract).then_inc(centered, 1)
            dve.wait_ge(var_mm, 1)
            dve.tensor_scalar(var[:, :], banks[1][:, 0:D], 1.0 / N, BN_EPS, ALU.mult, ALU.add).then_inc(var_ready, 1)
            dve.wait_ge(var_sqrt, 1)
            inv_sqrt(dve, scale[:, :], vroot[:, :], var[:, :])
            dve.drain()
            dve.tensor_tensor(scale[:, :], scale[:, :], gb[:, 0, :], ALU.mult)
            dve.drain()
            for g in range(NB):
                yv = acc[:, g * TG:(g + 1) * TG, 0:D]
                dve.tensor_tensor(yv, yv, scale[:, :].unsqueeze(1).to_broadcast([P, TG, D]), ALU.mult)
                dve.drain()
                dve.wait_ge(xbeta, NT)
                dve.tensor_tensor(yv, yv, xs[:, g * TG:(g + 1) * TG, :], ALU.add)
                dve.drain()
                for t in range(TG):
                    dve.bn_stats(stats[:, t, :], acc[:, g * TG + t, 0:D])
                dve.drain()
                for t in range(TG):
                    dve.bn_aggr(mv[:, g * TG + t, :], stats[:, t, :])
                dve.drain()
            dve.tensor_scalar(deg[:, :], mv[:, :, 1], LN_EPS, None, ALU.add).then_inc(lnvar_ready, 1)
            dve.wait_ge(lnvar_sqrt, 1)
            inv_sqrt(dve, rs[:, :], tmp[:, :], deg[:, :])
            dve.drain()
            for g in range(NB):
                for t in range(TG):
                    tile = g * TG + t
                    last = dve.tensor_scalar(acc[:, tile, 0:D], acc[:, tile, 0:D], mv[:, tile, 0:1], rs[:, tile:tile + 1],
                                             ALU.subtract, ALU.mult)
                last.then_inc(normed, 1)

        @block.tensor
        def _(pe):
            pe.wait_ge(const_d, 1)
            n = 0
            for which in range(LISTS):
                if which < 2:
                    pe.wait_ge(srch_f, which + 1)
                    lists = stage[:, (2 + which) * COLS:(3 + which) * COLS]
                else:
                    pe.wait_ge(dst_f, 1)
                    lists = srcT[:, :]
                for c in range(NTR):
                    if n >= 4:
                        pe.wait_ge(tr_copied, n - 3)
                    for j in range(min(4, EB - 4 * c)):
                        b = 4 * c + j
                        last = pe.transpose(banks[T_BANKS[n % 4]][:, j * P:(j + 1) * P], lists[:, b * P:(b + 1) * P], ident[:, :])
                    last.then_inc(tr_done, 1)
                    n += 1
            pe.wait_ge(dst_f, 2)
            for a in range(2):
                last = pe.transpose(banks[1][0:EB, a * P:(a + 1) * P], mnmx[:, a, :], ident[:, :])
            last.then_inc(mm_tr, 1)


            def hist(i, first, final=False):
                for q in range(2):
                    pe.wait_ge(lo_ready, i * 2 + (q + 1))
                    pe.wait_ge(hi_ready, i * 2 + (q + 1))
                    for c in range(HB):
                        last = pe.matmul(banks[0][:, 0:NT], lo_hot[:, q, c, :], hi_hot[:, q, c, :],
                                         start=first and q == 0 and c == 0, stop=final and q == 1 and c == HB - 1,
                                         skip_group_check=True)
                    last.then_inc(hist_mm, 1)
            hist(0, True)
            with pe.Fori(1, HSTEPS - 1) as i:
                hist(i, False)
            hist(HSTEPS - 1, False, True)

            pe.wait_ge(mm_row, 32)
            pe.matmul(banks[1][:, 0:GCOLS], ones[0:1, :], rng[0:1, 0, :], start=True, stop=True).then_inc(nb_done, 1)
            pe.wait_ge(code_ready, 1)

            extra = pe.alloc_register("pe_extra")
            pe.reg_mov(extra, 0)

            def multiply(bank, hots, q, done):
                for j in range(CPG):
                    for part in (2, 1, 0):
                        w = D + 1 if part == 2 else D
                        last = pe.matmul(bank[:, 0:w], hots[:, j, :], ring[:, q, j, part * D:part * D + w],
                                         start=j == 0 and part == 2, stop=j == CPG - 1 and part == 0,
                                         skip_group_check=True)
                last.then_inc(done, 1)

            def node_tile(t):
                pe.wait_ge(nd_m, t + 1)
                for k in range(DK):
                    pe.transpose(banks[3][:, k * P:(k + 1) * P], mS[:, k * P:(k + 1) * P], ident[:, :])
                pe.wait_ge(nd_x, t + 1)
                for k in range(DK):
                    last = pe.transpose(banks[3][:, (DK + k) * P:(DK + k + 1) * P], xS[:, k * P:(k + 1) * P], ident[:, :])
                last.then_inc(nd_tr, 1)
                pe.wait_ge(nd_t, t + 1)
                for k in range(2 * DK):
                    last = pe.matmul(banks[4][:, 0:D], tS[:, k, :], (wgc if k < DK else wres)[:, k % DK, :],
                                     start=k == 0, stop=k == 2 * DK - 1)
                last.then_inc(nd_proj, 1)
                pe.wait_ge(nd_y, t + 1)
                for k in range(DK):
                    last = pe.transpose(banks[3][:, k * P:(k + 1) * P], yS[:, k * P:(k + 1) * P], ident[:, :])
                last.then_inc(nd_ytr, 1)
                pe.wait_ge(nd_yt, t + 1)
                for k in range(DK):
                    last = pe.matmul(banks[5][:, 0:EX], ytS[:, k, :], wg[:, k, :], start=k == 0, stop=k == DK - 1)
                last.then_inc(nd_logit, 1)
                pe.wait_ge(nd_pick, t + 1)
                pe.matmul(banks[5][:, P:P + EX], tri[:, :], picked[:, :], start=True, stop=False)
                pe.matmul(banks[5][:, P:P + EX], ones_b[:, :], taken[:, :], start=False, stop=True).then_inc(nd_rank, 1)
                pe.wait_ge(nd_sel, t + 1)
                for k in range(TOPK):
                    for a in range(2):
                        last = pe.matmul(banks[6 + a][:, :], lo1[:, k, a, :], sel[:, k, :], start=False, stop=False,
                                         skip_group_check=True)
                last.then_inc(nd_slot, 1)

            pe.wait_ge(w_loaded, 16 * 7)
            for j in range(HK):
                last = pe.transpose(banks[3][:, j * EX:(j + 1) * EX], b1r[:, j * P:(j + 1) * P], ident[0:EX, 0:EX])
            last.then_inc(b1_t, 1)
            zb = zeros[:, :].bitcast(BF16)
            pe.wait_ge(tr_copied, LISTS * NTR)
            for a in range(2):
                pe.matmul(banks[6 + a][:, :], zb[:, 0:P], zb[:, 0:SC], start=True, stop=False, skip_group_check=True)

            def step(it, first):
                for q in range(RING):
                    g = it * RING + q
                    c = group_code(pe, g)
                    first_tile, last_tile = field(pe, c, 0), field(pe, c, 1)
                    pe.wait_ge(gath[q], it * (16 * CPG) + 16 * CPG)
                    with pe.If(last_tile > first_tile):
                        with pe.Fori(first_tile + 1, last_tile + 1) as t:
                            pe.reg_add(extra, extra, 1)
                            n = pe.snap(extra, min_val=1, max_val=GROUPS * NT)
                            pe.wait_ge(hotx_ready, n)
                            multiply(banks[2], hotx, q, groupx_mm)
                    pe.wait_ge(hot_ready, g + 1)
                    if not (first and q < 2):
                        pe.wait_ge(acc_added, g - 1)
                    multiply(banks[q % 2], hot[:, q, :, :], q, group_mm)
                    finished_tiles(pe, g, node_tile, c)
            step(0, True)
            with pe.Fori(1, STEPS) as it:
                step(it, False)
            for a in range(2):
                last = pe.matmul(banks[6 + a][:, :], zb[:, 0:P], zb[:, 0:SC], start=False, stop=True, skip_group_check=True)

            pe.matmul(banks[5][:, 2 * P:2 * P + EX], ones_b[:, :], taken[:, :], start=True, stop=True).then_inc(slots_mm, 1)

            nextra = pe.alloc_register("pe_nextra")
            pe.reg_mov(nextra, 0)

            def transpose_tokens(e, par):
                for k in range(MAIN):
                    pe.wait_ge(gathered[par][k], prior_scatter(e, par) + 16)
                    for c in range(DK):
                        last = pe.transpose(banks[k // 2][:, (k % 2) * D + c * P:(k % 2) * D + (c + 1) * P],
                                            xg[:, par, k, c * P:(c + 1) * P], ident[:, :])
                last.then_inc(tokens_t, 1)

            def first_layer(bank, par, xt, done):
                for j in range(HK):
                    for c in range(DK):
                        last = pe.matmul(bank[:, j * P:(j + 1) * P], w1s[:, par, c, j * P:(j + 1) * P], xt[:, c, :],
                                         start=c == 0, stop=c == DK - 1)
                last.then_inc(done, 1)

            def second_layer(dst, par, h, *done):
                for j in range(HK):
                    last = pe.matmul(dst, h[:, j, :], w2s[:, par, j, :], start=j == 0, stop=j == HK - 1)
                return last

            def expert(e, par, first, final=False):
                nch = pe.value_load(nch_i[0:1, bass.ds(e, 1)], min_val=1, max_val=SLOTCH)
                pe.wait_ge(weights_in[par], expert_loads(e, par))
                pe.wait_ge(tokens_s, e + 1)
                if not first:
                    pe.wait_ge(out_ready, e * MAIN)
                with pe.If(nch > MAIN):
                    with pe.Fori(MAIN, nch) as k:
                        pe.reg_add(nextra, nextra, 1)
                        n = pe.snap(nextra, min_val=1, max_val=EX * SLOTCH)
                        pe.wait_ge(xtra_gathered, n * 16)
                        for c in range(DK):
                            last = pe.transpose(banks[1][:, D + c * P:D + (c + 1) * P], xgx[:, c * P:(c + 1) * P], ident[:, :])
                        last.then_inc(xtra_t, 1)
                        pe.wait_ge(xtra_s, n)
                        first_layer(banks[5], par, xgTx, xtra_l1)
                        pe.wait_ge(xtra_h, n)
                        second_layer(banks[6][:, 0:D], par, h1x).then_inc(xtra_l2, 1)
                        pe.wait_ge(xtra_out, n)
                        pe.transpose(banks[5][:, 0:P], ident[:, :], ident[:, :])
                for k in range(MAIN):
                    if k == 0:
                        first_layer(banks[2 + k], par, xgT[:, k, :, :], l1_done[k])
                    else:
                        with pe.If(nch > k):
                            first_layer(banks[2 + k], par, xgT[:, k, :, :], l1_done[k])
                        with pe.Else():
                            pe.sem_inc(l1_done[k], 1)
                if not final:
                    transpose_tokens(e + 1, 1 - par)
                for k in reversed(range(MAIN)):
                    pe.wait_ge(h1_ready, e * MAIN + (k + 1))
                    if k == 0:
                        pe.wait_ge(out_ready, e * MAIN + 1)
                    elif not first:
                        pe.wait_ge(out_ready, e * MAIN)
                    if k == 0:
                        second_layer(out_bank(k), par, h1[:, k, :, :]).then_inc(l2_done[k], 1)
                    else:
                        with pe.If(nch > k):
                            second_layer(out_bank(k), par, h1[:, k, :, :]).then_inc(l2_done[k], 1)
                        with pe.Else():
                            pe.sem_inc(l2_done[k], 1)
                pe.drain().then_inc(expert_done, 1)

            transpose_tokens(0, 0)
            expert(0, 0, True)
            expert(1, 1, False)
            with pe.Fori(1, EX // 2 - 1) as i:
                expert(i * 2, 0, False)
                expert(i * 2 + 1, 1, False)
            expert(EX - 2, 0, False)
            expert(EX - 1, 1, False, True)

            for g in range(NB):
                pe.wait_ge(combined, g + 1)
                for t in range(TG):
                    tile = g * TG + t
                    last = pe.matmul(banks[0][:, 0:D], (ones_last if tile == NT - 1 else ones)[:, :], acc[:, tile, 0:D],
                                     start=tile == 0, stop=tile == NT - 1)
            last.then_inc(mean_mm, 1)
            for g in range(NB):
                pe.wait_ge(squared, g + 1)
                for t in range(TG):
                    tile = g * TG + t
                    last = pe.matmul(banks[1][:, 0:D], (ones_last if tile == NT - 1 else ones)[:, :], sq[:, g % 2, t, :],
                                     start=tile == 0, stop=tile == NT - 1)
                last.then_inc(sq_used, 1)
            pe.drain().then_inc(var_mm, 1)


_INS = ['x', 'src', 'dst', 'L0_gnn_W_gc', 'L0_gnn_b_gc', 'L0_gnn_W_res', 'L0_gnn_b_res', 'L0_gnn_Wg', 'L0_gnn_bg',
        'L0_gnn_w1', 'L0_gnn_b1', 'L0_gnn_w2', 'L0_gnn_b2', 'L0_gnn_gamma', 'L0_gnn_beta']
_OUTS = [((6250, 256), 'float32')]


def kernel(**inputs):
    import numpy as _np
    import concourse.bacc as _bacc
    from concourse import mybir as _mybir
    from concourse.bass_utils import run_bass_kernel_spmd as _run

    nc = _bacc.Bacc("TRN2", target_bir_lowering=False, num_devices=1)
    arrays, args = {}, []
    for name in _INS:
        a = _np.ascontiguousarray(inputs[name])
        arrays[f"in_{name}_dram"] = a
        args.append(nc.dram_tensor(f"in_{name}_dram", a.shape, _mybir.dt.from_np(a.dtype), kind="ExternalInput").ap())
    for i, (shape, dtype) in enumerate(_OUTS):
        dt = _mybir.dt.from_np(_np.dtype(dtype))
        args.append(nc.dram_tensor(f"out_{i}_dram", shape, dt, kind="ExternalOutput").ap())
    graph_moe_kernel(nc, *args)
    r = _run(nc, [arrays], core_ids=[0])
    return r.results[0]["out_0_dram"]
```

```python
import concourse.bass as bass
from concourse import mybir
from contextlib import ExitStack

F32 = mybir.dt.float32
BF16 = mybir.dt.bfloat16
I32 = mybir.dt.int32
U32 = mybir.dt.uint32
I16 = mybir.dt.int16
ALU = mybir.AluOpType
ACT = mybir.ActivationFunctionType
AX = mybir.AxisListType

P = 128
N, D, EDGES = 6250, 256, 200000
H, EX, TOPK, CAP = 512, 64, 2, 1024
BN_EPS = LN_EPS = 1e-5
NT = -(-N // P)
LAST = N - (NT - 1) * P
NPAD = NT * P
PARTS = 3
ROW = PARTS * D
EB = -(-EDGES // (P * P))
EFULL = EDGES // P
ETAIL = EDGES - EFULL * P
CPG = 8
COLS = EB * P
GCOLS = COLS // CPG
RING = 4
HOTS = 2
STEPS = -(-(-(-EDGES // P)) // (CPG * RING))
GROUPS = STEPS * RING
HB = 8
HSTEPS = -(-(-(-EDGES // P)) // (2 * HB))
SLOTCH = CAP // P
SC = EX * SLOTCH
MAIN = 3
TG = 7
NB = NT // TG
PAD_SRC = NPAD - 1
PAD_DST = 50 * P
UNUSED = 1.0e6
DK, HK = D // P, H // P


def graph_moe_kernel(nc, x, src, dst, W_gc, b_gc, W_res, b_res, Wg, bg, w1, b1, w2, b2, gamma, beta, out):
    ctx = ExitStack()
    with ctx:
        def sb(name, shape, dt=F32):
            return ctx.enter_context(nc.sbuf_tensor(name, shape, dt))

        def sem(name):
            return ctx.enter_context(nc.semaphore(name))

        table = nc.dram_tensor("table", (NPAD, ROW), BF16, kind="Internal").ap()
        nodes = nc.dram_tensor("nodes", (NPAD, D), F32, kind="Internal").ap()
        y2 = nc.dram_tensor("y2", (TOPK * NPAD, D), F32, kind="Internal").ap()

        xs = sb("xs", [P, NT, D])
        acc = sb("acc", [P, NT, D + 1])
        ident = sb("ident", [P, P])
        ones = sb("ones", [P, P])
        ones_last = sb("ones_last", [P, P])
        pcol = sb("pcol", [P, 1])
        iota_f = sb("iota_f", [P, P])
        iota_b = sb("iota_b", [P, P], BF16)
        iota_s = sb("iota_s", [P, SC], I16)
        zeros = sb("zeros", [P, 2 * D])
        wgc = sb("wgc", [P, DK, D])
        wres = sb("wres", [P, DK, D])
        wg = sb("wg", [P, DK, EX])
        bias = sb("bias", [P, D])
        bgb = sb("bgb", [P, EX])
        valid = sb("valid", [P, NT])
        acc_flat = acc[:, :, :].rearrange("p t d -> p (t d)")
        raw_src = acc_flat[:, 0:COLS].bitcast(I32).rearrange("p (b e) -> p b e", e=P)
        raw_dst = acc_flat[:, COLS:2 * COLS].bitcast(I32).rearrange("p (b e) -> p b e", e=P)
        loT = acc_flat[:, 2 * COLS:3 * COLS]
        hiT = acc_flat[:, 3 * COLS:4 * COLS]
        srcT = sb("srcT", [P, COLS])
        dstT = sb("dstT", [P, COLS])
        stage = sb("stage", [P, 4 * TG * D])
        ring_low = sb("ring", [P, RING // 2, CPG, ROW + 2], BF16)
        high0 = RING // 2 * CPG * (ROW + 2) // 2
        ring_high = stage[:, 0:high0].bitcast(BF16).rearrange("p (q j r) -> p q j r", q=RING // 2, j=CPG)
        ring_idx = sb("ring_idx", [P, RING, CPG], I32)
        hot = sb("hot", [P, HOTS, CPG, P], BF16)
        hotx = sb("hotx", [P, CPG, P], BF16)
        dstx = sb("dstx", [P, CPG])
        neg_tile = sb("neg_tile", [P, NT])
        neg_base = sb("neg_base", [P, GCOLS])
        mnmx = sb("mnmx", [P, 2, EB])
        rng_f = sb("rng_f", [EB, 2, P // CPG])
        rng_i = sb("rng_i", [EB, 2, P // CPG], I32)
        rng = sb("rng", [1, 2, GCOLS])
        code = sb("code", [1, GCOLS], I32)
        deg = sb("deg", [P, NT])
        rs = sb("rs", [P, NT])
        tmp = sb("tmp", [P, NT])
        mS = sb("mS", [P, D])
        xS = sb("xS", [P, D])
        tS = sb("tS", [P, 4, P])
        yS = sb("yS", [P, D])
        ytS = sb("ytS", [P, DK, P])
        lg = sb("lg", [P, EX])
        v8 = sb("v8", [P, 8])
        i8 = sb("i8", [P, 8], U32)
        i8f = sb("i8f", [P, TOPK])
        pick = sb("pick", [P, TOPK, EX], BF16)
        picked = sb("picked", [P, EX], BF16)
        taken = sb("taken", [P, EX], BF16)
        tri = sb("tri", [P, P], BF16)
        ones_b = sb("ones_b", [P, P], BF16)
        junk = sb("junk", [P, TOPK, EX], BF16)
        rk = sb("rk", [P, TOPK])
        rki = sb("rki", [P, 3, TOPK], I32)
        rkf = sb("rkf", [P, 2, TOPK])
        qs = sb("qs", [P, TOPK])
        inval = sb("inval", [P, NT])
        hnum = sb("hnum", [P, TOPK, NT])
        sel = sb("sel", [P, TOPK, SC], BF16)
        lo1 = sb("lo1", [P, TOPK, 2, P], BF16)
        top = sb("top", [P, NT, TOPK])
        rank = sb("rank", [P, NT, TOPK])
        gate = sb("gate", [P, NT, TOPK])
        tok_f = stage[:, 0:SC]
        tok_t = stage[:, SC:2 * SC]
        gidx = sb("gidx", [P, SC], I32)
        sidx = sb("sidx", [P, SC], I32)
        nch_f = sb("nch_f", [1, EX])
        nch_i = sb("nch_i", [1, EX], I32)
        b1r = sel[0:EX, :, :].rearrange("p k s -> p (k s)").bitcast(F32)
        b1T = sb("b1T", [P, HK, EX])
        b1e = sb("b1e", [P, HK])
        w1s = stage[:, 0:2 * DK * H].rearrange("p (b k h) -> p b k h", b=2, k=DK)
        w2s = stage[:, 2 * DK * H:4 * DK * H].rearrange("p (b j d) -> p b j d", b=2, j=HK)
        b2s = stage[:, 4 * DK * H:4 * DK * H + 2 * D].rearrange("p (b d) -> p b d", b=2)
        ybuf = stage[:, :].rearrange("p (b k t d) -> p b k t d", b=2, k=TOPK, t=TG)
        sq = stage[:, 0:2 * TG * D].rearrange("p (b t d) -> p b t d", b=2, t=TG)
        arena = ring_low[:, :, :, :].rearrange("p a b c -> p (a b c)").bitcast(F32)
        taken_to = [0]

        def piece(n):
            taken_to[0] += n
            return arena[:, taken_to[0] - n:taken_to[0]]

        xg = piece(2 * MAIN * D).rearrange("p (b k d) -> p b k d", b=2, k=MAIN)
        xgT = piece(MAIN * D).rearrange("p (k c r) -> p k c r", k=MAIN, c=DK)
        h1 = piece(MAIN * H).rearrange("p (k j r) -> p k j r", k=MAIN, j=HK)
        outs = piece(2 * MAIN * D).rearrange("p (b k d) -> p b k d", b=2, k=MAIN)
        xgx = piece(D)
        xgTx = piece(D).rearrange("p (c r) -> p c r", c=DK)
        late = hot[:, :, :, :].rearrange("p a b c -> p (a b c)").bitcast(F32)
        gb = late[:, 0:2 * D].rearrange("p (a d) -> p a d", a=2)
        h1x = late[:, 2 * D:2 * D + H].rearrange("p (j r) -> p j r", j=HK)
        outx = mS
        mean, var, vroot, scale = xS, yS, tS[:, 0:DK, :].rearrange("p c r -> p (c r)"), tS[:, DK:2 * DK, :].rearrange("p c r -> p (c r)")
        slot_idx = sb("slot_idx", [P, 2, 2, MAIN], I32)
        xtra_idx = sb("xtra_idx", [P, 2], I32)
        stats = srcT[:, 0:TG * 6].rearrange("p (t s) -> p t s", s=6)
        mv = srcT[:, TG * 6:TG * 6 + 2 * NT].rearrange("p (t s) -> p t s", s=2)

        banks = [ctx.enter_context(nc.psum_tensor(f"bank{i}", [P, 512], F32)) for i in range(8)]

        lo_hot = stage[:, 0:HB * P].bitcast(BF16).rearrange("p (b c n) -> p b c n", b=2, c=HB)
        hi_hot = stage[:, HB * P:HB * P + HB * NT].bitcast(BF16).rearrange("p (b c t) -> p b c t", b=2, c=HB)
        s0 = 2 * TG * ROW // 2
        SFX = 656
        sfx = stage[0:1, s0:s0 + 2 * SFX].rearrange("o (a g) -> o a g", a=2)
        code_f = stage[0:1, s0 + 2 * SFX:s0 + 2 * SFX + GCOLS]
        sfx_one = code[:, :].bitcast(F32)
        parts = stage[:, 0:2 * TG * ROW // 2].bitcast(BF16).rearrange("p (b t r) -> p b t r", b=2, t=TG)

        ini = sem("ini")
        const_p = sem("const_p")
        const_d = sem("const_d")
        src_loaded, dst_loaded, x_loaded, w_loaded = sem("src_loaded"), sem("dst_loaded"), sem("x_loaded"), sem("w_loaded")
        srch_f, dst_f = sem("srch_f"), sem("dst_f")
        tr_done, tr_copied = sem("tr_done"), sem("tr_copied")
        hi_diff, lo_ready, hi_ready, hist_mm = sem("hi_diff"), sem("lo_ready"), sem("hi_ready"), sem("hist_mm")
        mm_tr, mm_red, mm_row, nb_done, base_ready = sem("mm_tr"), sem("mm_red"), sem("mm_row"), sem("nb_done"), sem("base_ready")
        deg_ready, deg_sqrt, rs_ready = sem("deg_ready"), sem("deg_sqrt"), sem("rs_ready")
        h_ready, hi_part, r1_ready, mid_part, lo_part, table_out = (sem("h_ready"), sem("hi_part"), sem("r1_ready"),
                                                                     sem("mid_part"), sem("lo_part"), sem("table_out"))
        table_buf = [sem("table_buf0"), sem("table_buf1")]
        acc_zero = sem("acc_zero")
        code_ready = sem("code_ready")
        idx_ready = sem("idx_ready")
        gath = [sem(f"gath{q}") for q in range(RING)]
        hot_ready, group_mm, acc_added = sem("hot_ready"), sem("group_mm"), sem("acc_added")
        lo_rep, hot_rep, high_ones = sem("lo_rep"), sem("hot_rep"), sem("high_ones")
        hotx_ready, groupx_mm = sem("hotx_ready"), sem("groupx_mm")
        nd_deg, nd_sqrt, nd_in, nd_tr, nd_t = sem("nd_deg"), sem("nd_sqrt"), sem("nd_in"), sem("nd_tr"), sem("nd_t")
        nd_proj, nd_y, nd_yst, nd_ytr, nd_yt, nd_logit = (sem("nd_proj"), sem("nd_y"), sem("nd_yst"), sem("nd_ytr"),
                                                          sem("nd_yt"), sem("nd_logit"))
        nd_pick, nd_rank, nd_sel, nd_slot = sem("nd_pick"), sem("nd_rank"), sem("nd_sel"), sem("nd_slot")
        y2_zeroed = sem("y2_zeroed")
        nd_stored = sem("nd_stored")
        slots_mm = sem("slots_mm")
        tables_done, gb_in, gap_ready, exp_ready = sem("tables_done"), sem("gb_in"), sem("gap_ready"), sem("exp_ready")
        b1_t = sem("b1_t")
        w1_in, w2_in, b2_in = ([sem(f"{w}_in{par}") for par in range(2)] for w in ("w1", "w2", "b2"))
        gathered = [[sem(f"gathered{par}{k}") for k in range(MAIN)] for par in range(2)]
        scattered = [[sem(f"scattered{par}{k}") for k in range(MAIN)] for par in range(2)]
        row_copied = sem("row_copied")
        slot_copied, tokens_t, tokens_s = sem("slot_copied"), sem("tokens_t"), sem("tokens_s")
        l1_done = [sem(f"l1_done{k}") for k in range(MAIN)]
        l2_done = [sem(f"l2_done{k}") for k in range(MAIN)]
        h1_ready, out_ready, expert_done = sem("h1_ready"), sem("out_ready"), sem("expert_done")
        xtra_copied, xtra_gathered, xtra_t, xtra_s = sem("xtra_copied"), sem("xtra_gathered"), sem("xtra_t"), sem("xtra_s")
        xtra_l1, xtra_h, xtra_l2, xtra_out, xtra_scattered = (sem("xtra_l1"), sem("xtra_h"), sem("xtra_l2"), sem("xtra_out"),
                                                              sem("xtra_scattered"))
        xtra_all, pool_starts = sem("xtra_all"), sem("pool_starts")
        y2_in = [sem("y2_in0"), sem("y2_in1")]
        combined, mean_mm, centered, squared, sq_used, var_mm = (sem("combined"), sem("mean_mm"), sem("centered"),
                                                                 sem("squared"), sem("sq_used"), sem("var_mm"))
        var_ready, var_sqrt, lnvar_ready, lnvar_sqrt = sem("var_ready"), sem("var_sqrt"), sem("lnvar_ready"), sem("lnvar_sqrt")
        xbeta, normed, stored = sem("xbeta"), sem("normed"), sem("stored")

        def nth(e, par):
            return e // 2 if isinstance(e, int) else (e - par) // 2

        def landed(e, par):
            return nth(e, par) * 16 + 16

        def prior_scatter(e, par):
            return nth(e, par) * 16

        def out_bank(k):
            return banks[6 + k % 2][:, 0:D]

        def ring(q):
            return ring_low[:, q, :, :] if q < RING // 2 else ring_high[:, q - RING // 2, :, :]

        block = ctx.enter_context(nc.Block())

        T_BANKS = (4, 5, 6, 7)
        NTR = -(-EB // 4)
        LISTS = 3

        def group_code(eng, g):
            return eng.value_load(code[0:1, bass.ds(g, 1)], min_val=0, max_val=(1 << 24) - 1)

        def field(eng, c, k):
            return nc.s_assert_within(eng.snap((c >> (6 * k)) & 63), 0, NT if k > 1 else NT - 1,
                                      skip_runtime_bounds_check_because="the tables hold tiles below NT")

        def a_tile(t):
            return nc.s_assert_within(t, 0, NT - 1, skip_runtime_bounds_check_because="the codes hold tiles below NT")

        DEPTH = 3

        def ticks_of_group(eng, c, tick):
            before = field(eng, c, 2)
            now = field(eng, c, 3)
            with eng.If(now > before):
                i = a_tile(before)

                def behind(k, stage):
                    with eng.If(i > k - 1):
                        stage(nc.s_assert_within(i - k, 0, NT - 1 - k,
                                                 skip_runtime_bounds_check_because="the branch holds it above zero"))
                tick(i, behind)

        def last_ticks(eng, tick):
            i = field(eng, group_code(eng, GROUPS - 1), 3)
            with eng.If(i < NT):
                with eng.Fori(i, NT) as t:
                    t = a_tile(t)

                    def behind(k, stage):
                        with eng.If(t > k - 1):
                            stage(nc.s_assert_within(t - k, 0, NT - 1 - k,
                                                     skip_runtime_bounds_check_because="the branch holds it above zero"))
                    tick(t, behind)
            for t in range(NT, NT + DEPTH):
                def behind(k, stage):
                    if t - k < NT:
                        stage(t - k)
                tick(None, behind)

        def inv_sqrt(dve, r, s, d):
            dve.reciprocal(r, s)
            dve.drain()
            dve.tensor_tensor(s, r, r, ALU.mult)
            dve.drain()
            dve.tensor_tensor(s, s, d, ALU.mult)
            dve.drain()
            dve.tensor_scalar(s, s, -0.5, 1.5, ALU.mult, ALU.add)
            dve.drain()
            dve.tensor_tensor(r, r, s, ALU.mult)

        @block.sync
        def _(sp):
            sp.wait_ge(ini, 1)
            for raw, edges, loaded in ((raw_src, src, src_loaded), (raw_dst, dst, dst_loaded)):
                nb = EB - 1
                sp.dma_start(raw[:, 0:nb, :], edges[0:nb * P * P].rearrange("(b r e) -> r b e", r=P, e=P)).then_inc(loaded, 16)
                r = EFULL - nb * P
                sp.dma_start(raw[0:r, nb, :], edges[nb * P * P:EFULL * P].rearrange("(r e) -> r e", e=P)).then_inc(loaded, 16)
                sp.dma_start(raw[r:r + 1, nb, 0:ETAIL], edges[EFULL * P:EDGES].rearrange("(r e) -> r e", r=1)).then_inc(loaded, 16)
            sp.dma_start(xs[:, 0:NT - 1, :], x[0:(NT - 1) * P, :].rearrange("(t p) d -> p t d", p=P)).then_inc(x_loaded, 16)
            sp.dma_start(xs[0:LAST, NT - 1, :], x[(NT - 1) * P:N, :]).then_inc(x_loaded, 16)
            sp.dma_start(wgc[:, :, :], W_gc.rearrange("(k p) n -> p k n", p=P)).then_inc(w_loaded, 16)
            sp.dma_start(wres[:, :, :], W_res.rearrange("(k p) n -> p k n", p=P)).then_inc(w_loaded, 16)
            sp.dma_start(wg[:, :, :], Wg.rearrange("(k p) n -> p k n", p=P)).then_inc(w_loaded, 16)
            sp.dma_start(bias[:, :], b_gc.partition_broadcast(P)).then_inc(w_loaded, 16)
            sp.dma_start(yS[:, :], b_res.partition_broadcast(P)).then_inc(w_loaded, 16)
            sp.dma_start(bgb[:, :], bg.partition_broadcast(P)).then_inc(w_loaded, 16)
            sp.dma_start(b1r[:, :], b1).then_inc(w_loaded, 16)
            y2v = y2.rearrange("(p r) d -> p (r d)", p=P)
            with sp.Fori(0, TOPK * NPAD // P // 2) as i:
                sp.dma_start(y2v[:, bass.ds(i * (2 * D), 2 * D)], zeros[:, :]).then_inc(y2_zeroed, 16)
            sp.wait_ge(mm_red, 1)
            sp.dma_start(rng[0:1, 0, :], rng_f[:, 0, :]).then_inc(mm_row, 16)
            sp.dma_start(rng[0:1, 1, :], rng_f[:, 1, :]).then_inc(mm_row, 16)
            for g in range(NB):
                sp.wait_ge(lo_part, g + 1)
                tv = table[g * TG * P:(g + 1) * TG * P, :].rearrange("(t p) r -> p t r", p=P)
                sp.dma_start(tv, parts[:, g % 2, :, :]).then_inc(table_buf[g % 2], 16)
            def weights(e, par, first):
                if not first:
                    for k in range(MAIN):
                        sp.wait_ge(l1_done[k], e - 1)
                sp.dma_start(w1s[:, par, :, :], w1[bass.ds(e, 1), :, :].rearrange("o (k p) h -> p (o k) h", p=P)).then_inc(w1_in[par], 16)
                if not first:
                    sp.wait_ge(expert_done, e - 1)
                    sp.wait_ge(out_ready, MAIN * e - MAIN)
                sp.dma_start(w2s[:, par, :, :], w2[bass.ds(e, 1), :, :].rearrange("o (j p) d -> p (o j) d", p=P)).then_inc(w2_in[par], 16)
                sp.dma_start(b2s[:, par, :], b2[bass.ds(e, 1), :].rearrange("o d -> (o d)").partition_broadcast(P)).then_inc(b2_in[par], 16)
            sp.wait_ge(tables_done, 1)
            sp.dma_start(gb[:, 0, :], gamma.partition_broadcast(P)).then_inc(gb_in, 16)
            sp.dma_start(gb[:, 1, :], beta.partition_broadcast(P)).then_inc(gb_in, 16)
            weights(0, 0, True)
            weights(1, 1, True)
            with sp.Fori(1, EX // 2) as i:
                weights(i * 2, 0, False)
                weights(i * 2 + 1, 1, False)

            for par in range(2):
                for k in range(MAIN):
                    sp.wait_ge(scattered[par][k], 16 * EX // 2)
            sp.wait_ge(xtra_all, 1)
            sp.wait_ge(expert_done, EX)
            sp.wait_ge(out_ready, MAIN * EX)
            y2t = y2.rearrange("(k t p) d -> p k t d", k=TOPK, p=P)
            for g in range(NB):
                if g >= 2:
                    sp.wait_ge(combined, g - 1)
                for k in range(TOPK):
                    sp.dma_start(ybuf[:, g % 2, k, :, :], y2t[:, k, g * TG:(g + 1) * TG, :]).then_inc(y2_in[g % 2], 16)
            for g in range(NB):
                sp.wait_ge(normed, g + 1)
                full = TG if g < NB - 1 else TG - 1
                r = g * TG * P
                sp.dma_start(out[r:r + full * P, :].rearrange("(t p) d -> p t d", p=P), acc[:, g * TG:g * TG + full, 0:D]).then_inc(stored, 16)
            sp.dma_start(out[(NT - 1) * P:N, :], acc[0:LAST, NT - 1, 0:D]).then_inc(stored, 16)
            sp.wait_ge(stored, 16 * (NB + 1))

        @block.gpsimd
        def _(pool):
            pool.iota(iota_f[:, :], pattern=[[1, P]], base=0, channel_multiplier=0,
                      allow_small_or_imprecise_dtypes=True).then_inc(const_p, 1)
            pool.iota(iota_b[:, :], pattern=[[1, P]], base=0, channel_multiplier=0,
                      allow_small_or_imprecise_dtypes=True).then_inc(const_p, 1)
            pool.iota(pcol[:, :], pattern=[[0, 1]], base=0, channel_multiplier=1,
                      allow_small_or_imprecise_dtypes=True).then_inc(const_p, 1)
            pool.iota(iota_s[:, :], pattern=[[1, SC]], base=0, channel_multiplier=0,
                      allow_small_or_imprecise_dtypes=True).then_inc(const_p, 1)
            pool.iota(neg_tile[:, :], pattern=[[-P, NT]], base=0, channel_multiplier=0,
                      allow_small_or_imprecise_dtypes=True).then_inc(const_p, 1)
            pool.iota(hnum[:, :, :], pattern=[[NT, TOPK], [1, NT]], base=1, channel_multiplier=0,
                      allow_small_or_imprecise_dtypes=True).then_inc(const_p, 1)
            pool.memset(ring_low[:, :, :, ROW:ROW + 2], 1.0).then_inc(const_p, 1)

            pool.wait_ge(tr_copied, 2 * NTR)
            pool.wait_ge(const_p, 7)

            def hist(i, first):
                for q in range(2):
                    if not first:
                        pool.wait_ge(hist_mm, i * 2 + (q - 1))
                    pool.tensor_tensor(hi_hot[:, q, :, :],
                                       iota_f[:, 0:NT].unsqueeze(1).to_broadcast([P, HB, NT]),
                                       hiT[:, bass.ds((i * 2 + q) * HB, HB)].unsqueeze(2).to_broadcast([P, HB, NT]),
                                       ALU.subtract).then_inc(hi_diff, 1)
            hist(0, True)
            with pool.Fori(1, HSTEPS) as i:
                hist(i, False)

            pool.wait_ge(rs_ready, 1)
            pool.wait_ge(x_loaded, 32)
            for g in range(NB):
                pool.tensor_tensor(acc[:, g * TG:(g + 1) * TG, 0:D], xs[:, g * TG:(g + 1) * TG, :],
                                   rs[:, g * TG:(g + 1) * TG].unsqueeze(2).to_broadcast([P, TG, D]),
                                   ALU.mult).then_inc(h_ready, 1)

            node_reg, row_reg = pool.alloc_register("last_node"), pool.alloc_register("last_row")
            pool.reg_mov(node_reg, N - 1)
            pool.reg_mov(row_reg, TOPK * NPAD - 1)
            last_node, last_row = node_reg, row_reg

            def start():
                pool.sem_inc(pool_starts, 1)

            for q in range(2):
                pool.wait_ge(table_buf[q], 16 * ((NB + 1 - q) // 2))

            def gather(it, first):
                for q in range(RING):
                    if first and q == RING // 2:
                        pool.wait_ge(code_ready, 1)
                        pool.memset(ring_high[:, :, :, ROW:ROW + 2], 1.0).then_inc(high_ones, 1)
                    pool.wait_ge(idx_ready, it * RING + (q + 1))
                    if not first:
                        pool.wait_ge(group_mm, it * RING + (q - RING + 1))
                    start()
                    for j in range(CPG):
                        pool.indirect_dma_start(
                            out=ring(q)[:, j, 0:ROW], out_offset=None, in_=table[:, :],
                            in_offset=bass.IndirectOffsetOnAxis(ap=ring_idx[:, q, j:j + 1], axis=0),
                            bounds_check=last_node, oob_is_err=False).then_inc(gath[q], 16)
            gather(0, True)
            with pool.Fori(1, STEPS) as it:
                gather(it, False)

            pool.wait_ge(y2_zeroed, 16 * (TOPK * NPAD // P // 2))
            pool.wait_ge(tables_done, 1)
            pool.wait_ge(gb_in, 32)
            pool.wait_ge(nd_stored, 16 * NT + 16)

            def load_slots(e, par, first):
                if not first:
                    pool.wait_ge(tokens_t, e - 1)
                    start()
                pool.tensor_copy(slot_idx[:, par, 0, :], gidx[:, bass.ds(e * SLOTCH, MAIN)]).then_inc(slot_copied, 1)
                pool.wait_ge(slot_copied, e + 1)
                start()
                for k in range(MAIN):
                    pool.indirect_dma_start(
                        out=xg[:, par, k, :], out_offset=None, in_=nodes[:, :],
                        in_offset=bass.IndirectOffsetOnAxis(ap=slot_idx[:, par, 0, k:k + 1], axis=0),
                        bounds_check=last_node, oob_is_err=False).then_inc(gathered[par][k], 16)

            def store_slots(e, par, first):
                if not first:
                    for k in range(MAIN):
                        pool.wait_ge(scattered[par][k], prior_scatter(e, par))
                    start()
                pool.tensor_copy(slot_idx[:, par, 1, :], sidx[:, bass.ds(e * SLOTCH, MAIN)]).then_inc(row_copied, 1)
                pool.wait_ge(row_copied, e + 1)
                start()
                for k in range(MAIN):
                    pool.wait_ge(out_ready, e * MAIN + (k + 1))
                    start()
                    pool.indirect_dma_start(
                        out=y2[:, :], out_offset=bass.IndirectOffsetOnAxis(ap=slot_idx[:, par, 1, k:k + 1], axis=0),
                        in_=outs[:, par, k, :], in_offset=None,
                        bounds_check=last_row, oob_is_err=False).then_inc(scattered[par][k], 16)

            nextra = pool.alloc_register("pool_nextra")
            pool.reg_mov(nextra, 0)

            def extra_chunks(e, nch):
                with pool.If(nch > MAIN):
                    with pool.Fori(MAIN, nch) as k:
                        col = nc.s_assert_within(e * SLOTCH + k, 0, SC - 1,
                                                 skip_runtime_bounds_check_because="no expert has more than SLOTCH chunks")
                        pool.reg_add(nextra, nextra, 1)
                        n = pool.snap(nextra, min_val=1, max_val=EX * SLOTCH)
                        pool.tensor_copy(xtra_idx[:, 0:1], gidx[:, bass.ds(col, 1)])
                        pool.tensor_copy(xtra_idx[:, 1:2], sidx[:, bass.ds(col, 1)]).then_inc(xtra_copied, 1)
                        pool.wait_ge(xtra_copied, n)
                        start()
                        pool.indirect_dma_start(
                            out=xgx[:, :], out_offset=None, in_=nodes[:, :],
                            in_offset=bass.IndirectOffsetOnAxis(ap=xtra_idx[:, 0:1], axis=0),
                            bounds_check=last_node, oob_is_err=False).then_inc(xtra_gathered, 16)
                        pool.wait_ge(xtra_out, n)
                        start()
                        pool.indirect_dma_start(
                            out=y2[:, :], out_offset=bass.IndirectOffsetOnAxis(ap=xtra_idx[:, 1:2], axis=0),
                            in_=outx[:, :], in_offset=None,
                            bounds_check=last_row, oob_is_err=False).then_inc(xtra_scattered, 16)
                        pool.wait_ge(xtra_scattered, n * 16)
                        start()

            def chunks_of(e):
                return pool.value_load(nch_i[0:1, bass.ds(e, 1)], min_val=1, max_val=SLOTCH)

            def expert(e, par, first, ahead=True):
                extra_chunks(e, chunks_of(e))
                if ahead:
                    load_slots(e + 2, par, False)
                store_slots(e, par, first)

            load_slots(0, 0, True)
            load_slots(1, 1, True)
            expert(0, 0, True)
            expert(1, 1, True)
            with pool.Fori(1, EX // 2 - 1) as i:
                expert(i * 2, 0, False)
                expert(i * 2 + 1, 1, False)
            expert(EX - 2, 0, False, False)
            expert(EX - 1, 1, False, False)
            pool.drain().then_inc(xtra_all, 1)
            for t in range(NB):
                pool.tensor_tensor(xs[:, t * TG:(t + 1) * TG, :], xs[:, t * TG:(t + 1) * TG, :],
                                   gb[:, 1, :].unsqueeze(1).to_broadcast([P, TG, D]), ALU.add).then_inc(xbeta, TG)

        @block.scalar
        def _(act):
            n = 0
            for which in range(LISTS):
                target = (loT, hiT, dstT)[which]
                for c in range(NTR):
                    w = min(4, EB - 4 * c) * P
                    act.wait_ge(tr_done, n + 1)
                    act.activation(target[:, c * 512:c * 512 + w], banks[T_BANKS[n % 4]][:, 0:w], ACT.Copy).then_inc(tr_copied, 1)
                    n += 1

            def hist(i, first):
                for q in range(2):
                    if not first:
                        act.wait_ge(hist_mm, i * 2 + (q - 1))
                    act.activation(lo_hot[:, q, :, :],
                                   loT[:, bass.ds((i * 2 + q) * HB, HB)].unsqueeze(2).to_broadcast([P, HB, P]),
                                   ACT.Copy).then_inc(lo_rep, 1)
            act.wait_ge(srch_f, 2)
            hist(0, True)
            with act.Fori(1, HSTEPS) as i:
                hist(i, False)
            act.wait_ge(deg_ready, 1)
            act.activation(tmp[:, :], deg[:, :], ACT.Sqrt).then_inc(deg_sqrt, 1)
            for g in range(NB):
                hv = acc[:, g * TG:(g + 1) * TG, 0:D]
                if g >= 2:
                    act.wait_ge(table_buf[g % 2], 16 * (g // 2))
                act.wait_ge(h_ready, g + 1)
                act.activation(parts[:, g % 2, :, 2 * D:3 * D], hv, ACT.Copy).then_inc(hi_part, 1)
                act.wait_ge(r1_ready, g + 1)
                act.activation(parts[:, g % 2, :, D:2 * D], hv, ACT.Copy).then_inc(mid_part, 1)

            act.sem_inc(nd_stored, 16)
            act.sem_inc(nd_yst, 1)
            act.wait_ge(b1_t, 1)
            act.activation(b1T[:, :, :], banks[3][:, 0:HK * EX], ACT.Copy)
            act.drain()
            act.wait_ge(code_ready, 1)

            def indices(it, q, first):
                if not first:
                    act.wait_ge(gath[q], it * (16 * CPG))
                act.activation(ring_idx[:, q, :], srcT[:, bass.ds((it * RING + q) * CPG, CPG)], ACT.Copy).then_inc(idx_ready, 1)

            def repeat_dst(it, q, first):
                g = it * RING + q
                if not (first and q < HOTS):
                    act.wait_ge(group_mm, it * RING + (q - HOTS + 1))
                act.activation(hot[:, q % HOTS, :, :], dstT[:, bass.ds(g * CPG, CPG)].unsqueeze(2).to_broadcast([P, CPG, P]),
                               ACT.Identity, bias=neg_base[:, bass.ds(g, 1)]).then_inc(hot_rep, 1)

            def tick(i, behind):
                if i is not None:
                    act.wait_ge(nd_deg, i + 1)
                    act.activation(mS[:, :], acc[:, bass.ds(i, 1), 0:D], ACT.Copy)
                    act.activation(xS[:, :], xs[:, bass.ds(i, 1), :], ACT.Copy).then_inc(nd_in, 1)
                    act.activation(tmp[:, bass.ds(i, 1)], deg[:, bass.ds(i, 1)], ACT.Sqrt).then_inc(nd_sqrt, 1)

                def transposed_y(t):
                    act.wait_ge(nd_ytr, t + 1)
                    act.activation(ytS[:, :, :], banks[5][:, 0:D], ACT.Copy).then_inc(nd_yt, 1)
                behind(1, transposed_y)
                if i is not None:
                    act.wait_ge(nd_tr, i + 1)
                    act.activation(tS[:, :, :], banks[3][:, :], ACT.Copy).then_inc(nd_t, 1)

                def keep_y(t):
                    act.wait_ge(nd_y, t + 1)
                    act.dma_start(nodes[bass.ds(t * P, P), :], yS[:, :]).then_inc(nd_stored, 16)
                    act.activation(acc[:, bass.ds(t, 1), 0:D], yS[:, :], ACT.Copy).then_inc(nd_yst, 1)
                behind(1, keep_y)

            LEAD = RING
            for q in range(LEAD):
                indices(0, q, True)
            act.wait_ge(base_ready, 1)
            repeat_dst(0, 0, True)

            def step(it, first):
                for q in range(RING):
                    repeat_dst(it + (q + 1) // RING, (q + 1) % RING, first and q + 1 < RING)
                    ahead = q + LEAD
                    indices(it + ahead // RING, ahead % RING, first and ahead < RING)
                    ticks_of_group(act, group_code(act, it * RING + q), tick)
            step(0, True)
            with act.Fori(1, STEPS - 1) as it:
                step(it, False)
            it = STEPS - 1
            for q in range(RING):
                if q + 1 < RING:
                    repeat_dst(it, q + 1, False)
                ticks_of_group(act, group_code(act, it * RING + q), tick)
            last_ticks(act, tick)

            act.wait_ge(gap_ready, 1)
            act.activation(gate[:, :, 1], gate[:, :, 1], ACT.Exp).then_inc(exp_ready, 1)
            nextra = act.alloc_register("act_nextra")
            act.reg_mov(nextra, 0)

            def expert(e, first):
                act.drain()
                act.activation(b1e[:, :], b1T[:, :, bass.ds(e, 1)], ACT.Copy)
                act.drain()
                nch = act.value_load(nch_i[0:1, bass.ds(e, 1)], min_val=1, max_val=SLOTCH)
                with act.If(nch > MAIN):
                    with act.Fori(MAIN, nch) as k:
                        act.reg_add(nextra, nextra, 1)
                        n = act.snap(nextra, min_val=1, max_val=EX * SLOTCH)
                        act.wait_ge(xtra_l1, n)
                        for j in range(HK):
                            last = act.activation(h1x[:, j, :], banks[5][:, j * P:(j + 1) * P], ACT.Gelu,
                                                  bias=b1e[:, j:j + 1])
                        last.then_inc(xtra_h, 1)
                for k in range(MAIN):
                    act.wait_ge(l1_done[k], e + 1)
                    if not first:
                        act.wait_ge(l2_done[k], e)
                    for j in range(HK):
                        last = act.activation(h1[:, k, j, :], banks[2 + k][:, j * P:(j + 1) * P], ACT.Gelu,
                                              bias=b1e[:, j:j + 1])
                    last.then_inc(h1_ready, 1)
            expert(0, True)
            with act.Fori(1, EX) as e:
                expert(e, False)
            for g in range(NB):
                act.wait_ge(centered, g + 1)
                if g >= 2:
                    act.wait_ge(sq_used, g - 1)
                act.activation(sq[:, g % 2, :, :], acc[:, g * TG:(g + 1) * TG, 0:D], ACT.Square).then_inc(squared, 1)
            act.wait_ge(var_ready, 1)
            act.activation(vroot[:, :], var[:, :], ACT.Sqrt).then_inc(var_sqrt, 1)
            act.wait_ge(lnvar_ready, 1)
            act.activation(tmp[:, :], deg[:, :], ACT.Sqrt).then_inc(lnvar_sqrt, 1)

        @block.vector
        def _(dve):
            dve.memset(raw_src[:, EB - 1, :], PAD_SRC)
            dve.memset(raw_dst[:, EB - 1, :], PAD_DST)
            dve.memset(xs[:, NT - 1, :], 0.0)
            dve.memset(zeros[:, :], 0.0)
            dve.drain().then_inc(ini, 1)
            dve.memset(ones[:, :], 1.0)
            dve.memset(ones_b[:, :], 1.0)
            dve.memset(taken[:, :], 0.0)
            dve.memset(valid[:, :], 1.0)
            dve.wait_ge(const_p, 6)
            dve.tensor_scalar(ident[:, :], iota_f[:, :], pcol[:, 0:1], None, ALU.is_equal)
            dve.tensor_scalar(tri[:, :], iota_f[:, :], pcol[:, 0:1], None, ALU.is_gt)
            dve.drain()
            dve.tensor_scalar(valid[:, NT - 1:NT], pcol[:, :], float(LAST), None, ALU.is_lt)
            dve.drain()
            dve.tensor_scalar(inval[:, :], valid[:, :], -8192.0, 8192.0, ALU.mult, ALU.add)
            dve.tensor_scalar(ones_last[:, :], ones[:, :], valid[:, NT - 1:NT], None, ALU.mult)
            dve.drain().then_inc(const_d, 1)
            dve.wait_ge(src_loaded, 48)
            s_lo, s_hi = stage[:, 0:COLS].bitcast(I32), stage[:, COLS:2 * COLS].bitcast(I32)
            flat = raw_src[:, :, :].rearrange("p b e -> p (b e)")
            dve.tensor_scalar(s_lo, flat, P - 1, None, ALU.bitwise_and)
            dve.drain()
            dve.tensor_copy(stage[:, 2 * COLS:3 * COLS], s_lo).then_inc(srch_f, 1)
            dve.tensor_scalar(s_hi, flat, 7, None, ALU.arith_shift_right)
            dve.drain()
            dve.tensor_copy(stage[:, 3 * COLS:4 * COLS], s_hi).then_inc(srch_f, 1)
            dve.wait_ge(dst_loaded, 48)
            dstf = srcT[:, :]
            dve.tensor_copy(dstf, raw_dst[:, :, :].rearrange("p b e -> p (b e)")).then_inc(dst_f, 1)
            dve.drain()
            dv = dstf.rearrange("p (b e) -> p b e", e=P)
            dve.tensor_reduce(mnmx[:, 0, :], dv, op=ALU.min, axis=AX.X)
            dve.tensor_reduce(mnmx[:, 1, :], dv, op=ALU.max, axis=AX.X).then_inc(dst_f, 1)

            dve.wait_ge(tr_copied, 2 * NTR)

            def hist(i, first):
                for q in range(2):
                    dve.wait_ge(lo_rep, i * 2 + (q + 1))
                    dve.tensor_tensor(lo_hot[:, q, :, :], iota_b[:, :].unsqueeze(1).to_broadcast([P, HB, P]),
                                      lo_hot[:, q, :, :], ALU.is_equal).then_inc(lo_ready, 1)
                    dve.wait_ge(hi_diff, i * 2 + (q + 1))
                    dve.tensor_scalar(hi_hot[:, q, :, :], hi_hot[:, q, :, :], 0.0, None, ALU.is_equal).then_inc(hi_ready, 1)
            hist(0, True)
            with dve.Fori(1, HSTEPS) as i:
                hist(i, False)
            dve.wait_ge(tr_copied, LISTS * NTR)
            dve.scalar_tensor_tensor(srcT[:, :], hiT[:, :], float(P), loT[:, :], ALU.mult, ALU.add)
            dve.wait_ge(hist_mm, 2 * HSTEPS)
            dve.tensor_scalar(deg[:, :], banks[0][:, 0:NT], 1.0, None, ALU.max).then_inc(deg_ready, 1)
            dve.wait_ge(deg_sqrt, 1)
            inv_sqrt(dve, rs[:, :], tmp[:, :], deg[:, :])
            dve.drain().then_inc(rs_ready, 1)

            dve.wait_ge(mm_tr, 1)
            groups = P // CPG
            mt = banks[1][0:EB, 0:2 * P].rearrange("p (a g c) -> p a g c", a=2, c=CPG)
            dve.tensor_reduce(rng_f[:, 0, :], mt[:, 0, :, :], op=ALU.min, axis=AX.X)
            dve.tensor_reduce(rng_f[:, 1, :], mt[:, 1, :, :], op=ALU.max, axis=AX.X)
            dve.drain()
            dve.tensor_copy(rng_i[:, :, :], rng_f[:, :, :])
            dve.drain()
            dve.tensor_scalar(rng_i[:, :, :], rng_i[:, :, :], 7, None, ALU.arith_shift_right)
            dve.drain()
            dve.tensor_scalar(rng_f[:, :, :], rng_i[:, :, :], float(NT - 1), None, ALU.min).then_inc(mm_red, 1)
            dve.memset(sfx[:, :, :], float(NT))
            dve.memset(sfx_one[:, :], 1.0)
            for g in range(NB):
                hv = acc[:, g * TG:(g + 1) * TG, 0:D]
                pv = parts[:, g % 2, :, :]
                dve.wait_ge(hi_part, g + 1)
                dve.tensor_tensor(hv, hv, pv[:, :, 2 * D:3 * D], ALU.subtract).then_inc(r1_ready, 1)
                dve.wait_ge(mid_part, g + 1)
                dve.tensor_tensor(pv[:, :, 0:D], hv, pv[:, :, D:2 * D], ALU.subtract).then_inc(lo_part, 1)
            dve.wait_ge(mm_row, 32)
            dve.tensor_copy(sfx[:, 0, 0:GROUPS], rng[:, 0, 0:GROUPS])
            a, k = 0, 1
            while k < GROUPS:
                dve.drain()
                dve.tensor_tensor(sfx[:, 1 - a, 0:GROUPS], sfx[:, a, 0:GROUPS], sfx[:, a, k:GROUPS + k], ALU.min)
                a, k = 1 - a, 2 * k
            dve.drain()
            ticks = sfx[:, 1 - a, :]
            dve.memset(ticks[:, 0:1], 0.0)
            dve.tensor_tensor_scan(ticks[:, 1:GROUPS + 1], sfx_one[:, 0:GROUPS], sfx[:, a, 1:GROUPS + 1], 0.0, ALU.add, ALU.min)
            dve.drain()
            dve.scalar_tensor_tensor(code_f[:, :], rng[:, 1, :], 64.0, rng[:, 0, :], ALU.mult, ALU.add)
            dve.drain()
            dve.scalar_tensor_tensor(code_f[:, 1:GROUPS], ticks[:, 1:GROUPS], 64.0 ** 2, code_f[:, 1:GROUPS], ALU.mult, ALU.add)
            dve.drain()
            dve.scalar_tensor_tensor(code_f[:, 0:GROUPS], ticks[:, 1:GROUPS + 1], 64.0 ** 3, code_f[:, 0:GROUPS], ALU.mult, ALU.add)
            dve.drain()
            dve.tensor_copy(code[:, :], code_f[:, :]).then_inc(code_ready, 1)
            dve.wait_ge(nb_done, 1)
            dve.tensor_scalar(neg_base[:, :], banks[1][:, 0:GCOLS], -float(P), None, ALU.mult)
            dve.memset(acc[:, :, :], 0.0)
            dve.wait_ge(w_loaded, 16 * 7)
            dve.tensor_tensor(bias[:, :], bias[:, :], yS[:, :], ALU.add)
            dve.drain().then_inc(base_ready, 1)

            extra = dve.alloc_register("dve_extra")
            dve.reg_mov(extra, 0)

            def one_hots(it, q):
                dve.wait_ge(hot_rep, it * RING + (q + 1))
                dve.tensor_tensor(hot[:, q % HOTS, :, :], iota_b[:, :].unsqueeze(1).to_broadcast([P, CPG, P]),
                                  hot[:, q % HOTS, :, :], ALU.is_equal).then_inc(hot_ready, 1)

            def extras(g, c):
                first_tile, last_tile = field(dve, c, 0), field(dve, c, 1)
                with dve.If(last_tile > first_tile):
                    with dve.Fori(first_tile + 1, last_tile + 1) as tile:
                        t = a_tile(tile)
                        dve.reg_add(extra, extra, 1)
                        n = dve.snap(extra, min_val=1, max_val=GROUPS * NT)
                        dve.drain()
                        dve.tensor_scalar(dstx[:, :], dstT[:, bass.ds(g * CPG, CPG)], neg_tile[:, bass.ds(t, 1)], None, ALU.add)
                        dve.drain()
                        dve.tensor_tensor(hotx[:, :, :], iota_b[:, :].unsqueeze(1).to_broadcast([P, CPG, P]),
                                          dstx[:, :].unsqueeze(2).to_broadcast([P, CPG, P]), ALU.is_equal).then_inc(hotx_ready, 1)
                        dve.drain()
                        dve.wait_ge(groupx_mm, n)
                        dve.tensor_tensor(acc[:, bass.ds(t, 1), :], acc[:, bass.ds(t, 1), :],
                                          banks[2][:, 0:D + 1], ALU.add)
                return first_tile

            def tick(i, behind):
                if i is not None:
                    dve.drain()
                    dve.tensor_scalar(deg[:, bass.ds(i, 1)], acc[:, bass.ds(i, 1), D:D + 1], 1.0, None, ALU.max).then_inc(nd_deg, 1)

                def project(t):
                    r = rs[:, bass.ds(t, 1)]
                    dve.wait_ge(nd_sqrt, t + 1)
                    inv_sqrt(dve, r, tmp[:, bass.ds(t, 1)], deg[:, bass.ds(t, 1)])
                    dve.wait_ge(nd_proj, t + 1)
                    dve.wait_ge(nd_stored, t * 16 + 16)
                    dve.wait_ge(nd_yst, t + 1)
                    dve.tensor_tensor(yS[:, :], banks[4][:, D:2 * D], bias[:, :], ALU.add)
                    dve.drain()
                    dve.scalar_tensor_tensor(yS[:, :], banks[4][:, 0:D], r, yS[:, :], ALU.mult, ALU.add).then_inc(nd_y, 1)
                behind(1, project)

                def place(t):
                    dve.wait_ge(nd_rank, t + (DEPTH + 1))
                    for k in range(TOPK):
                        dve.tensor_tensor_reduce(out=junk[:, k, :], in0=pick[:, k, :], in1=banks[2][:, 5 * EX:6 * EX], scale=1.0,
                                                 scalar=0.0, op0=ALU.mult, op1=ALU.add, accum_out=rk[:, k:k + 1])
                    dve.tensor_tensor(taken[:, :], taken[:, :], picked[:, :], ALU.add)
                    dve.drain()
                    dve.tensor_copy(rki[:, 0, :], rk[:, :])
                    dve.tensor_copy(rank[:, bass.ds(t, 1), :], rk[:, :])
                    dve.drain()
                    dve.tensor_scalar(rki[:, 1, :], rki[:, 0, :], P - 1, None, ALU.bitwise_and)
                    dve.tensor_scalar(rki[:, 2, :], rki[:, 0, :], 7, None, ALU.arith_shift_right)
                    dve.drain()
                    dve.tensor_copy(rkf[:, :, :], rki[:, 1:3, :])
                    dve.drain()
                    dve.scalar_tensor_tensor(qs[:, :], i8f[:, :], float(SLOTCH), rkf[:, 1, :], ALU.mult, ALU.add)
                    dve.tensor_scalar(rk[:, :], rkf[:, 1, :], float(SLOTCH), 8192.0, ALU.is_ge, ALU.mult)
                    dve.wait_ge(nd_slot, t + (DEPTH + 1))
                    for k in range(TOPK):
                        dve.tensor_scalar(lo1[:, k, 0, :], iota_b[:, :], rkf[:, 0, k:k + 1], hnum[:, k, bass.ds(t, 1)],
                                          ALU.is_equal, ALU.mult)
                        dve.tensor_scalar(lo1[:, k, 1, :], iota_b[:, :], rkf[:, 0, k:k + 1], pcol[:, 0:1],
                                          ALU.is_equal, ALU.mult)
                    dve.drain()
                    dve.scalar_tensor_tensor(qs[:, :], rk[:, :], inval[:, bass.ds(t, 1)], qs[:, :], ALU.add, ALU.add)
                    dve.drain()
                    for k in range(TOPK):
                        last = dve.tensor_scalar(sel[:, k, :], iota_s[:, :], qs[:, k:k + 1], None, ALU.is_equal)
                    last.then_inc(nd_sel, 1)
                behind(2, place)

                def choose(t):
                    dve.wait_ge(nd_logit, t + 1)
                    dve.tensor_tensor(lg[:, :], banks[5][:, D:D + EX], bgb[:, :], ALU.add)
                    dve.drain()
                    dve.max(v8[:, :], lg[:, :])
                    dve.drain()
                    dve.max_index(i8[:, :], v8[:, :], lg[:, :])
                    dve.tensor_copy(top[:, bass.ds(t, 1), :], v8[:, 0:TOPK])
                    dve.drain()
                    dve.tensor_copy(i8f[:, :], i8[:, 0:TOPK])
                    dve.drain()
                    for k in range(TOPK):
                        dve.tensor_scalar(pick[:, k, :], iota_b[:, 0:EX], i8f[:, k:k + 1], valid[:, bass.ds(t, 1)],
                                          ALU.is_equal, ALU.mult)
                    dve.drain()
                    dve.tensor_tensor(picked[:, :], pick[:, 0, :], pick[:, 1, :], ALU.add).then_inc(nd_pick, 1)
                behind(1, choose)

            one_hots(0, 0)
            dve.sem_inc(nd_pick, DEPTH)
            dve.sem_inc(nd_sel, DEPTH)

            def step(it, first, final=False):
                for q in range(RING):
                    g = it * RING + q
                    if q + 1 < RING:
                        one_hots(it, q + 1)
                    elif not final:
                        one_hots(it + 1, 0)
                    c = group_code(dve, g)
                    first_tile = extras(g, c)
                    dve.drain()
                    dve.wait_ge(group_mm, g + 1)
                    dve.tensor_tensor(acc[:, bass.ds(first_tile, 1), :], acc[:, bass.ds(first_tile, 1), :],
                                      banks[q % 2][:, 0:D + 1], ALU.add).then_inc(acc_added, 1)
                    ticks_of_group(dve, c, tick)
            step(0, True)
            with dve.Fori(1, STEPS - 1) as it:
                step(it, False)
            step(STEPS - 1, False, True)
            last_ticks(dve, tick)

            dve.wait_ge(slots_mm, 1)
            dve.tensor_scalar(tok_t, banks[6][:, :], float(P), -float(P), ALU.mult, ALU.add)
            dve.drain()
            dve.tensor_tensor(tok_f, tok_t, banks[7][:, :], ALU.add)
            dve.drain()
            dve.tensor_scalar(tok_t, tok_f, 0.0, UNUSED, ALU.is_lt, ALU.mult)
            dve.drain()
            dve.tensor_tensor(tok_f, tok_f, tok_t, ALU.add)
            dve.drain()
            dve.tensor_copy(sidx[:, :], tok_f)
            dve.tensor_scalar(tok_t, tok_f, float(NPAD), -float(NPAD), ALU.is_ge, ALU.mult)
            dve.drain()
            dve.tensor_tensor(tok_f, tok_f, tok_t, ALU.add)
            dve.drain()
            dve.tensor_copy(gidx[:, :], tok_f)
            dve.tensor_scalar(nch_f[:, :], banks[5][0:1, 2 * P:2 * P + EX], float(CAP), float(P - 1), ALU.min, ALU.add)
            dve.drain()
            dve.tensor_copy(nch_i[:, :], nch_f[:, :])
            dve.drain()
            dve.tensor_scalar(nch_i[:, :], nch_i[:, :], 7, None, ALU.arith_shift_right)
            dve.drain()
            dve.tensor_scalar(nch_f[:, :], nch_i[:, :], 1.0, None, ALU.max)
            dve.drain()
            dve.tensor_copy(nch_i[:, :], nch_f[:, :])
            dve.memset(xg[:, :, :, :], 0.0)
            dve.memset(xgx[:, :], 0.0)
            dve.drain().then_inc(tables_done, 1)
            dve.tensor_tensor(gate[:, :, 1], top[:, :, 1], top[:, :, 0], ALU.subtract).then_inc(gap_ready, 1)
            dve.wait_ge(exp_ready, 1)
            dve.tensor_scalar(gate[:, :, 0], gate[:, :, 1], 1.0, None, ALU.add)
            dve.drain()
            dve.reciprocal(gate[:, :, 0], gate[:, :, 0])
            dve.drain()
            dve.tensor_tensor(gate[:, :, 1], gate[:, :, 1], gate[:, :, 0], ALU.mult)
            dve.tensor_scalar(rank[:, :, :], rank[:, :, :], float(CAP), None, ALU.is_lt)
            dve.drain()
            dve.tensor_tensor(gate[:, :, :], gate[:, :, :], rank[:, :, :], ALU.mult)

            def to_sbuf(e):
                dve.wait_ge(tokens_t, e + 1)
                dve.tensor_copy(xgT[:, 0:2, :, :], banks[0][:, :])
                dve.tensor_copy(xgT[:, 2, :, :], banks[1][:, 0:D]).then_inc(tokens_s, 1)

            nextra = dve.alloc_register("dve_nextra")
            dve.reg_mov(nextra, 0)

            def extra_chunks(e, par, nch):
                with dve.If(nch > MAIN):
                    with dve.Fori(MAIN, nch) as k:
                        dve.reg_add(nextra, nextra, 1)
                        n = dve.snap(nextra, min_val=1, max_val=EX * SLOTCH)
                        dve.wait_ge(xtra_t, n)
                        dve.tensor_copy(xgTx[:, :, :], banks[1][:, D:2 * D]).then_inc(xtra_s, 1)
                        dve.wait_ge(b2_in[par], landed(e, par))
                        dve.wait_ge(xtra_l2, n)
                        dve.tensor_tensor(outx[:, :], banks[6][:, 0:D], b2s[:, par, :], ALU.add).then_inc(xtra_out, 1)

            def expert(e, par, first, final=False):
                nch = dve.value_load(nch_i[0:1, bass.ds(e, 1)], min_val=1, max_val=SLOTCH)
                extra_chunks(e, par, nch)
                if not final:
                    to_sbuf(e + 1)
                dve.wait_ge(b2_in[par], landed(e, par))
                for k in range(MAIN):
                    dve.wait_ge(l2_done[k], e + 1)
                    if not first:
                        dve.wait_ge(scattered[par][k], prior_scatter(e, par))
                    dve.tensor_tensor(outs[:, par, k, :], out_bank(k), b2s[:, par, :], ALU.add).then_inc(out_ready, 1)
            to_sbuf(0)
            expert(0, 0, True)
            expert(1, 1, True)
            with dve.Fori(1, EX // 2 - 1) as i:
                expert(i * 2, 0, False)
                expert(i * 2 + 1, 1, False)
            expert(EX - 2, 0, False)
            expert(EX - 1, 1, False, True)

            dve.drain()
            for g in range(NB):
                dve.wait_ge(y2_in[g % 2], 16 * TOPK * (g // 2 + 1))
                for k in range(TOPK):
                    for t in range(TG):
                        tile = g * TG + t
                        last = dve.scalar_tensor_tensor(acc[:, tile, 0:D], ybuf[:, g % 2, k, t, :], gate[:, tile, k:k + 1],
                                                        acc[:, tile, 0:D], ALU.mult, ALU.add)
                    if k == 0:
                        dve.drain()
                last.then_inc(combined, 1)
            dve.wait_ge(mean_mm, 1)
            dve.tensor_scalar(mean[:, :], banks[0][:, 0:D], 1.0 / N, None, ALU.mult)
            dve.drain()
            for g in range(NB):
                yv = acc[:, g * TG:(g + 1) * TG, 0:D]
                dve.tensor_tensor(yv, yv, mean[:, :].unsqueeze(1).to_broadcast([P, TG, D]), ALU.subtract).then_inc(centered, 1)
            dve.wait_ge(var_mm, 1)
            dve.tensor_scalar(var[:, :], banks[1][:, 0:D], 1.0 / N, BN_EPS, ALU.mult, ALU.add).then_inc(var_ready, 1)
            dve.wait_ge(var_sqrt, 1)
            inv_sqrt(dve, scale[:, :], vroot[:, :], var[:, :])
            dve.drain()
            dve.tensor_tensor(scale[:, :], scale[:, :], gb[:, 0, :], ALU.mult)
            dve.drain()
            for g in range(NB):
                yv = acc[:, g * TG:(g + 1) * TG, 0:D]
                dve.tensor_tensor(yv, yv, scale[:, :].unsqueeze(1).to_broadcast([P, TG, D]), ALU.mult)
                dve.drain()
                dve.wait_ge(xbeta, NT)
                dve.tensor_tensor(yv, yv, xs[:, g * TG:(g + 1) * TG, :], ALU.add)
                dve.drain()
                for t in range(TG):
                    dve.bn_stats(stats[:, t, :], acc[:, g * TG + t, 0:D])
                dve.drain()
                for t in range(TG):
                    dve.bn_aggr(mv[:, g * TG + t, :], stats[:, t, :])
                dve.drain()
            dve.tensor_scalar(deg[:, :], mv[:, :, 1], LN_EPS, None, ALU.add).then_inc(lnvar_ready, 1)
            dve.wait_ge(lnvar_sqrt, 1)
            inv_sqrt(dve, rs[:, :], tmp[:, :], deg[:, :])
            dve.drain()
            for g in range(NB):
                for t in range(TG):
                    tile = g * TG + t
                    last = dve.tensor_scalar(acc[:, tile, 0:D], acc[:, tile, 0:D], mv[:, tile, 0:1], rs[:, tile:tile + 1],
                                             ALU.subtract, ALU.mult)
                last.then_inc(normed, 1)

        @block.tensor
        def _(pe):
            pe.wait_ge(const_d, 1)
            n = 0
            for which in range(LISTS):
                if which < 2:
                    pe.wait_ge(srch_f, which + 1)
                    lists = stage[:, (2 + which) * COLS:(3 + which) * COLS]
                else:
                    pe.wait_ge(dst_f, 1)
                    lists = srcT[:, :]
                for c in range(NTR):
                    if n >= 4:
                        pe.wait_ge(tr_copied, n - 3)
                    for j in range(min(4, EB - 4 * c)):
                        b = 4 * c + j
                        last = pe.transpose(banks[T_BANKS[n % 4]][:, j * P:(j + 1) * P], lists[:, b * P:(b + 1) * P], ident[:, :])
                    last.then_inc(tr_done, 1)
                    n += 1
            pe.wait_ge(dst_f, 2)
            for a in range(2):
                last = pe.transpose(banks[1][0:EB, a * P:(a + 1) * P], mnmx[:, a, :], ident[:, :])
            last.then_inc(mm_tr, 1)


            def hist(i, first, final=False):
                for q in range(2):
                    pe.wait_ge(lo_ready, i * 2 + (q + 1))
                    pe.wait_ge(hi_ready, i * 2 + (q + 1))
                    for c in range(HB):
                        last = pe.matmul(banks[0][:, 0:NT], lo_hot[:, q, c, :], hi_hot[:, q, c, :],
                                         start=first and q == 0 and c == 0, stop=final and q == 1 and c == HB - 1,
                                         skip_group_check=True)
                    last.then_inc(hist_mm, 1)
            hist(0, True)
            with pe.Fori(1, HSTEPS - 1) as i:
                hist(i, False)
            hist(HSTEPS - 1, False, True)

            pe.wait_ge(mm_row, 32)
            pe.matmul(banks[1][:, 0:GCOLS], ones[0:1, :], rng[0:1, 0, :], start=True, stop=True).then_inc(nb_done, 1)
            pe.wait_ge(code_ready, 1)

            extra = pe.alloc_register("pe_extra")
            pe.reg_mov(extra, 0)

            def multiply(bank, hots, q, done):
                for j in range(CPG):
                    for part in (2, 1, 0):
                        w = D + 1 if part == 2 else D
                        last = pe.matmul(bank[:, 0:w], hots[:, j, :], ring(q)[:, j, part * D:part * D + w],
                                         start=j == 0 and part == 2, stop=j == CPG - 1 and part == 0,
                                         skip_group_check=True)
                last.then_inc(done, 1)

            def tick(i, behind):
                if i is not None:
                    pe.wait_ge(nd_deg, i + 1)

                def places(t):
                    pe.wait_ge(nd_pick, t + (DEPTH + 1))
                    pe.matmul(banks[2][:, 5 * EX:6 * EX], tri[:, :], picked[:, :], start=True, stop=False)
                    pe.matmul(banks[2][:, 5 * EX:6 * EX], ones_b[:, :], taken[:, :], start=False, stop=True).then_inc(nd_rank, 1)
                behind(2, places)

                def slots(t):
                    pe.wait_ge(nd_sel, t + (DEPTH + 1))
                    for k in range(TOPK):
                        for a in range(2):
                            last = pe.matmul(banks[6 + a][:, :], lo1[:, k, a, :], sel[:, k, :], start=False, stop=False,
                                             skip_group_check=True)
                    last.then_inc(nd_slot, 1)
                behind(3, slots)
                if i is not None:
                    pe.wait_ge(nd_in, i + 1)
                    for k in range(2 * DK):
                        last = pe.transpose(banks[3][:, k * P:(k + 1) * P], (mS if k < DK else xS)[:, (k % DK) * P:(k % DK + 1) * P],
                                            ident[:, :])
                    last.then_inc(nd_tr, 1)

                def transpose_y(t):
                    pe.wait_ge(nd_y, t + 1)
                    for k in range(DK):
                        last = pe.transpose(banks[5][:, k * P:(k + 1) * P], yS[:, k * P:(k + 1) * P], ident[:, :])
                    last.then_inc(nd_ytr, 1)
                behind(1, transpose_y)
                if i is not None:
                    pe.wait_ge(nd_t, i + 1)
                    for a in range(2):
                        for k in range(DK):
                            last = pe.matmul(banks[4][:, a * D:(a + 1) * D], tS[:, a * DK + k, :], (wgc, wres)[a][:, k, :],
                                             start=k == 0, stop=k == DK - 1)
                    last.then_inc(nd_proj, 1)

                def logits(t):
                    pe.wait_ge(nd_yt, t + 1)
                    for k in range(DK):
                        last = pe.matmul(banks[5][:, D:D + EX], ytS[:, k, :], wg[:, k, :], start=k == 0, stop=k == DK - 1)
                    last.then_inc(nd_logit, 1)
                behind(1, logits)

            pe.sem_inc(nd_rank, DEPTH)
            pe.sem_inc(nd_slot, DEPTH + 1)
            pe.wait_ge(w_loaded, 16 * 7)
            for j in range(HK):
                last = pe.transpose(banks[3][:, j * EX:(j + 1) * EX], b1r[:, j * P:(j + 1) * P], ident[0:EX, 0:EX])
            last.then_inc(b1_t, 1)
            zb = zeros[:, :].bitcast(BF16)
            pe.wait_ge(tr_copied, LISTS * NTR)
            for a in range(2):
                pe.matmul(banks[6 + a][:, :], zb[:, 0:P], zb[:, 0:SC], start=True, stop=False, skip_group_check=True)

            def step(it, first):
                for q in range(RING):
                    g = it * RING + q
                    c = group_code(pe, g)
                    first_tile, last_tile = field(pe, c, 0), field(pe, c, 1)
                    pe.wait_ge(gath[q], it * (16 * CPG) + 16 * CPG)
                    if first and q == RING // 2:
                        pe.wait_ge(high_ones, 1)
                    with pe.If(last_tile > first_tile):
                        with pe.Fori(first_tile + 1, last_tile + 1) as t:
                            pe.reg_add(extra, extra, 1)
                            n = pe.snap(extra, min_val=1, max_val=GROUPS * NT)
                            pe.wait_ge(hotx_ready, n)
                            multiply(banks[2], hotx, q, groupx_mm)
                    pe.wait_ge(hot_ready, g + 1)
                    if not (first and q < 2):
                        pe.wait_ge(acc_added, g - 1)
                    multiply(banks[q % 2], hot[:, q % HOTS, :, :], q, group_mm)
                    ticks_of_group(pe, c, tick)
            step(0, True)
            with pe.Fori(1, STEPS) as it:
                step(it, False)
            last_ticks(pe, tick)
            for a in range(2):
                last = pe.matmul(banks[6 + a][:, :], zb[:, 0:P], zb[:, 0:SC], start=False, stop=True, skip_group_check=True)

            pe.matmul(banks[5][:, 2 * P:2 * P + EX], ones_b[:, :], taken[:, :], start=True, stop=True).then_inc(slots_mm, 1)

            nextra = pe.alloc_register("pe_nextra")
            pe.reg_mov(nextra, 0)

            def transpose_tokens(e, par):
                for k in range(MAIN):
                    pe.wait_ge(gathered[par][k], prior_scatter(e, par) + 16)
                    for c in range(DK):
                        last = pe.transpose(banks[k // 2][:, (k % 2) * D + c * P:(k % 2) * D + (c + 1) * P],
                                            xg[:, par, k, c * P:(c + 1) * P], ident[:, :])
                last.then_inc(tokens_t, 1)

            def first_layer(bank, par, xt, done):
                for j in range(HK):
                    for c in range(DK):
                        last = pe.matmul(bank[:, j * P:(j + 1) * P], w1s[:, par, c, j * P:(j + 1) * P], xt[:, c, :],
                                         start=c == 0, stop=c == DK - 1)
                last.then_inc(done, 1)

            def second_layer(dst, par, h, *done):
                for j in range(HK):
                    last = pe.matmul(dst, h[:, j, :], w2s[:, par, j, :], start=j == 0, stop=j == HK - 1)
                return last

            def expert(e, par, first, final=False):
                nch = pe.value_load(nch_i[0:1, bass.ds(e, 1)], min_val=1, max_val=SLOTCH)
                pe.wait_ge(w1_in[par], landed(e, par))
                pe.wait_ge(tokens_s, e + 1)
                with pe.If(nch > MAIN):
                    with pe.Fori(MAIN, nch) as k:
                        pe.reg_add(nextra, nextra, 1)
                        n = pe.snap(nextra, min_val=1, max_val=EX * SLOTCH)
                        pe.wait_ge(w2_in[par], landed(e, par))
                        if not first:
                            pe.wait_ge(out_ready, e * MAIN)
                        pe.wait_ge(xtra_gathered, n * 16)
                        for c in range(DK):
                            last = pe.transpose(banks[1][:, D + c * P:D + (c + 1) * P], xgx[:, c * P:(c + 1) * P], ident[:, :])
                        last.then_inc(xtra_t, 1)
                        pe.wait_ge(xtra_s, n)
                        first_layer(banks[5], par, xgTx, xtra_l1)
                        pe.wait_ge(xtra_h, n)
                        second_layer(banks[6][:, 0:D], par, h1x).then_inc(xtra_l2, 1)
                        pe.wait_ge(xtra_out, n)
                        pe.transpose(banks[5][:, 0:P], ident[:, :], ident[:, :])
                for k in range(MAIN):
                    if k == 0:
                        first_layer(banks[2 + k], par, xgT[:, k, :, :], l1_done[k])
                    else:
                        with pe.If(nch > k):
                            first_layer(banks[2 + k], par, xgT[:, k, :, :], l1_done[k])
                        with pe.Else():
                            pe.sem_inc(l1_done[k], 1)
                if not final:
                    transpose_tokens(e + 1, 1 - par)
                pe.wait_ge(w2_in[par], landed(e, par))
                if not first:
                    pe.wait_ge(out_ready, e * MAIN)
                for k in range(MAIN):
                    pe.wait_ge(h1_ready, e * MAIN + (k + 1))
                    if k == 0:
                        second_layer(out_bank(k), par, h1[:, k, :, :]).then_inc(l2_done[k], 1)
                    else:
                        with pe.If(nch > k):
                            if k == 2:
                                pe.wait_ge(out_ready, e * MAIN + 1)
                            second_layer(out_bank(k), par, h1[:, k, :, :]).then_inc(l2_done[k], 1)
                        with pe.Else():
                            pe.sem_inc(l2_done[k], 1)
                pe.drain().then_inc(expert_done, 1)

            transpose_tokens(0, 0)
            expert(0, 0, True)
            expert(1, 1, False)
            with pe.Fori(1, EX // 2 - 1) as i:
                expert(i * 2, 0, False)
                expert(i * 2 + 1, 1, False)
            expert(EX - 2, 0, False)
            expert(EX - 1, 1, False, True)

            for g in range(NB):
                pe.wait_ge(combined, g + 1)
                for t in range(TG):
                    tile = g * TG + t
                    last = pe.matmul(banks[0][:, 0:D], (ones_last if tile == NT - 1 else ones)[:, :], acc[:, tile, 0:D],
                                     start=tile == 0, stop=tile == NT - 1)
            last.then_inc(mean_mm, 1)
            for g in range(NB):
                pe.wait_ge(squared, g + 1)
                for t in range(TG):
                    tile = g * TG + t
                    last = pe.matmul(banks[1][:, 0:D], (ones_last if tile == NT - 1 else ones)[:, :], sq[:, g % 2, t, :],
                                     start=tile == 0, stop=tile == NT - 1)
                last.then_inc(sq_used, 1)
            pe.drain().then_inc(var_mm, 1)


_INS = ['x', 'src', 'dst', 'L0_gnn_W_gc', 'L0_gnn_b_gc', 'L0_gnn_W_res', 'L0_gnn_b_res', 'L0_gnn_Wg', 'L0_gnn_bg',
        'L0_gnn_w1', 'L0_gnn_b1', 'L0_gnn_w2', 'L0_gnn_b2', 'L0_gnn_gamma', 'L0_gnn_beta']
_OUTS = [((6250, 256), 'float32')]


def kernel(**inputs):
    import numpy as _np
    import concourse.bacc as _bacc
    from concourse import mybir as _mybir
    from concourse.bass_utils import run_bass_kernel_spmd as _run

    nc = _bacc.Bacc("TRN2", target_bir_lowering=False, num_devices=1)
    arrays, args = {}, []
    for name in _INS:
        a = _np.ascontiguousarray(inputs[name])
        arrays[f"in_{name}_dram"] = a
        args.append(nc.dram_tensor(f"in_{name}_dram", a.shape, _mybir.dt.from_np(a.dtype), kind="ExternalInput").ap())
    for i, (shape, dtype) in enumerate(_OUTS):
        dt = _mybir.dt.from_np(_np.dtype(dtype))
        args.append(nc.dram_tensor(f"out_{i}_dram", shape, dt, kind="ExternalOutput").ap())
    graph_moe_kernel(nc, *args)
    r = _run(nc, [arrays], core_ids=[0])
    return r.results[0]["out_0_dram"]
```

```python
import concourse.bass as bass
from concourse import mybir
from contextlib import ExitStack

F32 = mybir.dt.float32
BF16 = mybir.dt.bfloat16
I32 = mybir.dt.int32
U32 = mybir.dt.uint32
I16 = mybir.dt.int16
ALU = mybir.AluOpType
ACT = mybir.ActivationFunctionType
AX = mybir.AxisListType

P = 128
N, D, EDGES = 6250, 256, 200000
H, EX, TOPK, CAP = 512, 64, 2, 1024
BN_EPS = LN_EPS = 1e-5
NT = -(-N // P)
LAST = N - (NT - 1) * P
NPAD = NT * P
EB = -(-EDGES // (P * P))
EFULL = EDGES // P
ETAIL = EDGES - EFULL * P
CPG = 8
COLS = EB * P
GCOLS = COLS // CPG
RING = 6
HOTS = 2
GROUPS = -(-EDGES // (P * CPG))
STEPS = -(-GROUPS // RING)
LASTQ = GROUPS - (STEPS - 1) * RING
HB = 16
HQ = 4
HSTEPS = -(-(-(-EDGES // P)) // (HQ * HB))
SLOTCH = CAP // P
SC = EX * SLOTCH
MAIN = 3
TG = 7
NB = NT // TG
PAD_SRC = NPAD - 1
PAD_DST = 50 * P
UNUSED = 1.0e6
POOL_SCALES = tuple(range(2, NB))
DVE_NORMS = 4
DK, HK = D // P, H // P


def graph_moe_kernel(nc, x, src, dst, W_gc, b_gc, W_res, b_res, Wg, bg, w1, b1, w2, b2, gamma, beta, out):
    ctx = ExitStack()
    with ctx:
        def sb(name, shape, dt=F32):
            return ctx.enter_context(nc.sbuf_tensor(name, shape, dt))

        def sem(name):
            return ctx.enter_context(nc.semaphore(name))

        table = nc.dram_tensor("table", (NPAD, D), F32, kind="Internal").ap()
        nodes = nc.dram_tensor("nodes", (NPAD, D), F32, kind="Internal").ap()
        y2 = nc.dram_tensor("y2", (TOPK * NPAD, D), F32, kind="Internal").ap()

        xs = sb("xs", [P, NT, D])
        acc = sb("acc", [P, NT, D + 1])
        ident = sb("ident", [P, P])
        ones = sb("ones", [P, P])
        ones_last = sb("ones_last", [P, P])
        pcol = sb("pcol", [P, 1])
        iota_f = sb("iota_f", [P, P])
        iota_b = sb("iota_b", [P, P], BF16)
        iota_s = sb("iota_s", [P, SC], I16)
        zeros = sb("zeros", [P, 2 * D])
        wgc = sb("wgc", [P, DK, D])
        wres = sb("wres", [P, DK, D])
        wg = sb("wg", [P, DK, EX])
        bias = sb("bias", [P, D])
        bgb = sb("bgb", [P, EX])
        valid = sb("valid", [P, NT])
        acc_flat = acc[:, :, :].rearrange("p t d -> p (t d)")
        raw_src = acc_flat[:, 0:COLS].bitcast(I32).rearrange("p (b e) -> p b e", e=P)
        raw_dst = acc_flat[:, COLS:2 * COLS].bitcast(I32).rearrange("p (b e) -> p b e", e=P)
        loT = acc_flat[:, 2 * COLS:3 * COLS]
        hiT = acc_flat[:, 3 * COLS:4 * COLS]
        srcT = sb("srcT", [P, COLS])
        dstT = sb("dstT", [P, COLS])
        high0 = RING // 2 * CPG * (D + 1)
        stage = sb("stage", [P, high0 + CPG * P])
        ring_low = sb("ring", [P, RING // 2, CPG, D + 1])
        ring_high = stage[:, 0:high0].rearrange("p (q j r) -> p q j r", q=RING // 2, j=CPG)
        ring_idx = sb("ring_idx", [P, RING, CPG], I32)
        hot_low = sb("hot", [P, CPG, P])
        hot = (hot_low[:, :, :], stage[:, high0:high0 + CPG * P].rearrange("p (j d) -> p j d", j=CPG))
        slots = sb("slots", [P, 2, SC], I32)
        hotx = slots[:, :, :].rearrange("p a s -> p (a s)").bitcast(F32).rearrange("p (j d) -> p j d", j=CPG)
        dstx = sb("dstx", [P, CPG])
        dstq = sb("dstq", [P, HOTS, CPG])
        neg_tile = sb("neg_tile", [P, NT])
        neg_base = sb("neg_base", [P, GCOLS])
        mnmx = sb("mnmx", [P, 2, EB])
        rng_f = sb("rng_f", [EB, 2, P // CPG])
        rng_i = sb("rng_i", [EB, 2, P // CPG], I32)
        rng = sb("rng", [1, 2, GCOLS])
        code = sb("code", [1, GCOLS], I32)
        deg = sb("deg", [P, NT])
        rs = sb("rs", [P, NT])
        tmp = sb("tmp", [P, NT])
        mS = sb("mS", [P, D])
        xS = sb("xS", [P, D])
        tS = sb("tS", [P, 4, P])
        yS = sb("yS", [P, D])
        ytS = sb("ytS", [P, DK, P])
        lg = sb("lg", [P, EX])
        v8 = sb("v8", [P, 8])
        i8 = sb("i8", [P, 8], U32)
        i8f = sb("i8f", [P, TOPK])
        pick = sb("pick", [P, TOPK, EX], BF16)
        picked = sb("picked", [P, EX], BF16)
        taken = sb("taken", [P, EX], BF16)
        tri = sb("tri", [P, P], BF16)
        ones_b = sb("ones_b", [P, P], BF16)
        junk = sb("junk", [P, TOPK, EX], BF16)
        rk = sb("rk", [P, TOPK])
        rki = sb("rki", [P, 3, TOPK], I32)
        rkf = sb("rkf", [P, 2, TOPK])
        qs = sb("qs", [P, TOPK])
        inval = sb("inval", [P, NT])
        hnum = sb("hnum", [P, TOPK, NT])
        sel = sb("sel", [P, TOPK, SC], BF16)
        lo1 = sb("lo1", [P, TOPK, 2, P], BF16)
        top = sb("top", [P, NT, TOPK])
        rank = sb("rank", [P, NT, TOPK])
        gate = sb("gate", [P, NT, TOPK])
        tok_f = hot_low[:, :, :].rearrange("p j d -> p (j d)")[:, 0:SC]
        tok_t = hot_low[:, :, :].rearrange("p j d -> p (j d)")[:, SC:2 * SC]
        gidx, sidx = slots[:, 0, :], slots[:, 1, :]
        nch_f = sb("nch_f", [1, EX])
        nch_i = sb("nch_i", [1, EX], I32)
        b1r = sel[0:EX, :, :].rearrange("p k s -> p (k s)").bitcast(F32)
        b1T = sb("b1T", [P, HK, EX])
        b1e = sb("b1e", [P, HK])
        w1s = stage[:, 0:2 * DK * H].rearrange("p (b k h) -> p b k h", b=2, k=DK)
        w2s = stage[:, 2 * DK * H:4 * DK * H].rearrange("p (b j d) -> p b j d", b=2, j=HK)
        b2s = stage[:, 4 * DK * H:4 * DK * H + 2 * D].rearrange("p (b d) -> p b d", b=2)
        ybuf = stage[:, 0:4 * TG * D].rearrange("p (b k t d) -> p b k t d", b=2, k=TOPK, t=TG)
        sq = stage[:, 0:2 * TG * D].rearrange("p (b t d) -> p b t d", b=2, t=TG)
        arena = ring_low[:, :, :, :].rearrange("p a b c -> p (a b c)")
        taken_to = [0]

        def piece(n):
            taken_to[0] += n
            return arena[:, taken_to[0] - n:taken_to[0]]

        xg = piece(2 * MAIN * D).rearrange("p (b k d) -> p b k d", b=2, k=MAIN)
        xgT = piece(MAIN * D).rearrange("p (k c r) -> p k c r", k=MAIN, c=DK)
        h1 = piece(MAIN * H).rearrange("p (k j r) -> p k j r", k=MAIN, j=HK)
        outs = piece(2 * MAIN * D).rearrange("p (b k d) -> p b k d", b=2, k=MAIN)
        xgx = piece(D)
        xgTx = piece(D).rearrange("p (c r) -> p c r", c=DK)
        late = hot_low[:, :, :].rearrange("p a b -> p (a b)")
        gb = late[:, 0:2 * D].rearrange("p (a d) -> p a d", a=2)
        h1x = late[:, 2 * D:2 * D + H].rearrange("p (j r) -> p j r", j=HK)
        outx = mS
        mean, var, vroot, scale = xS, yS, tS[:, 0:DK, :].rearrange("p c r -> p (c r)"), tS[:, DK:2 * DK, :].rearrange("p c r -> p (c r)")
        slot_idx = sb("slot_idx", [P, 2, 2, MAIN], I32)
        xtra_idx = sb("xtra_idx", [P, 2], I32)
        stats = srcT[:, 0:TG * 6].rearrange("p (t s) -> p t s", s=6)
        mv = srcT[:, TG * 6:TG * 6 + 2 * NT].rearrange("p (t s) -> p t s", s=2)

        banks = [ctx.enter_context(nc.psum_tensor(f"bank{i}", [P, 512], F32)) for i in range(8)]

        lo_hot = stage[:, 0:HQ * HB * P // 2].bitcast(BF16).rearrange("p (b c n) -> p b c n", b=HQ, c=HB)
        hi0 = HQ * HB * P // 2
        hi_hot = stage[:, hi0:hi0 + HQ * HB * NT // 2].bitcast(BF16).rearrange("p (b c t) -> p b c t", b=HQ, c=HB)
        s0 = 2 * TG * D
        SFX = 656
        sfx = stage[0:1, s0:s0 + 2 * SFX].rearrange("o (a g) -> o a g", a=2)
        code_f = stage[0:1, s0 + 2 * SFX:s0 + 2 * SFX + GCOLS]
        sfx_one = code[:, :].bitcast(F32)
        scaled = stage[:, 0:2 * TG * D].rearrange("p (b t d) -> p b t d", b=2, t=TG)

        ini = sem("ini")
        const_p = sem("const_p")
        const_d = sem("const_d")
        src_loaded, dst_loaded, x_loaded, w_loaded = sem("src_loaded"), sem("dst_loaded"), sem("x_loaded"), sem("w_loaded")
        srch_f, dst_f = sem("srch_f"), sem("dst_f")
        tr_done, tr_copied = sem("tr_done"), sem("tr_copied")
        hi_diff, lo_ready, hi_ready, hist_mm = sem("hi_diff"), sem("lo_ready"), sem("hi_ready"), sem("hist_mm")
        mm_tr, mm_red, mm_row, nb_done = sem("mm_tr"), sem("mm_red"), sem("mm_row"), sem("nb_done")
        deg_ready, deg_sqrt, rs_ready = sem("deg_ready"), sem("deg_sqrt"), sem("rs_ready")
        h_ready = sem("h_ready")
        table_buf = [sem("table_buf0"), sem("table_buf1")]
        acc_zero = sem("acc_zero")
        code_ready = sem("code_ready")
        idx_ready = sem("idx_ready")
        gath = [sem(f"gath{q}") for q in range(RING)]
        hot_ready, group_mm, acc_added = sem("hot_ready"), sem("group_mm"), sem("acc_added")
        lo_rep, high_ones = sem("lo_rep"), sem("high_ones")
        hotx_ready, groupx_mm = sem("hotx_ready"), sem("groupx_mm")
        nd_recip, nd_root = sem("nd_recip"), sem("nd_root")
        nd_deg, nd_sqrt, nd_in, nd_tr, nd_t = sem("nd_deg"), sem("nd_sqrt"), sem("nd_in"), sem("nd_tr"), sem("nd_t")
        nd_proj, nd_y, nd_yst, nd_ytr, nd_yt, nd_logit = (sem("nd_proj"), sem("nd_y"), sem("nd_yst"), sem("nd_ytr"),
                                                          sem("nd_yt"), sem("nd_logit"))
        nd_pick, nd_rank, nd_sel, nd_slot = sem("nd_pick"), sem("nd_rank"), sem("nd_sel"), sem("nd_slot")
        y2_zeroed = sem("y2_zeroed")
        nd_stored = sem("nd_stored")
        slots_mm, tokens_clear, slots_ready = sem("slots_mm"), sem("tokens_clear"), sem("slots_ready")
        tables_done, gb_in, gap_ready, exp_ready = sem("tables_done"), sem("gb_in"), sem("gap_ready"), sem("exp_ready")
        b1_t = sem("b1_t")
        w1_in, w2_in, b2_in = ([sem(f"{w}_in{par}") for par in range(2)] for w in ("w1", "w2", "b2"))
        gathered = [[sem(f"gathered{par}{k}") for k in range(MAIN)] for par in range(2)]
        scattered = [[sem(f"scattered{par}{k}") for k in range(MAIN)] for par in range(2)]
        row_copied = sem("row_copied")
        slot_copied, tokens_t, tokens_s = sem("slot_copied"), sem("tokens_t"), sem("tokens_s")
        l1_done = [sem(f"l1_done{k}") for k in range(MAIN)]
        l2_done = [sem(f"l2_done{k}") for k in range(MAIN)]
        h1_ready = [sem(f"h1_ready{k}") for k in range(MAIN)]
        out_ready = sem("out_ready")
        xtra_copied, xtra_gathered, xtra_t, xtra_s = sem("xtra_copied"), sem("xtra_gathered"), sem("xtra_t"), sem("xtra_s")
        xtra_l1, xtra_h, xtra_l2, xtra_out, xtra_scattered = (sem("xtra_l1"), sem("xtra_h"), sem("xtra_l2"), sem("xtra_out"),
                                                              sem("xtra_scattered"))
        xtra_all, pool_starts, act_starts = sem("xtra_all"), sem("pool_starts"), sem("act_starts")
        y2_in = [sem("y2_in0"), sem("y2_in1")]
        combined, mean_mm, centered, squared, sq_used, var_mm = (sem("combined"), sem("mean_mm"), sem("centered"),
                                                                 sem("squared"), sem("sq_used"), sem("var_mm"))
        var_ready, var_sqrt, lnvar_ready, lnvar_sqrt = sem("var_ready"), sem("var_sqrt"), sem("lnvar_ready"), sem("lnvar_sqrt")
        scale_ready, pool_scaled, roots_ready, normed_d = sem("scale_ready"), sem("pool_scaled"), sem("roots_ready"), sem("normed_d")
        xbeta, normed, stored = sem("xbeta"), sem("normed"), sem("stored")

        def nth(e, par):
            return e // 2 if isinstance(e, int) else (e - par) // 2

        def landed(e, par):
            return nth(e, par) * 16 + 16

        def prior_scatter(e, par):
            return nth(e, par) * 16

        def out_bank(k):
            return banks[6 + k % 2][:, 0:D]

        def ring(q):
            return ring_low[:, q, :, :] if q < RING // 2 else ring_high[:, q - RING // 2, :, :]

        block = ctx.enter_context(nc.Block())

        T_BANKS = (4, 5, 6, 7)
        NTR = -(-EB // 4)
        LISTS = 3

        def group_code(eng, g):
            return eng.value_load(code[0:1, bass.ds(g, 1)], min_val=0, max_val=(1 << 24) - 1)

        def field(eng, c, k):
            return nc.s_assert_within(eng.snap((c >> (6 * k)) & 63), 0, NT if k > 1 else NT - 1,
                                      skip_runtime_bounds_check_because="the tables hold tiles below NT")

        def a_tile(t):
            return nc.s_assert_within(t, 0, NT - 1, skip_runtime_bounds_check_because="the codes hold tiles below NT")

        DEPTH = 3

        def ticks_of_group(eng, c, tick):
            before = field(eng, c, 2)
            now = field(eng, c, 3)
            with eng.If(now > before):
                i = a_tile(before)

                def behind(k, stage):
                    with eng.If(i > k - 1):
                        stage(nc.s_assert_within(i - k, 0, NT - 1 - k,
                                                 skip_runtime_bounds_check_because="the branch holds it above zero"))
                tick(i, behind)

        def last_ticks(eng, tick):
            i = field(eng, group_code(eng, GROUPS - 1), 3)
            with eng.If(i < NT):
                with eng.Fori(i, NT) as t:
                    t = a_tile(t)

                    def behind(k, stage):
                        with eng.If(t > k - 1):
                            stage(nc.s_assert_within(t - k, 0, NT - 1 - k,
                                                     skip_runtime_bounds_check_because="the branch holds it above zero"))
                    tick(t, behind)
            for t in range(NT, NT + DEPTH):
                def behind(k, stage):
                    if t - k < NT:
                        stage(t - k)
                tick(None, behind)

        def inv_sqrt(dve, r, s, d):
            dve.reciprocal(r, s)
            dve.drain()
            dve.tensor_tensor(s, r, r, ALU.mult)
            dve.drain()
            dve.tensor_tensor(s, s, d, ALU.mult)
            dve.drain()
            dve.tensor_scalar(s, s, -0.5, 1.5, ALU.mult, ALU.add)
            dve.drain()
            dve.tensor_tensor(r, r, s, ALU.mult)

        @block.sync
        def _(sp):
            sp.wait_ge(ini, 1)
            for raw, edges, loaded in ((raw_src, src, src_loaded), (raw_dst, dst, dst_loaded)):
                nb = EB - 1
                sp.dma_start(raw[:, 0:nb, :], edges[0:nb * P * P].rearrange("(b r e) -> r b e", r=P, e=P)).then_inc(loaded, 16)
                r = EFULL - nb * P
                sp.dma_start(raw[0:r, nb, :], edges[nb * P * P:EFULL * P].rearrange("(r e) -> r e", e=P)).then_inc(loaded, 16)
                sp.dma_start(raw[r:r + 1, nb, 0:ETAIL], edges[EFULL * P:EDGES].rearrange("(r e) -> r e", r=1)).then_inc(loaded, 16)
            sp.dma_start(xs[:, 0:NT - 1, :], x[0:(NT - 1) * P, :].rearrange("(t p) d -> p t d", p=P)).then_inc(x_loaded, 16)
            sp.dma_start(xs[0:LAST, NT - 1, :], x[(NT - 1) * P:N, :]).then_inc(x_loaded, 16)
            sp.dma_start(wgc[:, :, :], W_gc.rearrange("(k p) n -> p k n", p=P)).then_inc(w_loaded, 16)
            sp.dma_start(wres[:, :, :], W_res.rearrange("(k p) n -> p k n", p=P)).then_inc(w_loaded, 16)
            sp.dma_start(wg[:, :, :], Wg.rearrange("(k p) n -> p k n", p=P)).then_inc(w_loaded, 16)
            sp.dma_start(bias[:, :], b_gc.partition_broadcast(P)).then_inc(w_loaded, 16)
            sp.dma_start(yS[:, :], b_res.partition_broadcast(P)).then_inc(w_loaded, 16)
            sp.dma_start(bgb[:, :], bg.partition_broadcast(P)).then_inc(w_loaded, 16)
            sp.dma_start(b1r[:, :], b1).then_inc(w_loaded, 16)
            y2v = y2.rearrange("(p r) d -> p (r d)", p=P)
            with sp.Fori(0, TOPK * NPAD // P // 2) as i:
                sp.dma_start(y2v[:, bass.ds(i * (2 * D), 2 * D)], zeros[:, :]).then_inc(y2_zeroed, 16)
            sp.wait_ge(mm_red, 1)
            sp.dma_start(rng[0:1, 0, :], rng_f[:, 0, :]).then_inc(mm_row, 16)
            sp.dma_start(rng[0:1, 1, :], rng_f[:, 1, :]).then_inc(mm_row, 16)
            for g in range(NB):
                sp.wait_ge(h_ready, g + 1)
                tv = table[g * TG * P:(g + 1) * TG * P, :].rearrange("(t p) r -> p t r", p=P)
                sp.dma_start(tv, scaled[:, g % 2, :, :]).then_inc(table_buf[g % 2], 16)
            def weights(e, par, first):
                if not first:
                    for k in range(MAIN):
                        sp.wait_ge(l1_done[k], e - 1)
                sp.dma_start(w1s[:, par, :, :], w1[bass.ds(e, 1), :, :].rearrange("o (k p) h -> p (o k) h", p=P)).then_inc(w1_in[par], 16)
                if not first:
                    for k in range(MAIN):
                        sp.wait_ge(l2_done[k], e - 1)
                    sp.wait_ge(out_ready, MAIN * e - MAIN)
                sp.dma_start(w2s[:, par, :, :], w2[bass.ds(e, 1), :, :].rearrange("o (j p) d -> p (o j) d", p=P)).then_inc(w2_in[par], 16)
                sp.dma_start(b2s[:, par, :], b2[bass.ds(e, 1), :].rearrange("o d -> (o d)").partition_broadcast(P)).then_inc(b2_in[par], 16)
            sp.wait_ge(slots_mm, 1)
            weights(0, 0, True)
            weights(1, 1, True)
            sp.wait_ge(tables_done, 1)
            sp.dma_start(gb[:, 0, :], gamma.partition_broadcast(P)).then_inc(gb_in, 16)
            sp.dma_start(gb[:, 1, :], beta.partition_broadcast(P)).then_inc(gb_in, 16)
            with sp.Fori(1, EX // 2) as i:
                weights(i * 2, 0, False)
                weights(i * 2 + 1, 1, False)

            for par in range(2):
                for k in range(MAIN):
                    sp.wait_ge(scattered[par][k], 16 * EX // 2)
            sp.wait_ge(xtra_all, 1)
            for k in range(MAIN):
                sp.wait_ge(l2_done[k], EX)
            sp.wait_ge(out_ready, MAIN * EX)
            y2t = y2.rearrange("(k t p) d -> p k t d", k=TOPK, p=P)
            for g in range(NB):
                if g >= 2:
                    sp.wait_ge(combined, g - 1)
                for k in range(TOPK):
                    sp.dma_start(ybuf[:, g % 2, k, :, :], y2t[:, k, g * TG:(g + 1) * TG, :]).then_inc(y2_in[g % 2], 16)
            for g in range(NB):
                sp.wait_ge(normed, g + 1)
                if g == NB - 1:
                    sp.wait_ge(normed_d, 1)
                full = TG if g < NB - 1 else TG - 1
                r = g * TG * P
                sp.dma_start(out[r:r + full * P, :].rearrange("(t p) d -> p t d", p=P), acc[:, g * TG:g * TG + full, 0:D]).then_inc(stored, 16)
            sp.dma_start(out[(NT - 1) * P:N, :], acc[0:LAST, NT - 1, 0:D]).then_inc(stored, 16)
            sp.wait_ge(stored, 16 * (NB + 1))

        @block.gpsimd
        def _(pool):
            pool.iota(iota_f[:, :], pattern=[[1, P]], base=0, channel_multiplier=0,
                      allow_small_or_imprecise_dtypes=True).then_inc(const_p, 1)
            pool.iota(iota_b[:, :], pattern=[[1, P]], base=0, channel_multiplier=0,
                      allow_small_or_imprecise_dtypes=True).then_inc(const_p, 1)
            pool.iota(pcol[:, :], pattern=[[0, 1]], base=0, channel_multiplier=1,
                      allow_small_or_imprecise_dtypes=True).then_inc(const_p, 1)
            pool.iota(iota_s[:, :], pattern=[[1, SC]], base=0, channel_multiplier=0,
                      allow_small_or_imprecise_dtypes=True).then_inc(const_p, 1)
            pool.iota(neg_tile[:, :], pattern=[[-P, NT]], base=0, channel_multiplier=0,
                      allow_small_or_imprecise_dtypes=True).then_inc(const_p, 1)
            pool.iota(hnum[:, :, :], pattern=[[NT, TOPK], [1, NT]], base=1, channel_multiplier=0,
                      allow_small_or_imprecise_dtypes=True).then_inc(const_p, 1)
            pool.memset(ring_low[:, :, :, D:D + 1], 1.0).then_inc(const_p, 1)

            pool.wait_ge(tr_copied, 2 * NTR)
            pool.wait_ge(const_p, 7)

            def hist(i, first):
                for q in range(HQ):
                    if not first:
                        pool.wait_ge(hist_mm, i * HQ + (q - HQ + 1))
                    pool.tensor_tensor(hi_hot[:, q, :, :],
                                       iota_f[:, 0:NT].unsqueeze(1).to_broadcast([P, HB, NT]),
                                       hiT[:, bass.ds((i * HQ + q) * HB, HB)].unsqueeze(2).to_broadcast([P, HB, NT]),
                                       ALU.subtract).then_inc(hi_diff, 1)
            hist(0, True)
            with pool.Fori(1, HSTEPS) as i:
                hist(i, False)

            pool.wait_ge(rs_ready, 1)
            pool.memset(acc[:, :, :], 0.0).then_inc(acc_zero, 1)

            node_reg, row_reg = pool.alloc_register("last_node"), pool.alloc_register("last_row")
            pool.reg_mov(node_reg, N - 1)
            pool.reg_mov(row_reg, TOPK * NPAD - 1)
            last_node, last_row = node_reg, row_reg

            def start():
                pool.sem_inc(pool_starts, 1)

            for q in range(2):
                pool.wait_ge(table_buf[q], 16 * ((NB + 1 - q) // 2))

            def gather(it, first, final=False):
                for q in range(LASTQ if final else RING):
                    if first and q == RING // 2:
                        pool.wait_ge(code_ready, 1)
                        pool.memset(ring_high[:, :, :, D:D + 1], 1.0).then_inc(high_ones, 1)
                    pool.wait_ge(idx_ready, it * RING + (q + 1))
                    if not first:
                        pool.wait_ge(acc_added, it * RING + (q - RING + 1))
                    start()
                    for j in range(CPG):
                        pool.indirect_dma_start(
                            out=ring(q)[:, j, 0:D], out_offset=None, in_=table[:, :],
                            in_offset=bass.IndirectOffsetOnAxis(ap=ring_idx[:, q, j:j + 1], axis=0),
                            bounds_check=last_node, oob_is_err=False).then_inc(gath[q], 16)
            gather(0, True)
            with pool.Fori(1, STEPS - 1) as it:
                gather(it, False)
            gather(STEPS - 1, False, True)

            pool.wait_ge(y2_zeroed, 16 * (TOPK * NPAD // P // 2))
            pool.wait_ge(nd_stored, 16 * NT + 16)
            pool.wait_ge(slots_mm, 1)
            pool.memset(xg[:, :, :, :], 0.0).then_inc(tokens_clear, 1)
            pool.memset(xgx[:, :], 0.0).then_inc(tokens_clear, 1)
            pool.wait_ge(tokens_clear, 2)
            pool.wait_ge(slots_ready, 1)

            def load_slots(e, par, first):
                if not first:
                    pool.wait_ge(tokens_t, e - 1)
                    start()
                pool.tensor_copy(slot_idx[:, par, 0, :], gidx[:, bass.ds(e * SLOTCH, MAIN)]).then_inc(slot_copied, 1)
                pool.wait_ge(slot_copied, e + 1)
                start()
                for k in range(MAIN):
                    pool.indirect_dma_start(
                        out=xg[:, par, k, :], out_offset=None, in_=nodes[:, :],
                        in_offset=bass.IndirectOffsetOnAxis(ap=slot_idx[:, par, 0, k:k + 1], axis=0),
                        bounds_check=last_node, oob_is_err=False).then_inc(gathered[par][k], 16)

            def store_slots(e, par, first):
                if not first:
                    for k in range(MAIN):
                        pool.wait_ge(scattered[par][k], prior_scatter(e, par))
                    start()
                pool.tensor_copy(slot_idx[:, par, 1, :], sidx[:, bass.ds(e * SLOTCH, MAIN)]).then_inc(row_copied, 1)
                pool.wait_ge(row_copied, e + 1)
                start()
                for k in range(MAIN):
                    pool.wait_ge(out_ready, e * MAIN + (k + 1))
                    start()
                    pool.indirect_dma_start(
                        out=y2[:, :], out_offset=bass.IndirectOffsetOnAxis(ap=slot_idx[:, par, 1, k:k + 1], axis=0),
                        in_=outs[:, par, k, :], in_offset=None,
                        bounds_check=last_row, oob_is_err=False).then_inc(scattered[par][k], 16)

            nextra = pool.alloc_register("pool_nextra")
            pool.reg_mov(nextra, 0)

            def extra_chunks(e, nch):
                with pool.If(nch > MAIN):
                    with pool.Fori(MAIN, nch) as k:
                        col = nc.s_assert_within(e * SLOTCH + k, 0, SC - 1,
                                                 skip_runtime_bounds_check_because="no expert has more than SLOTCH chunks")
                        pool.reg_add(nextra, nextra, 1)
                        n = pool.snap(nextra, min_val=1, max_val=EX * SLOTCH)
                        pool.tensor_copy(xtra_idx[:, 0:1], gidx[:, bass.ds(col, 1)])
                        pool.tensor_copy(xtra_idx[:, 1:2], sidx[:, bass.ds(col, 1)]).then_inc(xtra_copied, 1)
                        pool.wait_ge(xtra_copied, n)
                        start()
                        pool.indirect_dma_start(
                            out=xgx[:, :], out_offset=None, in_=nodes[:, :],
                            in_offset=bass.IndirectOffsetOnAxis(ap=xtra_idx[:, 0:1], axis=0),
                            bounds_check=last_node, oob_is_err=False).then_inc(xtra_gathered, 16)
                        pool.wait_ge(xtra_out, n)
                        start()
                        pool.indirect_dma_start(
                            out=y2[:, :], out_offset=bass.IndirectOffsetOnAxis(ap=xtra_idx[:, 1:2], axis=0),
                            in_=outx[:, :], in_offset=None,
                            bounds_check=last_row, oob_is_err=False).then_inc(xtra_scattered, 16)
                        pool.wait_ge(xtra_scattered, n * 16)
                        start()

            def chunks_of(e):
                return pool.value_load(nch_i[0:1, bass.ds(e, 1)], min_val=1, max_val=SLOTCH)

            def expert(e, par, first, ahead=True):
                extra_chunks(e, chunks_of(e))
                if ahead:
                    load_slots(e + 2, par, False)
                store_slots(e, par, first)

            load_slots(0, 0, True)
            load_slots(1, 1, True)
            pool.wait_ge(tables_done, 1)
            expert(0, 0, True)
            expert(1, 1, True)
            with pool.Fori(1, EX // 2 - 1) as i:
                expert(i * 2, 0, False)
                expert(i * 2 + 1, 1, False)
            expert(EX - 2, 0, False, False)
            expert(EX - 1, 1, False, False)
            pool.drain().then_inc(xtra_all, 1)
            pool.wait_ge(gb_in, 32)
            for t in range(NB):
                pool.tensor_tensor(xs[:, t * TG:(t + 1) * TG, :], xs[:, t * TG:(t + 1) * TG, :],
                                   gb[:, 1, :].unsqueeze(1).to_broadcast([P, TG, D]), ALU.add).then_inc(xbeta, 1)
            pool.wait_ge(scale_ready, 1)
            for g in POOL_SCALES:
                yv = acc[:, g * TG:(g + 1) * TG, 0:D]
                pool.tensor_tensor(yv, yv, scale[:, :].unsqueeze(1).to_broadcast([P, TG, D]), ALU.mult).then_inc(pool_scaled, 1)

        @block.scalar
        def _(act):
            n = 0
            for which in range(LISTS):
                target = (loT, hiT, dstT)[which]
                for c in range(NTR):
                    w = min(4, EB - 4 * c) * P
                    act.wait_ge(tr_done, n + 1)
                    act.activation(target[:, c * 512:c * 512 + w], banks[T_BANKS[n % 4]][:, 0:w], ACT.Copy).then_inc(tr_copied, 1)
                    n += 1

            def hist(i, first):
                for q in range(HQ - 1):
                    if not first:
                        act.wait_ge(hist_mm, i * HQ + (q - HQ + 1))
                    act.activation(lo_hot[:, q, :, :],
                                   loT[:, bass.ds((i * HQ + q) * HB, HB)].unsqueeze(2).to_broadcast([P, HB, P]),
                                   ACT.Copy).then_inc(lo_rep, 1)
            act.wait_ge(srch_f, 2)
            hist(0, True)
            with act.Fori(1, HSTEPS) as i:
                hist(i, False)
            act.wait_ge(deg_ready, 1)
            act.activation(tmp[:, :], deg[:, :], ACT.Sqrt).then_inc(deg_sqrt, 1)
            act.sem_inc(nd_stored, 16)
            act.sem_inc(nd_yst, 1)
            act.wait_ge(b1_t, 1)
            act.activation(b1T[:, :, :], banks[3][:, 0:HK * EX], ACT.Copy)
            act.drain()
            act.wait_ge(code_ready, 1)

            def indices(it, q, first):
                if not first:
                    act.wait_ge(gath[q], it * (16 * CPG))
                act.activation(ring_idx[:, q, :], srcT[:, bass.ds((it * RING + q) * CPG, CPG)], ACT.Copy).then_inc(idx_ready, 1)

            def tick(i, behind):
                if i is not None:
                    act.wait_ge(nd_deg, i + 1)
                    act.activation(mS[:, :], acc[:, bass.ds(i, 1), 0:D], ACT.Copy)
                    act.activation(xS[:, :], xs[:, bass.ds(i, 1), :], ACT.Copy).then_inc(nd_in, 1)
                    act.activation(tmp[:, bass.ds(i, 1)], deg[:, bass.ds(i, 1)], ACT.Sqrt).then_inc(nd_sqrt, 1)

                def transposed_y(t):
                    act.wait_ge(nd_ytr, t + 1)
                    act.activation(ytS[:, :, :], banks[5][:, 0:D], ACT.Copy).then_inc(nd_yt, 1)
                behind(1, transposed_y)
                if i is not None:
                    act.wait_ge(nd_tr, i + 1)
                    act.activation(tS[:, :, :], banks[3][:, :], ACT.Copy).then_inc(nd_t, 1)

                def keep_y(t):
                    act.wait_ge(nd_y, t + 1)
                    act.dma_start(nodes[bass.ds(t * P, P), :], yS[:, :]).then_inc(nd_stored, 16)
                    act.activation(acc[:, bass.ds(t, 1), 0:D], yS[:, :], ACT.Copy).then_inc(nd_yst, 1)
                behind(1, keep_y)
                if i is not None:
                    r, d, s = rs[:, bass.ds(i, 1)], deg[:, bass.ds(i, 1)], tmp[:, bass.ds(i, 1)]
                    act.wait_ge(nd_recip, i + 1)
                    act.activation(s, r, ACT.Square)
                    act.drain()
                    act.activation(s, s, ACT.Identity, scale=d)
                    act.drain()
                    act.activation(s, s, ACT.Copy, scale=-0.5, bias=1.5)
                    act.drain()
                    act.activation(r, s, ACT.Identity, scale=r).then_inc(nd_root, 1)

            LEAD = RING
            for q in range(LEAD):
                indices(0, q, True)

            def step(it, first):
                for q in range(RING):
                    ahead = q + LEAD
                    indices(it + ahead // RING, ahead % RING, first and ahead < RING)
                    ticks_of_group(act, group_code(act, it * RING + q), tick)
            step(0, True)
            with act.Fori(1, STEPS - 1) as it:
                step(it, False)
            it = STEPS - 1
            for q in range(LASTQ):
                ticks_of_group(act, group_code(act, it * RING + q), tick)
            last_ticks(act, tick)

            act.wait_ge(gap_ready, 1)
            act.activation(gate[:, :, 1], gate[:, :, 1], ACT.Exp).then_inc(exp_ready, 1)
            nextra = act.alloc_register("act_nextra")
            act.reg_mov(nextra, 0)

            def expert(e, first):
                act.drain()
                act.activation(b1e[:, :], b1T[:, :, bass.ds(e, 1)], ACT.Copy)
                act.drain()
                nch = act.value_load(nch_i[0:1, bass.ds(e, 1)], min_val=1, max_val=SLOTCH)
                with act.If(nch > MAIN):
                    with act.Fori(MAIN, nch) as k:
                        act.reg_add(nextra, nextra, 1)
                        n = act.snap(nextra, min_val=1, max_val=EX * SLOTCH)
                        act.wait_ge(xtra_l1, n)
                        for j in range(HK):
                            last = act.activation(h1x[:, j, :], banks[5][:, j * P:(j + 1) * P], ACT.Gelu,
                                                  bias=b1e[:, j:j + 1])
                        last.then_inc(xtra_h, 1)
                def hidden(k):
                    for j in range(HK):
                        last = act.activation(h1[:, k, j, :], banks[2 + k][:, j * P:(j + 1) * P], ACT.Gelu,
                                              bias=b1e[:, j:j + 1])
                    last.then_inc(h1_ready[k], 1)
                for k in range(MAIN):
                    act.wait_ge(l1_done[k], e + 1)
                    if not first:
                        act.wait_ge(l2_done[k], e)
                    if k == 0:
                        hidden(k)
                    else:
                        act.sem_inc(act_starts, 1)
                        with act.If(nch > k):
                            hidden(k)
                        with act.Else():
                            act.sem_inc(h1_ready[k], 1)
            expert(0, True)
            with act.Fori(1, EX) as e:
                expert(e, False)
            for g in range(NB):
                act.wait_ge(centered, g + 1)
                if g >= 2:
                    act.wait_ge(sq_used, g - 1)
                act.activation(sq[:, g % 2, :, :], acc[:, g * TG:(g + 1) * TG, 0:D], ACT.Square).then_inc(squared, 1)
            act.wait_ge(var_ready, 1)
            act.activation(vroot[:, :], var[:, :], ACT.Sqrt).then_inc(var_sqrt, 1)
            def normalise(g):
                act.wait_ge(roots_ready, g + 1)
                for t in range(TG if g < NB - 1 else TG - DVE_NORMS):
                    tile = g * TG + t
                    last = act.activation(acc[:, tile, 0:D], acc[:, tile, 0:D], ACT.Identity, bias=deg[:, tile:tile + 1],
                                          scale=rs[:, tile:tile + 1])
                last.then_inc(normed, 1)
            for g in range(NB):
                act.wait_ge(lnvar_ready, g + 1)
                act.activation(tmp[:, g * TG:(g + 1) * TG], deg[:, g * TG:(g + 1) * TG], ACT.Sqrt).then_inc(lnvar_sqrt, 1)
                if g:
                    normalise(g - 1)
            normalise(NB - 1)

        @block.vector
        def _(dve):
            dve.memset(raw_src[:, EB - 1, :], PAD_SRC)
            dve.memset(raw_dst[:, EB - 1, :], PAD_DST)
            dve.memset(xs[:, NT - 1, :], 0.0)
            dve.memset(zeros[:, :], 0.0)
            dve.drain().then_inc(ini, 1)
            dve.memset(ones[:, :], 1.0)
            dve.memset(ones_b[:, :], 1.0)
            dve.memset(taken[:, :], 0.0)
            dve.memset(valid[:, :], 1.0)
            dve.wait_ge(const_p, 6)
            dve.tensor_scalar(ident[:, :], iota_f[:, :], pcol[:, 0:1], None, ALU.is_equal)
            dve.tensor_scalar(tri[:, :], iota_f[:, :], pcol[:, 0:1], None, ALU.is_gt)
            dve.drain()
            dve.tensor_scalar(valid[:, NT - 1:NT], pcol[:, :], float(LAST), None, ALU.is_lt)
            dve.drain()
            dve.tensor_scalar(inval[:, :], valid[:, :], -8192.0, 8192.0, ALU.mult, ALU.add)
            dve.tensor_scalar(ones_last[:, :], ones[:, :], valid[:, NT - 1:NT], None, ALU.mult)
            dve.drain().then_inc(const_d, 1)
            dve.wait_ge(src_loaded, 48)
            s_lo, s_hi = stage[:, 0:COLS].bitcast(I32), stage[:, COLS:2 * COLS].bitcast(I32)
            flat = raw_src[:, :, :].rearrange("p b e -> p (b e)")
            dve.tensor_scalar(s_lo, flat, P - 1, None, ALU.bitwise_and)
            dve.drain()
            dve.tensor_copy(stage[:, 2 * COLS:3 * COLS], s_lo).then_inc(srch_f, 1)
            dve.tensor_scalar(s_hi, flat, 7, None, ALU.arith_shift_right)
            dve.drain()
            dve.tensor_copy(stage[:, 3 * COLS:4 * COLS], s_hi).then_inc(srch_f, 1)
            dve.wait_ge(dst_loaded, 48)
            dstf = srcT[:, :]
            dve.tensor_copy(dstf, raw_dst[:, :, :].rearrange("p b e -> p (b e)")).then_inc(dst_f, 1)
            dve.drain()
            dv = dstf.rearrange("p (b e) -> p b e", e=P)
            dve.tensor_reduce(mnmx[:, 0, :], dv, op=ALU.min, axis=AX.X)
            dve.tensor_reduce(mnmx[:, 1, :], dv, op=ALU.max, axis=AX.X).then_inc(dst_f, 1)

            dve.wait_ge(tr_copied, 2 * NTR)

            def hist(i, first):
                for q in range(HQ):
                    if q < HQ - 1:
                        dve.wait_ge(lo_rep, i * (HQ - 1) + (q + 1))
                        lo = lo_hot[:, q, :, :]
                    else:
                        if not first:
                            dve.wait_ge(hist_mm, i * HQ + (q - HQ + 1))
                        lo = loT[:, bass.ds((i * HQ + q) * HB, HB)].unsqueeze(2).to_broadcast([P, HB, P])
                    dve.tensor_tensor(lo_hot[:, q, :, :], iota_b[:, :].unsqueeze(1).to_broadcast([P, HB, P]),
                                      lo, ALU.is_equal).then_inc(lo_ready, 1)
                    dve.wait_ge(hi_diff, i * HQ + (q + 1))
                    dve.tensor_scalar(hi_hot[:, q, :, :], hi_hot[:, q, :, :], 0.0, None, ALU.is_equal).then_inc(hi_ready, 1)
            hist(0, True)
            with dve.Fori(1, HSTEPS) as i:
                hist(i, False)
            dve.wait_ge(tr_copied, LISTS * NTR)
            dve.scalar_tensor_tensor(srcT[:, :], hiT[:, :], float(P), loT[:, :], ALU.mult, ALU.add)
            dve.wait_ge(hist_mm, HQ * HSTEPS)
            dve.tensor_scalar(deg[:, :], banks[0][:, 0:NT], 1.0, None, ALU.max).then_inc(deg_ready, 1)
            dve.wait_ge(deg_sqrt, 1)
            inv_sqrt(dve, rs[:, :], tmp[:, :], deg[:, :])
            dve.drain().then_inc(rs_ready, 1)

            def scale_nodes(g):
                if g >= 2:
                    dve.wait_ge(table_buf[g % 2], 16 * (g // 2))
                for t in range(TG):
                    tile = g * TG + t
                    last = dve.tensor_scalar(scaled[:, g % 2, t, :], xs[:, tile, :], rs[:, tile:tile + 1], None, ALU.mult)
                last.then_inc(h_ready, 1)
            dve.wait_ge(x_loaded, 32)
            scale_nodes(0)
            scale_nodes(1)
            dve.wait_ge(mm_tr, 1)
            mt = banks[1][0:EB, 0:2 * P].rearrange("p (a g c) -> p a g c", a=2, c=CPG)
            dve.tensor_reduce(rng_f[:, 0, :], mt[:, 0, :, :], op=ALU.min, axis=AX.X)
            dve.tensor_reduce(rng_f[:, 1, :], mt[:, 1, :, :], op=ALU.max, axis=AX.X)
            dve.drain()
            dve.tensor_copy(rng_i[:, :, :], rng_f[:, :, :])
            dve.drain()
            dve.tensor_scalar(rng_i[:, :, :], rng_i[:, :, :], 7, None, ALU.arith_shift_right)
            dve.drain()
            dve.tensor_scalar(rng_f[:, :, :], rng_i[:, :, :], float(NT - 1), None, ALU.min).then_inc(mm_red, 1)
            dve.memset(sfx[:, :, :], float(NT))
            dve.memset(sfx_one[:, :], 1.0)
            for g in range(2, NB):
                scale_nodes(g)
            dve.wait_ge(mm_row, 32)
            dve.tensor_copy(sfx[:, 0, 0:GROUPS], rng[:, 0, 0:GROUPS])
            a, k = 0, 1
            while k < GROUPS:
                dve.drain()
                dve.tensor_tensor(sfx[:, 1 - a, 0:GROUPS], sfx[:, a, 0:GROUPS], sfx[:, a, k:GROUPS + k], ALU.min)
                a, k = 1 - a, 2 * k
            dve.drain()
            ticks = sfx[:, 1 - a, :]
            dve.memset(ticks[:, 0:1], 0.0)
            dve.tensor_tensor_scan(ticks[:, 1:GROUPS + 1], sfx_one[:, 0:GROUPS], sfx[:, a, 1:GROUPS + 1], 0.0, ALU.add, ALU.min)
            dve.drain()
            dve.scalar_tensor_tensor(code_f[:, :], rng[:, 1, :], 64.0, rng[:, 0, :], ALU.mult, ALU.add)
            dve.drain()
            dve.scalar_tensor_tensor(code_f[:, 1:GROUPS], ticks[:, 1:GROUPS], 64.0 ** 2, code_f[:, 1:GROUPS], ALU.mult, ALU.add)
            dve.drain()
            dve.scalar_tensor_tensor(code_f[:, 0:GROUPS], ticks[:, 1:GROUPS + 1], 64.0 ** 3, code_f[:, 0:GROUPS], ALU.mult, ALU.add)
            dve.drain()
            dve.tensor_copy(code[:, :], code_f[:, :]).then_inc(code_ready, 1)
            dve.wait_ge(nb_done, 1)
            dve.tensor_scalar(neg_base[:, :], banks[1][:, 0:GCOLS], -float(P), None, ALU.mult)
            dve.wait_ge(acc_zero, 1)
            dve.wait_ge(w_loaded, 16 * 7)
            dve.tensor_tensor(bias[:, :], bias[:, :], yS[:, :], ALU.add)
            dve.drain()

            extra = dve.alloc_register("dve_extra")
            dve.reg_mov(extra, 0)

            def one_hots(it, q, first=False):
                g = it * RING + q
                if not (first and q < HOTS):
                    dve.wait_ge(group_mm, it * RING + (q - HOTS + 1))
                dve.tensor_scalar(dstq[:, q % HOTS, :], dstT[:, bass.ds(g * CPG, CPG)], neg_base[:, bass.ds(g, 1)], None, ALU.add)
                dve.drain()
                dve.tensor_tensor(hot[q % HOTS], iota_b[:, :].unsqueeze(1).to_broadcast([P, CPG, P]),
                                  dstq[:, q % HOTS, :].unsqueeze(2).to_broadcast([P, CPG, P]), ALU.is_equal).then_inc(hot_ready, 1)

            def extras(g, c):
                first_tile, last_tile = field(dve, c, 0), field(dve, c, 1)
                with dve.If(last_tile > first_tile):
                    with dve.Fori(first_tile + 1, last_tile + 1) as tile:
                        t = a_tile(tile)
                        dve.reg_add(extra, extra, 1)
                        n = dve.snap(extra, min_val=1, max_val=GROUPS * NT)
                        dve.drain()
                        dve.tensor_scalar(dstx[:, :], dstT[:, bass.ds(g * CPG, CPG)], neg_tile[:, bass.ds(t, 1)], None, ALU.add)
                        dve.drain()
                        dve.tensor_tensor(hotx[:, :, :], iota_b[:, :].unsqueeze(1).to_broadcast([P, CPG, P]),
                                          dstx[:, :].unsqueeze(2).to_broadcast([P, CPG, P]), ALU.is_equal).then_inc(hotx_ready, 1)
                        dve.drain()
                        dve.wait_ge(groupx_mm, n)
                        dve.tensor_tensor(acc[:, bass.ds(t, 1), :], acc[:, bass.ds(t, 1), :],
                                          banks[2][:, 0:D + 1], ALU.add)
                return first_tile

            def tick(i, behind):
                if i is not None:
                    dve.drain()
                    dve.tensor_scalar(deg[:, bass.ds(i, 1)], acc[:, bass.ds(i, 1), D:D + 1], 1.0, None, ALU.max).then_inc(nd_deg, 1)

                def project(t):
                    r = rs[:, bass.ds(t, 1)]
                    dve.wait_ge(nd_root, t + 1)
                    dve.wait_ge(nd_proj, t + 1)
                    dve.wait_ge(nd_stored, t * 16 + 16)
                    dve.wait_ge(nd_yst, t + 1)
                    dve.tensor_tensor(yS[:, :], banks[4][:, D:2 * D], bias[:, :], ALU.add)
                    dve.drain()
                    dve.scalar_tensor_tensor(yS[:, :], banks[4][:, 0:D], r, yS[:, :], ALU.mult, ALU.add).then_inc(nd_y, 1)
                behind(1, project)

                def place(t):
                    dve.wait_ge(nd_rank, t + (DEPTH + 1))
                    for k in range(TOPK):
                        dve.tensor_tensor_reduce(out=junk[:, k, :], in0=pick[:, k, :], in1=banks[2][:, 5 * EX:6 * EX], scale=1.0,
                                                 scalar=0.0, op0=ALU.mult, op1=ALU.add, accum_out=rk[:, k:k + 1])
                    dve.tensor_tensor(taken[:, :], taken[:, :], picked[:, :], ALU.add)
                    dve.drain()
                    dve.tensor_copy(rki[:, 0, :], rk[:, :])
                    dve.tensor_copy(rank[:, bass.ds(t, 1), :], rk[:, :])
                    dve.drain()
                    dve.tensor_scalar(rki[:, 1, :], rki[:, 0, :], P - 1, None, ALU.bitwise_and)
                    dve.tensor_scalar(rki[:, 2, :], rki[:, 0, :], 7, None, ALU.arith_shift_right)
                    dve.drain()
                    dve.tensor_copy(rkf[:, :, :], rki[:, 1:3, :])
                    dve.drain()
                    dve.scalar_tensor_tensor(qs[:, :], i8f[:, :], float(SLOTCH), rkf[:, 1, :], ALU.mult, ALU.add)
                    dve.tensor_scalar(rk[:, :], rkf[:, 1, :], float(SLOTCH), 8192.0, ALU.is_ge, ALU.mult)
                    dve.wait_ge(nd_slot, t + (DEPTH + 1))
                    for k in range(TOPK):
                        dve.tensor_scalar(lo1[:, k, 0, :], iota_b[:, :], rkf[:, 0, k:k + 1], hnum[:, k, bass.ds(t, 1)],
                                          ALU.is_equal, ALU.mult)
                        dve.tensor_scalar(lo1[:, k, 1, :], iota_b[:, :], rkf[:, 0, k:k + 1], pcol[:, 0:1],
                                          ALU.is_equal, ALU.mult)
                    dve.drain()
                    dve.scalar_tensor_tensor(qs[:, :], rk[:, :], inval[:, bass.ds(t, 1)], qs[:, :], ALU.add, ALU.add)
                    dve.drain()
                    for k in range(TOPK):
                        last = dve.tensor_scalar(sel[:, k, :], iota_s[:, :], qs[:, k:k + 1], None, ALU.is_equal)
                    last.then_inc(nd_sel, 1)
                behind(2, place)

                def choose(t):
                    dve.wait_ge(nd_logit, t + 1)
                    dve.tensor_tensor(lg[:, :], banks[5][:, D:D + EX], bgb[:, :], ALU.add)
                    dve.drain()
                    dve.max(v8[:, :], lg[:, :])
                    dve.drain()
                    dve.max_index(i8[:, :], v8[:, :], lg[:, :])
                    dve.tensor_copy(top[:, bass.ds(t, 1), :], v8[:, 0:TOPK])
                    dve.drain()
                    dve.tensor_copy(i8f[:, :], i8[:, 0:TOPK])
                    dve.drain()
                    for k in range(TOPK):
                        dve.tensor_scalar(pick[:, k, :], iota_b[:, 0:EX], i8f[:, k:k + 1], valid[:, bass.ds(t, 1)],
                                          ALU.is_equal, ALU.mult)
                    dve.drain()
                    dve.tensor_tensor(picked[:, :], pick[:, 0, :], pick[:, 1, :], ALU.add).then_inc(nd_pick, 1)
                behind(1, choose)
                if i is not None:
                    dve.wait_ge(nd_sqrt, i + 1)
                    dve.reciprocal(rs[:, bass.ds(i, 1)], tmp[:, bass.ds(i, 1)]).then_inc(nd_recip, 1)

            one_hots(0, 0, True)
            dve.sem_inc(nd_pick, DEPTH)
            dve.sem_inc(nd_sel, DEPTH)

            def step(it, first, final=False):
                for q in range(LASTQ if final else RING):
                    g = it * RING + q
                    if q + 1 < (LASTQ if final else RING):
                        one_hots(it, q + 1, first)
                    elif not final:
                        one_hots(it + 1, 0)
                    c = group_code(dve, g)
                    first_tile = extras(g, c)
                    dve.drain()
                    dve.wait_ge(group_mm, g + 1)
                    dve.tensor_tensor(acc[:, bass.ds(first_tile, 1), :], acc[:, bass.ds(first_tile, 1), :],
                                      banks[q % 2][:, 0:D + 1], ALU.add).then_inc(acc_added, 1)
                    ticks_of_group(dve, c, tick)
            step(0, True)
            with dve.Fori(1, STEPS - 1) as it:
                step(it, False)
            step(STEPS - 1, False, True)
            last_ticks(dve, tick)

            dve.wait_ge(slots_mm, 1)
            dve.tensor_scalar(tok_t, banks[6][:, :], float(P), -float(P), ALU.mult, ALU.add)
            dve.drain()
            dve.tensor_tensor(tok_f, tok_t, banks[7][:, :], ALU.add)
            dve.drain()
            dve.tensor_scalar(tok_t, tok_f, 0.0, UNUSED, ALU.is_lt, ALU.mult)
            dve.drain()
            dve.tensor_tensor(tok_f, tok_f, tok_t, ALU.add)
            dve.drain()
            dve.tensor_copy(sidx[:, :], tok_f)
            dve.tensor_scalar(tok_t, tok_f, float(NPAD), -float(NPAD), ALU.is_ge, ALU.mult)
            dve.drain()
            dve.tensor_tensor(tok_f, tok_f, tok_t, ALU.add)
            dve.drain()
            dve.tensor_copy(gidx[:, :], tok_f).then_inc(slots_ready, 1)
            dve.tensor_scalar(nch_f[:, :], banks[5][0:1, 2 * P:2 * P + EX], float(CAP), float(P - 1), ALU.min, ALU.add)
            dve.drain()
            dve.tensor_copy(nch_i[:, :], nch_f[:, :])
            dve.drain()
            dve.tensor_scalar(nch_i[:, :], nch_i[:, :], 7, None, ALU.arith_shift_right)
            dve.drain()
            dve.tensor_scalar(nch_f[:, :], nch_i[:, :], 1.0, None, ALU.max)
            dve.drain()
            dve.tensor_copy(nch_i[:, :], nch_f[:, :])
            dve.drain().then_inc(tables_done, 1)
            dve.tensor_tensor(gate[:, :, 1], top[:, :, 1], top[:, :, 0], ALU.subtract).then_inc(gap_ready, 1)
            dve.wait_ge(exp_ready, 1)
            dve.tensor_scalar(gate[:, :, 0], gate[:, :, 1], 1.0, None, ALU.add)
            dve.drain()
            dve.reciprocal(gate[:, :, 0], gate[:, :, 0])
            dve.drain()
            dve.tensor_tensor(gate[:, :, 1], gate[:, :, 1], gate[:, :, 0], ALU.mult)
            dve.tensor_scalar(rank[:, :, :], rank[:, :, :], float(CAP), None, ALU.is_lt)
            dve.drain()
            dve.tensor_tensor(gate[:, :, :], gate[:, :, :], rank[:, :, :], ALU.mult)

            def to_sbuf(e):
                dve.wait_ge(tokens_t, e + 1)
                dve.tensor_copy(xgT[:, 0:2, :, :], banks[0][:, :])
                dve.tensor_copy(xgT[:, 2, :, :], banks[1][:, 0:D]).then_inc(tokens_s, 1)

            nextra = dve.alloc_register("dve_nextra")
            dve.reg_mov(nextra, 0)

            def extra_chunks(e, par, nch):
                with dve.If(nch > MAIN):
                    with dve.Fori(MAIN, nch) as k:
                        dve.reg_add(nextra, nextra, 1)
                        n = dve.snap(nextra, min_val=1, max_val=EX * SLOTCH)
                        dve.wait_ge(xtra_t, n)
                        dve.tensor_copy(xgTx[:, :, :], banks[1][:, D:2 * D]).then_inc(xtra_s, 1)
                        dve.wait_ge(b2_in[par], landed(e, par))
                        dve.wait_ge(xtra_l2, n)
                        dve.tensor_tensor(outx[:, :], banks[6][:, 0:D], b2s[:, par, :], ALU.add).then_inc(xtra_out, 1)

            def expert(e, par, first, final=False):
                nch = dve.value_load(nch_i[0:1, bass.ds(e, 1)], min_val=1, max_val=SLOTCH)
                extra_chunks(e, par, nch)
                if not final:
                    to_sbuf(e + 1)
                dve.wait_ge(b2_in[par], landed(e, par))
                for k in range(MAIN):
                    dve.wait_ge(l2_done[k], e + 1)
                    if not first:
                        dve.wait_ge(scattered[par][k], prior_scatter(e, par))
                    dve.tensor_tensor(outs[:, par, k, :], out_bank(k), b2s[:, par, :], ALU.add).then_inc(out_ready, 1)
            to_sbuf(0)
            expert(0, 0, True)
            expert(1, 1, True)
            with dve.Fori(1, EX // 2 - 1) as i:
                expert(i * 2, 0, False)
                expert(i * 2 + 1, 1, False)
            expert(EX - 2, 0, False)
            expert(EX - 1, 1, False, True)

            dve.drain()
            for g in range(NB):
                dve.wait_ge(y2_in[g % 2], 16 * TOPK * (g // 2 + 1))
                for k in range(TOPK):
                    for t in range(TG):
                        tile = g * TG + t
                        last = dve.scalar_tensor_tensor(acc[:, tile, 0:D], ybuf[:, g % 2, k, t, :], gate[:, tile, k:k + 1],
                                                        acc[:, tile, 0:D], ALU.mult, ALU.add)
                    if k == 0:
                        dve.drain()
                last.then_inc(combined, 1)
            dve.wait_ge(mean_mm, 1)
            dve.tensor_scalar(mean[:, :], banks[0][:, 0:D], 1.0 / N, None, ALU.mult)
            dve.drain()
            for g in range(NB):
                yv = acc[:, g * TG:(g + 1) * TG, 0:D]
                dve.tensor_tensor(yv, yv, mean[:, :].unsqueeze(1).to_broadcast([P, TG, D]), ALU.subtract).then_inc(centered, 1)
            dve.wait_ge(var_mm, 1)
            dve.tensor_scalar(var[:, :], banks[1][:, 0:D], 1.0 / N, BN_EPS, ALU.mult, ALU.add).then_inc(var_ready, 1)
            dve.wait_ge(var_sqrt, 1)
            inv_sqrt(dve, scale[:, :], vroot[:, :], var[:, :])
            dve.drain()
            dve.wait_ge(gb_in, 32)
            dve.tensor_tensor(scale[:, :], scale[:, :], gb[:, 0, :], ALU.mult).then_inc(scale_ready, 1)
            dve.drain()

            def group_roots(g):
                v, root = deg[:, g * TG:(g + 1) * TG], rs[:, g * TG:(g + 1) * TG]
                dve.wait_ge(lnvar_sqrt, g + 1)
                inv_sqrt(dve, root, tmp[:, g * TG:(g + 1) * TG], v)
                dve.drain()
                dve.scalar_tensor_tensor(v, mv[:, g * TG:(g + 1) * TG, 0], -1.0, root, ALU.mult, ALU.mult).then_inc(roots_ready, 1)
            dve.wait_ge(xbeta, NB)
            for g in range(NB):
                yv = acc[:, g * TG:(g + 1) * TG, 0:D]
                if g in POOL_SCALES:
                    dve.wait_ge(pool_scaled, POOL_SCALES.index(g) + 1)
                else:
                    dve.tensor_tensor(yv, yv, scale[:, :].unsqueeze(1).to_broadcast([P, TG, D]), ALU.mult)
                    dve.drain()
                dve.tensor_tensor(yv, yv, xs[:, g * TG:(g + 1) * TG, :], ALU.add)
                dve.drain()
                for t in range(TG):
                    dve.bn_stats(stats[:, t, :], acc[:, g * TG + t, 0:D])
                dve.drain()
                for t in range(TG):
                    dve.bn_aggr(mv[:, g * TG + t, :], stats[:, t, :])
                dve.drain()
                dve.tensor_scalar(deg[:, g * TG:(g + 1) * TG], mv[:, g * TG:(g + 1) * TG, 1], LN_EPS, None,
                                  ALU.add).then_inc(lnvar_ready, 1)
                if g:
                    group_roots(g - 1)
            group_roots(NB - 1)
            for t in range(DVE_NORMS):
                tile = NT - DVE_NORMS + t
                last = dve.tensor_scalar(acc[:, tile, 0:D], acc[:, tile, 0:D], mv[:, tile, 0:1], rs[:, tile:tile + 1],
                                         ALU.subtract, ALU.mult)
            last.then_inc(normed_d, 1)

        @block.tensor
        def _(pe):
            pe.wait_ge(const_d, 1)
            n = 0
            for which in range(LISTS):
                if which < 2:
                    pe.wait_ge(srch_f, which + 1)
                    lists = stage[:, (2 + which) * COLS:(3 + which) * COLS]
                else:
                    pe.wait_ge(dst_f, 1)
                    lists = srcT[:, :]
                for c in range(NTR):
                    if n >= 4:
                        pe.wait_ge(tr_copied, n - 3)
                    for j in range(min(4, EB - 4 * c)):
                        b = 4 * c + j
                        last = pe.transpose(banks[T_BANKS[n % 4]][:, j * P:(j + 1) * P], lists[:, b * P:(b + 1) * P], ident[:, :])
                    last.then_inc(tr_done, 1)
                    n += 1
            pe.wait_ge(dst_f, 2)
            for a in range(2):
                last = pe.transpose(banks[1][0:EB, a * P:(a + 1) * P], mnmx[:, a, :], ident[:, :])
            last.then_inc(mm_tr, 1)


            def hist(i, first, final=False):
                for q in range(HQ):
                    pe.wait_ge(lo_ready, i * HQ + (q + 1))
                    pe.wait_ge(hi_ready, i * HQ + (q + 1))
                    for c in range(HB):
                        last = pe.matmul(banks[0][:, 0:NT], lo_hot[:, q, c, :], hi_hot[:, q, c, :],
                                         start=first and q == 0 and c == 0, stop=final and q == HQ - 1 and c == HB - 1,
                                         skip_group_check=True)
                    last.then_inc(hist_mm, 1)
            hist(0, True)
            with pe.Fori(1, HSTEPS - 1) as i:
                hist(i, False)
            hist(HSTEPS - 1, False, True)

            pe.wait_ge(mm_row, 32)
            pe.matmul(banks[1][:, 0:GCOLS], ones[0:1, :], rng[0:1, 0, :], start=True, stop=True).then_inc(nb_done, 1)
            pe.wait_ge(code_ready, 1)

            extra = pe.alloc_register("pe_extra")
            pe.reg_mov(extra, 0)

            def multiply(bank, hots, q, done):
                for j in range(CPG):
                    last = pe.matmul(bank[:, 0:D + 1], hots[:, j, :], ring(q)[:, j, :], start=j == 0, stop=j == CPG - 1)
                last.then_inc(done, 1)

            def tick(i, behind):
                if i is not None:
                    pe.wait_ge(nd_deg, i + 1)

                def places(t):
                    pe.wait_ge(nd_pick, t + (DEPTH + 1))
                    pe.matmul(banks[2][:, 5 * EX:6 * EX], tri[:, :], picked[:, :], start=True, stop=False)
                    pe.matmul(banks[2][:, 5 * EX:6 * EX], ones_b[:, :], taken[:, :], start=False, stop=True).then_inc(nd_rank, 1)
                behind(2, places)

                def slots(t):
                    pe.wait_ge(nd_sel, t + (DEPTH + 1))
                    for k in range(TOPK):
                        for a in range(2):
                            last = pe.matmul(banks[6 + a][:, :], lo1[:, k, a, :], sel[:, k, :], start=False, stop=False,
                                             skip_group_check=True)
                    last.then_inc(nd_slot, 1)
                behind(3, slots)
                if i is not None:
                    pe.wait_ge(nd_in, i + 1)
                    for k in range(2 * DK):
                        last = pe.transpose(banks[3][:, k * P:(k + 1) * P], (mS if k < DK else xS)[:, (k % DK) * P:(k % DK + 1) * P],
                                            ident[:, :])
                    last.then_inc(nd_tr, 1)

                def transpose_y(t):
                    pe.wait_ge(nd_y, t + 1)
                    for k in range(DK):
                        last = pe.transpose(banks[5][:, k * P:(k + 1) * P], yS[:, k * P:(k + 1) * P], ident[:, :])
                    last.then_inc(nd_ytr, 1)
                behind(1, transpose_y)
                if i is not None:
                    pe.wait_ge(nd_t, i + 1)
                    for a in range(2):
                        for k in range(DK):
                            last = pe.matmul(banks[4][:, a * D:(a + 1) * D], tS[:, a * DK + k, :], (wgc, wres)[a][:, k, :],
                                             start=k == 0, stop=k == DK - 1)
                    last.then_inc(nd_proj, 1)

                def logits(t):
                    pe.wait_ge(nd_yt, t + 1)
                    for k in range(DK):
                        last = pe.matmul(banks[5][:, D:D + EX], ytS[:, k, :], wg[:, k, :], start=k == 0, stop=k == DK - 1)
                    last.then_inc(nd_logit, 1)
                behind(1, logits)

            pe.sem_inc(nd_rank, DEPTH)
            pe.sem_inc(nd_slot, DEPTH + 1)
            pe.wait_ge(w_loaded, 16 * 7)
            for j in range(HK):
                last = pe.transpose(banks[3][:, j * EX:(j + 1) * EX], b1r[:, j * P:(j + 1) * P], ident[0:EX, 0:EX])
            last.then_inc(b1_t, 1)
            zb = zeros[:, :].bitcast(BF16)
            pe.wait_ge(tr_copied, LISTS * NTR)
            for a in range(2):
                pe.matmul(banks[6 + a][:, :], zb[:, 0:P], zb[:, 0:SC], start=True, stop=False, skip_group_check=True)

            def step(it, first, final=False):
                for q in range(LASTQ if final else RING):
                    g = it * RING + q
                    c = group_code(pe, g)
                    first_tile, last_tile = field(pe, c, 0), field(pe, c, 1)
                    pe.wait_ge(gath[q], it * (16 * CPG) + 16 * CPG)
                    if first and q == RING // 2:
                        pe.wait_ge(high_ones, 1)
                    pe.wait_ge(hot_ready, g + 1)
                    if not (first and q < 2):
                        pe.wait_ge(acc_added, g - 1)
                    multiply(banks[q % 2], hot[q % HOTS], q, group_mm)
                    with pe.If(last_tile > first_tile):
                        with pe.Fori(first_tile + 1, last_tile + 1) as t:
                            pe.reg_add(extra, extra, 1)
                            n = pe.snap(extra, min_val=1, max_val=GROUPS * NT)
                            pe.wait_ge(hotx_ready, n)
                            multiply(banks[2], hotx, q, groupx_mm)
                    ticks_of_group(pe, c, tick)
            step(0, True)
            with pe.Fori(1, STEPS - 1) as it:
                step(it, False)
            step(STEPS - 1, False, True)
            last_ticks(pe, tick)
            for a in range(2):
                last = pe.matmul(banks[6 + a][:, :], zb[:, 0:P], zb[:, 0:SC], start=False, stop=True, skip_group_check=True)

            pe.matmul(banks[5][:, 2 * P:2 * P + EX], ones_b[:, :], taken[:, :], start=True, stop=True).then_inc(slots_mm, 1)

            nextra = pe.alloc_register("pe_nextra")
            pe.reg_mov(nextra, 0)

            def transpose_tokens(e, par):
                for k in range(MAIN):
                    pe.wait_ge(gathered[par][k], prior_scatter(e, par) + 16)
                    for c in range(DK):
                        last = pe.transpose(banks[k // 2][:, (k % 2) * D + c * P:(k % 2) * D + (c + 1) * P],
                                            xg[:, par, k, c * P:(c + 1) * P], ident[:, :])
                last.then_inc(tokens_t, 1)

            def first_layer(bank, par, xt, done):
                for j in range(HK):
                    for c in range(DK):
                        last = pe.matmul(bank[:, j * P:(j + 1) * P], w1s[:, par, c, j * P:(j + 1) * P], xt[:, c, :],
                                         start=c == 0, stop=c == DK - 1)
                last.then_inc(done, 1)

            def second_layer(dst, par, h, *done):
                for j in range(HK):
                    last = pe.matmul(dst, h[:, j, :], w2s[:, par, j, :], start=j == 0, stop=j == HK - 1)
                return last

            def expert(e, par, first, final=False):
                nch = pe.value_load(nch_i[0:1, bass.ds(e, 1)], min_val=1, max_val=SLOTCH)
                pe.wait_ge(w1_in[par], landed(e, par))
                pe.wait_ge(tokens_s, e + 1)
                with pe.If(nch > MAIN):
                    with pe.Fori(MAIN, nch) as k:
                        pe.reg_add(nextra, nextra, 1)
                        n = pe.snap(nextra, min_val=1, max_val=EX * SLOTCH)
                        pe.wait_ge(w2_in[par], landed(e, par))
                        if not first:
                            pe.wait_ge(out_ready, e * MAIN)
                        pe.wait_ge(xtra_gathered, n * 16)
                        for c in range(DK):
                            last = pe.transpose(banks[1][:, D + c * P:D + (c + 1) * P], xgx[:, c * P:(c + 1) * P], ident[:, :])
                        last.then_inc(xtra_t, 1)
                        pe.wait_ge(xtra_s, n)
                        first_layer(banks[5], par, xgTx, xtra_l1)
                        pe.wait_ge(xtra_h, n)
                        second_layer(banks[6][:, 0:D], par, h1x).then_inc(xtra_l2, 1)
                        pe.wait_ge(xtra_out, n)
                        pe.transpose(banks[5][:, 0:P], ident[:, :], ident[:, :])
                for k in range(MAIN):
                    if k == 0:
                        first_layer(banks[2 + k], par, xgT[:, k, :, :], l1_done[k])
                    else:
                        with pe.If(nch > k):
                            first_layer(banks[2 + k], par, xgT[:, k, :, :], l1_done[k])
                        with pe.Else():
                            pe.sem_inc(l1_done[k], 1)
                if not final:
                    transpose_tokens(e + 1, 1 - par)
                pe.wait_ge(w2_in[par], landed(e, par))
                if not first:
                    pe.wait_ge(out_ready, e * MAIN)
                for k in range(MAIN):
                    if k == 0:
                        pe.wait_ge(h1_ready[k], e + 1)
                        second_layer(out_bank(k), par, h1[:, k, :, :]).then_inc(l2_done[k], 1)
                    else:
                        with pe.If(nch > k):
                            pe.wait_ge(h1_ready[k], e + 1)
                            if k == 2:
                                pe.wait_ge(out_ready, e * MAIN + 1)
                            second_layer(out_bank(k), par, h1[:, k, :, :]).then_inc(l2_done[k], 1)
                        with pe.Else():
                            pe.sem_inc(l2_done[k], 1)

            transpose_tokens(0, 0)
            pe.wait_ge(tables_done, 1)
            expert(0, 0, True)
            expert(1, 1, False)
            with pe.Fori(1, EX // 2 - 1) as i:
                expert(i * 2, 0, False)
                expert(i * 2 + 1, 1, False)
            expert(EX - 2, 0, False)
            expert(EX - 1, 1, False, True)

            for g in range(NB):
                pe.wait_ge(combined, g + 1)
                for t in range(TG):
                    tile = g * TG + t
                    last = pe.matmul(banks[0][:, 0:D], (ones_last if tile == NT - 1 else ones)[:, :], acc[:, tile, 0:D],
                                     start=tile == 0, stop=tile == NT - 1)
            last.then_inc(mean_mm, 1)
            for g in range(NB):
                pe.wait_ge(squared, g + 1)
                for t in range(TG):
                    tile = g * TG + t
                    last = pe.matmul(banks[1][:, 0:D], (ones_last if tile == NT - 1 else ones)[:, :], sq[:, g % 2, t, :],
                                     start=tile == 0, stop=tile == NT - 1)
                last.then_inc(sq_used, 1)
            pe.drain().then_inc(var_mm, 1)


_INS = ['x', 'src', 'dst', 'L0_gnn_W_gc', 'L0_gnn_b_gc', 'L0_gnn_W_res', 'L0_gnn_b_res', 'L0_gnn_Wg', 'L0_gnn_bg',
        'L0_gnn_w1', 'L0_gnn_b1', 'L0_gnn_w2', 'L0_gnn_b2', 'L0_gnn_gamma', 'L0_gnn_beta']
_OUTS = [((6250, 256), 'float32')]


def kernel(**inputs):
    import numpy as _np
    import concourse.bacc as _bacc
    from concourse import mybir as _mybir
    from concourse.bass_utils import run_bass_kernel_spmd as _run

    nc = _bacc.Bacc("TRN2", target_bir_lowering=False, num_devices=1)
    arrays, args = {}, []
    for name in _INS:
        a = _np.ascontiguousarray(inputs[name])
        arrays[f"in_{name}_dram"] = a
        args.append(nc.dram_tensor(f"in_{name}_dram", a.shape, _mybir.dt.from_np(a.dtype), kind="ExternalInput").ap())
    for i, (shape, dtype) in enumerate(_OUTS):
        dt = _mybir.dt.from_np(_np.dtype(dtype))
        args.append(nc.dram_tensor(f"out_{i}_dram", shape, dt, kind="ExternalOutput").ap())
    graph_moe_kernel(nc, *args)
    r = _run(nc, [arrays], core_ids=[0])
    return r.results[0]["out_0_dram"]
```
